# Optimizing a Trainium2 kernel written in Bass

```python
import numpy as np
import jax
import jax.numpy as jnp

def _softmax(x, axis=-1):
    return jax.nn.softmax(x, axis=axis)

def _gelu(x):
    return jax.nn.gelu(x, approximate=True)

def _silu(x):
    return jax.nn.silu(x)

def _sigmoid(x):
    return jax.nn.sigmoid(x)

def _layernorm(x, axis=-1, eps=1e-05):
    m = jnp.mean(x, axis=axis, keepdims=True)
    v = jnp.var(x, axis=axis, keepdims=True)
    return (x - m) / jnp.sqrt(v + eps)

def _scatter_add(tgt, idx, src, axis=0):
    return tgt.at[idx].add(src)

def _segment_sum(src, seg, n):
    return jax.ops.segment_sum(src, seg, n)
kernel_name = 'mk_lm_tower_d4_tok_ids256_r4_59a847'

def setup_inputs(seed: int=0):
    np.random.seed(seed)
    _w = jnp.asarray

    def _rec_inputs():
        import jax
        import jax.numpy as jnp
        _rk = jax.random.key(seed)
        x = jax.random.randint(jax.random.fold_in(_rk, 1), (8, 256), 0, 64, jnp.int32)
        return x
    x = _rec_inputs()

    def _L0_tok_setup():
        import jax, jax.numpy as jnp
        import numpy as np
        MOE_DIM = 64
        MOE_INTER_DIM = 128
        N_EXPERTS = 4
        N_LAYERS = 2
        VOCAB = 64
        key = jax.random.key(seed)
        ks = jax.random.split(key, 6)
        B, S = (64, 1024)
        input_ids = jax.random.randint(ks[0], (B, S), 0, VOCAB)
        sd = 0.02
        embed = jax.random.normal(ks[1], (VOCAB, MOE_DIM), jnp.float32) * sd
        Wg = jax.random.normal(ks[2], (N_LAYERS, N_EXPERTS, MOE_INTER_DIM, MOE_DIM), jnp.float32) * sd
        Wu = jax.random.normal(ks[3], (N_LAYERS, N_EXPERTS, MOE_INTER_DIM, MOE_DIM), jnp.float32) * sd
        Wd = jax.random.normal(ks[4], (N_LAYERS, N_EXPERTS, MOE_DIM, MOE_INTER_DIM), jnp.float32) * sd
        lm_head = jax.random.normal(ks[5], (VOCAB, MOE_DIM), jnp.float32) * sd
        return {'input_ids': input_ids, 'embed': embed, 'Wg': Wg, 'Wu': Wu, 'Wd': Wd, 'lm_head': lm_head}
    _L0_tok_all = _L0_tok_setup()
    _L0_tok_in = {k: v for k, v in _L0_tok_all.items() if k in ('embed', 'Wg', 'Wu', 'Wd', 'lm_head')}
    del _L0_tok_all

    def _L0_attn_setup():
        import jax, jax.numpy as jnp
        import numpy as np
        B, N, D, H = (2, 512, 64, 8)
        DH = D // H
        E = 16384
        EPS = 1e-05

        def _layer_norm(y, gamma, beta):
            mu = jnp.mean(y, axis=-1, keepdims=True)
            var = jnp.var(y, axis=-1, keepdims=True)
            return (y - mu) * jax.lax.rsqrt(var + EPS) * gamma + beta
        key = jax.random.key(seed)
        ks = jax.random.split(key, 12)
        s = 0.02
        inp = {'x': jax.random.normal(ks[0], (B, N, D), jnp.float32), 'edge_index': jax.random.randint(ks[1], (2, E), 0, N, jnp.int64), 'Wq': jax.random.normal(ks[2], (D, D), jnp.float32) * s, 'bq': jnp.zeros((D,), jnp.float32), 'Wk': jax.random.normal(ks[3], (D, D), jnp.float32) * s, 'bk': jnp.zeros((D,), jnp.float32), 'Wv': jax.random.normal(ks[4], (D, D), jnp.float32) * s, 'bv': jnp.zeros((D,), jnp.float32), 'Wo': jax.random.normal(ks[5], (D, D), jnp.float32) * s, 'bo': jnp.zeros((D,), jnp.float32), 'gamma': jnp.ones((D,), jnp.float32), 'beta': jnp.zeros((D,), jnp.float32)}
        return inp
    _L0_attn_all = _L0_attn_setup()
    _L0_attn_in = {k: v for k, v in _L0_attn_all.items() if k in ('edge_index', 'Wq', 'bq', 'Wk', 'bk', 'Wv', 'bv', 'Wo', 'bo', 'gamma', 'beta')}
    del _L0_attn_all

    def _L0_ffn_setup():
        import jax, jax.numpy as jnp
        import numpy as np
        TOP_K = 6
        LN_EPS = 1e-05
        key = jax.random.key(seed)
        ks = jax.random.split(key, 4)
        B, S, D, E = (2, 64, 64, 64)
        x = jax.random.normal(ks[0], (B, S, D), dtype=jnp.float32)
        gate_w = jax.random.normal(ks[1], (E, D), dtype=jnp.float32) * 0.02
        lattice_weights = jax.random.normal(ks[2], (E, D, D), dtype=jnp.float32) * 0.02
        out_w = jax.random.normal(ks[3], (D, D), dtype=jnp.float32) * 0.02
        out_b = jnp.zeros((D,), dtype=jnp.float32)
        ln_g = jnp.ones((D,), dtype=jnp.float32)
        ln_b = jnp.zeros((D,), dtype=jnp.float32)
        return {'x': x, 'gate_w': gate_w, 'lattice_weights': lattice_weights, 'out_w': out_w, 'out_b': out_b, 'ln_g': ln_g, 'ln_b': ln_b}
    _L0_ffn_all = _L0_ffn_setup()
    _L0_ffn_in = {k: v for k, v in _L0_ffn_all.items() if k in ('gate_w', 'lattice_weights', 'out_w', 'out_b', 'ln_g', 'ln_b')}
    del _L0_ffn_all

    def _L1_attn_setup():
        import jax, jax.numpy as jnp
        import numpy as np
        import math
        B, T, D_MODEL = (1, 512, 64)
        N_Q, N_KV = (16, 1)
        D_HEAD = D_MODEL // N_KV
        QPG = N_Q // N_KV
        ROPE_BASE = 10000.0
        WINDOW = 128
        EPS = 1.1920929e-07
        NEG = -1e+30

        def _rope(x, base=ROPE_BASE):
            t, d = (x.shape[-2], x.shape[-1])
            freqs = base ** (-2.0 * jnp.arange(d // 2, dtype=jnp.float32) / d)
            theta = jnp.arange(t, dtype=jnp.float32)[:, None] * freqs[None, :]
            cos, sin = (jnp.cos(theta), jnp.sin(theta))
            x1, x2 = (x[..., 0::2], x[..., 1::2])
            r1 = x1 * cos - x2 * sin
            r2 = x1 * sin + x2 * cos
            return jnp.stack([r1, r2], axis=-1).reshape(x.shape)

        def _rmsnorm(x, w):
            return x * jax.lax.rsqrt(jnp.mean(x * x, axis=-1, keepdims=True) + EPS) * w
        key = jax.random.key(seed)
        k0, k1, k2, k3 = jax.random.split(key, 4)
        x = jax.random.normal(k0, (B, T, D_MODEL), dtype=jnp.float32)
        wq = jax.random.normal(k1, (QPG * N_KV * D_HEAD, D_MODEL), dtype=jnp.float32) * 0.02
        wkv = jax.random.normal(k2, (2 * D_HEAD * N_KV, D_MODEL), dtype=jnp.float32) * 0.02
        wo = jax.random.normal(k3, (D_MODEL, D_HEAD * N_Q * N_KV), dtype=jnp.float32) * 0.02
        q_norm_w = jnp.ones((D_HEAD,), dtype=jnp.float32)
        k_norm_w = jnp.ones((D_HEAD,), dtype=jnp.float32)
        return {'x': x, 'wq': wq, 'wkv': wkv, 'wo': wo, 'q_norm_w': q_norm_w, 'k_norm_w': k_norm_w}
    _L1_attn_all = _L1_attn_setup()
    _L1_attn_in = {k: v for k, v in _L1_attn_all.items() if k in ('wq', 'wkv', 'wo', 'q_norm_w', 'k_norm_w')}
    del _L1_attn_all

    def _L1_ffn_setup():
        import jax, jax.numpy as jnp
        import numpy as np
        B, K, D = (128, 16, 64)
        E = 32
        H = int(D * 0.25)
        key = jax.random.key(seed)
        ks = jax.random.split(key, 7)
        d_rs = D ** (-0.5)
        h_rs = H ** (-0.5)
        x = jax.random.normal(ks[0], (B, K, D), dtype=jnp.float32)
        router_w = jax.random.uniform(ks[1], (E, D), jnp.float32, -d_rs, d_rs)
        router_b = jax.random.uniform(ks[2], (E,), jnp.float32, -d_rs, d_rs)
        W1 = jax.random.uniform(ks[3], (E, D, H), jnp.float32, -h_rs, h_rs)
        b1 = jax.random.uniform(ks[4], (E, H), jnp.float32, -h_rs, h_rs)
        W2 = jax.random.uniform(ks[5], (E, H, D), jnp.float32, -d_rs, d_rs)
        b2 = jax.random.uniform(ks[6], (E, D), jnp.float32, -d_rs, d_rs)
        return {'x': x, 'router_w': router_w, 'router_b': router_b, 'W1': W1, 'b1': b1, 'W2': W2, 'b2': b2}
    _L1_ffn_all = _L1_ffn_setup()
    _L1_ffn_in = {k: v for k, v in _L1_ffn_all.items() if k in ('router_w', 'router_b', 'W1', 'b1', 'W2', 'b2')}
    del _L1_ffn_all

    def _L2_attn_setup():
        import jax, jax.numpy as jnp
        import numpy as np
        HEAD_SIZE = 64
        HEAD_SIZE_R = HEAD_SIZE // 4
        HEAD_SIZE_C = HEAD_SIZE - HEAD_SIZE_R
        N_EMBD = 64

        def rope(x, start_pos=0):
            B, T, d = x.shape
            half = d // 2
            theta = 1.0 / 10000.0 ** (jnp.arange(half, dtype=x.dtype) / half)
            idx = jnp.arange(start_pos, start_pos + T, dtype=x.dtype)[:, None] * theta[None, :]
            sin, cos = (jnp.sin(idx), jnp.cos(idx))
            xs = x.reshape(B, T, half, 2)
            x1, x2 = (xs[..., 0], xs[..., 1])
            rot = jnp.stack([x1 * cos - x2 * sin, x1 * sin + x2 * cos], axis=-1)
            return rot.reshape(B, T, d)

        def _reference_tuple_inner(x, Wq_comp, Wkv_comp, Wqc, Wqr, Wkc, Wkr, Wv):
            c_q = x @ Wq_comp
            c_kv = x @ Wkv_comp
            q_c = c_q @ Wqc
            q_r = rope(c_q @ Wqr, start_pos=0)
            q = jnp.concatenate([q_c, q_r], axis=-1)
            k_c = c_kv @ Wkc
            k_r = rope(c_kv @ Wkr, start_pos=0)
            k = jnp.concatenate([k_c, k_r], axis=-1)
            v = c_kv @ Wv
            scale = 1.0 / jnp.sqrt(jnp.asarray(HEAD_SIZE, dtype=x.dtype))
            wei = jnp.einsum('bqd,bkd->bqk', q, k) * scale
            T_q = q.shape[1]
            mask = jnp.tril(jnp.ones((T_q, T_q), dtype=bool))
            wei = jnp.where(mask, wei, jnp.asarray(-jnp.inf, dtype=wei.dtype))
            wei = jax.nn.softmax(wei, axis=-1)
            out = jnp.einsum('bqk,bkd->bqd', wei, v)
            return (out, (k, v))
        key = jax.random.key(seed)
        ks = jax.random.split(key, 8)
        B, T = (32, 512)
        s = 0.05
        return {'x': jax.random.normal(ks[0], (B, T, N_EMBD), dtype=jnp.float32), 'Wq_comp': jax.random.normal(ks[1], (N_EMBD, N_EMBD), dtype=jnp.float32) * s, 'Wkv_comp': jax.random.normal(ks[2], (N_EMBD, N_EMBD), dtype=jnp.float32) * s, 'Wqc': jax.random.normal(ks[3], (N_EMBD, HEAD_SIZE_C), dtype=jnp.float32) * s, 'Wqr': jax.random.normal(ks[4], (N_EMBD, HEAD_SIZE_R), dtype=jnp.float32) * s, 'Wkc': jax.random.normal(ks[5], (N_EMBD, HEAD_SIZE_C), dtype=jnp.float32) * s, 'Wkr': jax.random.normal(ks[6], (N_EMBD, HEAD_SIZE_R), dtype=jnp.float32) * s, 'Wv': jax.random.normal(ks[7], (N_EMBD, HEAD_SIZE), dtype=jnp.float32) * s}
    _L2_attn_all = _L2_attn_setup()
    _L2_attn_in = {k: v for k, v in _L2_attn_all.items() if k in ('Wq_comp', 'Wkv_comp', 'Wqc', 'Wqr', 'Wkc', 'Wkr', 'Wv')}
    del _L2_attn_all

    def _L2_ffn_setup():
        import math
        import jax, jax.numpy as jnp
        import numpy as np
        CAPACITY_FACTOR = 1.25
        key = jax.random.key(seed)
        ks = jax.random.split(key, 5)
        B, L, D, F, E = (8, 2048, 64, 256, 8)
        h = jax.random.normal(ks[0], (B, L, D), dtype=jnp.float32)
        gate_w = jax.random.normal(ks[1], (D, E), dtype=jnp.float32) * 0.02
        gate_b = jnp.zeros((E,), dtype=jnp.float32)
        w1 = jax.random.normal(ks[2], (E, D, F), dtype=jnp.float32) * (1.0 / math.sqrt(D))
        b1 = jnp.zeros((E, F), dtype=jnp.float32)
        w2 = jax.random.normal(ks[3], (E, F, D), dtype=jnp.float32) * (1.0 / math.sqrt(F))
        b2 = jnp.zeros((E, D), dtype=jnp.float32)
        return {'h': h, 'gate_w': gate_w, 'gate_b': gate_b, 'w1': w1, 'b1': b1, 'w2': w2, 'b2': b2}
    _L2_ffn_all = _L2_ffn_setup()
    _L2_ffn_in = {k: v for k, v in _L2_ffn_all.items() if k in ('gate_w', 'gate_b', 'w1', 'b1', 'w2', 'b2')}
    del _L2_ffn_all

    def _L3_attn_setup():
        import jax, jax.numpy as jnp
        import numpy as np
        key = jax.random.key(seed)
        ks = jax.random.split(key, 4)
        B, S, D = (4, 1024, 64)
        x = jax.random.normal(ks[0], (B, S, D), dtype=jnp.float32)
        Wq = jax.random.normal(ks[1], (D, D), dtype=jnp.float32) * 0.02
        Wk = jax.random.normal(ks[2], (D, D), dtype=jnp.float32) * 0.02
        Wv = jax.random.normal(ks[3], (D, D), dtype=jnp.float32) * 0.02
        bq = jnp.zeros((D,), dtype=jnp.float32)
        bk = jnp.zeros((D,), dtype=jnp.float32)
        bv = jnp.zeros((D,), dtype=jnp.float32)
        return {'x': x, 'Wq': Wq, 'bq': bq, 'Wk': Wk, 'bk': bk, 'Wv': Wv, 'bv': bv}
    _L3_attn_all = _L3_attn_setup()
    _L3_attn_in = {k: v for k, v in _L3_attn_all.items() if k in ('Wq', 'bq', 'Wk', 'bk', 'Wv', 'bv')}
    del _L3_attn_all

    def _L3_ffn_setup():
        import jax, jax.numpy as jnp
        import numpy as np
        B, T, C = (64, 96, 64)
        NH, NKV = (4, 2)
        HD = C // NH
        NREP = NH // NKV
        NE, TOPK = (8, 2)
        HID = int(8 / 3 * C)
        EPS_RMS = 1e-06

        def _rope_tables(t_len):
            inv_freq = 1.0 / 10000.0 ** (np.arange(0, HD, 2, dtype=np.float32) / HD)
            t = np.arange(t_len, dtype=np.float32)
            freqs = np.outer(t, inv_freq)
            emb = np.concatenate([freqs, freqs], axis=-1)
            return (jnp.asarray(np.cos(emb)), jnp.asarray(np.sin(emb)))

        def _rotate_half(x):
            h = x.shape[-1] // 2
            return jnp.concatenate([-x[..., h:], x[..., :h]], axis=-1)

        def _rmsnorm(v, w):
            return v * jax.lax.rsqrt(jnp.mean(v * v, axis=-1, keepdims=True) + EPS_RMS) * w
        key = jax.random.key(seed)
        ks = jax.random.split(key, 10)
        s = lambda k, shape: jax.random.normal(k, shape, jnp.float32) * 0.02
        return {'x': jax.random.normal(ks[0], (B, T, C), jnp.float32), 'ln1_w': jnp.ones((C,), jnp.float32), 'ln2_w': jnp.ones((C,), jnp.float32), 'wq': s(ks[1], (NH * HD, C)), 'wk': s(ks[2], (NKV * HD, C)), 'wv': s(ks[3], (NKV * HD, C)), 'wo': s(ks[4], (C, C)), 'router_w': s(ks[5], (NE, C)), 'w1': s(ks[6], (NE, HID, C)), 'w2': s(ks[7], (NE, C, HID)), 'w3': s(ks[8], (NE, HID, C))}
    _L3_ffn_all = _L3_ffn_setup()
    _L3_ffn_in = {k: v for k, v in _L3_ffn_all.items() if k in ('ln1_w', 'ln2_w', 'wq', 'wk', 'wv', 'wo', 'router_w', 'w1', 'w2', 'w3')}
    del _L3_ffn_all
    return {'x': x, 'L0_tok_embed': _L0_tok_in['embed'], 'L0_tok_Wg': _L0_tok_in['Wg'], 'L0_tok_Wu': _L0_tok_in['Wu'], 'L0_tok_Wd': _L0_tok_in['Wd'], 'L0_tok_lm_head': _L0_tok_in['lm_head'], 'L0_attn_edge_index': _L0_attn_in['edge_index'], 'L0_attn_Wq': _L0_attn_in['Wq'], 'L0_attn_bq': _L0_attn_in['bq'], 'L0_attn_Wk': _L0_attn_in['Wk'], 'L0_attn_bk': _L0_attn_in['bk'], 'L0_attn_Wv': _L0_attn_in['Wv'], 'L0_attn_bv': _L0_attn_in['bv'], 'L0_attn_Wo': _L0_attn_in['Wo'], 'L0_attn_bo': _L0_attn_in['bo'], 'L0_attn_gamma': _L0_attn_in['gamma'], 'L0_attn_beta': _L0_attn_in['beta'], 'L0_ffn_gate_w': _L0_ffn_in['gate_w'], 'L0_ffn_lattice_weights': _L0_ffn_in['lattice_weights'], 'L0_ffn_out_w': _L0_ffn_in['out_w'], 'L0_ffn_out_b': _L0_ffn_in['out_b'], 'L0_ffn_ln_g': _L0_ffn_in['ln_g'], 'L0_ffn_ln_b': _L0_ffn_in['ln_b'], 'L1_attn_wq': _L1_attn_in['wq'], 'L1_attn_wkv': _L1_attn_in['wkv'], 'L1_attn_wo': _L1_attn_in['wo'], 'L1_attn_q_norm_w': _L1_attn_in['q_norm_w'], 'L1_attn_k_norm_w': _L1_attn_in['k_norm_w'], 'L1_ffn_router_w': _L1_ffn_in['router_w'], 'L1_ffn_router_b': _L1_ffn_in['router_b'], 'L1_ffn_W1': _L1_ffn_in['W1'], 'L1_ffn_b1': _L1_ffn_in['b1'], 'L1_ffn_W2': _L1_ffn_in['W2'], 'L1_ffn_b2': _L1_ffn_in['b2'], 'L2_attn_Wq_comp': _L2_attn_in['Wq_comp'], 'L2_attn_Wkv_comp': _L2_attn_in['Wkv_comp'], 'L2_attn_Wqc': _L2_attn_in['Wqc'], 'L2_attn_Wqr': _L2_attn_in['Wqr'], 'L2_attn_Wkc': _L2_attn_in['Wkc'], 'L2_attn_Wkr': _L2_attn_in['Wkr'], 'L2_attn_Wv': _L2_attn_in['Wv'], 'L2_ffn_gate_w': _L2_ffn_in['gate_w'], 'L2_ffn_gate_b': _L2_ffn_in['gate_b'], 'L2_ffn_w1': _L2_ffn_in['w1'], 'L2_ffn_b1': _L2_ffn_in['b1'], 'L2_ffn_w2': _L2_ffn_in['w2'], 'L2_ffn_b2': _L2_ffn_in['b2'], 'L3_attn_Wq': _L3_attn_in['Wq'], 'L3_attn_bq': _L3_attn_in['bq'], 'L3_attn_Wk': _L3_attn_in['Wk'], 'L3_attn_bk': _L3_attn_in['bk'], 'L3_attn_Wv': _L3_attn_in['Wv'], 'L3_attn_bv': _L3_attn_in['bv'], 'L3_ffn_ln1_w': _L3_ffn_in['ln1_w'], 'L3_ffn_ln2_w': _L3_ffn_in['ln2_w'], 'L3_ffn_wq': _L3_ffn_in['wq'], 'L3_ffn_wk': _L3_ffn_in['wk'], 'L3_ffn_wv': _L3_ffn_in['wv'], 'L3_ffn_wo': _L3_ffn_in['wo'], 'L3_ffn_router_w': _L3_ffn_in['router_w'], 'L3_ffn_w1': _L3_ffn_in['w1'], 'L3_ffn_w2': _L3_ffn_in['w2'], 'L3_ffn_w3': _L3_ffn_in['w3']}

def reference(x, L0_tok_embed, L0_tok_Wg, L0_tok_Wu, L0_tok_Wd, L0_tok_lm_head, L0_attn_edge_index, L0_attn_Wq, L0_attn_bq, L0_attn_Wk, L0_attn_bk, L0_attn_Wv, L0_attn_bv, L0_attn_Wo, L0_attn_bo, L0_attn_gamma, L0_attn_beta, L0_ffn_gate_w, L0_ffn_lattice_weights, L0_ffn_out_w, L0_ffn_out_b, L0_ffn_ln_g, L0_ffn_ln_b, L1_attn_wq, L1_attn_wkv, L1_attn_wo, L1_attn_q_norm_w, L1_attn_k_norm_w, L1_ffn_router_w, L1_ffn_router_b, L1_ffn_W1, L1_ffn_b1, L1_ffn_W2, L1_ffn_b2, L2_attn_Wq_comp, L2_attn_Wkv_comp, L2_attn_Wqc, L2_attn_Wqr, L2_attn_Wkc, L2_attn_Wkr, L2_attn_Wv, L2_ffn_gate_w, L2_ffn_gate_b, L2_ffn_w1, L2_ffn_b1, L2_ffn_w2, L2_ffn_b2, L3_attn_Wq, L3_attn_bq, L3_attn_Wk, L3_attn_bk, L3_attn_Wv, L3_attn_bv, L3_ffn_ln1_w, L3_ffn_ln2_w, L3_ffn_wq, L3_ffn_wk, L3_ffn_wv, L3_ffn_wo, L3_ffn_router_w, L3_ffn_w1, L3_ffn_w2, L3_ffn_w3):
    import jax
    import jax.numpy as jnp

    def _L0_tok_ref(input_ids, embed, Wg, Wu, Wd, lm_head):
        import jax, jax.numpy as jnp
        import numpy as np
        MOE_DIM = 64
        MOE_INTER_DIM = 128
        N_EXPERTS = 4
        N_LAYERS = 2
        VOCAB = 64
        x = embed[input_ids]
        for l in range(N_LAYERS):
            g = jnp.einsum('bsd,efd->ebsf', x, Wg[l])
            u = jnp.einsum('bsd,efd->ebsf', x, Wu[l])
            h = jax.nn.silu(g) * u
            eo = jnp.einsum('ebsf,edf->ebsd', h, Wd[l])
            x = x + eo.mean(axis=0)
        logits = jnp.einsum('bsd,vd->bsv', x, lm_head)
        return logits

    def _L0_attn_ref(x, edge_index, Wq, bq, Wk, bk, Wv, bv, Wo, bo, gamma, beta):
        import jax, jax.numpy as jnp
        import numpy as np
        B, N, D, H = (2, 512, 64, 8)
        DH = D // H
        E = 16384
        EPS = 1e-05

        def _layer_norm(y, gamma, beta):
            mu = jnp.mean(y, axis=-1, keepdims=True)
            var = jnp.var(y, axis=-1, keepdims=True)
            return (y - mu) * jax.lax.rsqrt(var + EPS) * gamma + beta
        b, n, _ = x.shape
        scale = DH ** (-0.5)
        q = (x @ Wq + bq).reshape(b, n, H, DH)
        k = (x @ Wk + bk).reshape(b, n, H, DH)
        v = (x @ Wv + bv).reshape(b, n, H, DH)
        scores = jnp.einsum('bnhd,bmhd->bhnm', q, k) * scale
        diag = jnp.arange(n)
        mask = jnp.zeros((n, n), bool).at[diag, diag].set(True)
        mask = mask.at[edge_index[0], edge_index[1]].set(True)
        scores = jnp.where(mask[None, None], scores, -jnp.inf)
        w = jax.nn.softmax(scores, axis=-1)
        attended = jnp.einsum('bhnm,bmhd->bnhd', w, v).reshape(b, n, D)
        out = attended @ Wo + bo
        return _layer_norm(out + x, gamma, beta)

    def _L0_ffn_ref(x, gate_w, lattice_weights, out_w, out_b, ln_g, ln_b):
        import jax, jax.numpy as jnp
        import numpy as np
        TOP_K = 6
        LN_EPS = 1e-05
        logits = jnp.einsum('bsd,ed->bse', x, gate_w)
        top_logits, indices = jax.lax.top_k(logits, TOP_K)
        scores = jax.nn.softmax(top_logits, axis=-1)
        W_sel = lattice_weights[indices]
        xW = jnp.einsum('bsd,bskde->bske', x, W_sel)
        lattice_out = jnp.einsum('bske,bsk->bse', xW, scores)
        proj = jnp.einsum('bsd,ed->bse', lattice_out, out_w) + out_b
        h = x + proj
        mu = jnp.mean(h, axis=-1, keepdims=True)
        var = jnp.mean(jnp.square(h - mu), axis=-1, keepdims=True)
        return (h - mu) * jax.lax.rsqrt(var + LN_EPS) * ln_g + ln_b

    def _L1_attn_ref(x, wq, wkv, wo, q_norm_w, k_norm_w):
        import jax, jax.numpy as jnp
        import numpy as np
        import math
        B, T, D_MODEL = (1, 512, 64)
        N_Q, N_KV = (16, 1)
        D_HEAD = D_MODEL // N_KV
        QPG = N_Q // N_KV
        ROPE_BASE = 10000.0
        WINDOW = 128
        EPS = 1.1920929e-07
        NEG = -1e+30

        def _rope(x, base=ROPE_BASE):
            t, d = (x.shape[-2], x.shape[-1])
            freqs = base ** (-2.0 * jnp.arange(d // 2, dtype=jnp.float32) / d)
            theta = jnp.arange(t, dtype=jnp.float32)[:, None] * freqs[None, :]
            cos, sin = (jnp.cos(theta), jnp.sin(theta))
            x1, x2 = (x[..., 0::2], x[..., 1::2])
            r1 = x1 * cos - x2 * sin
            r2 = x1 * sin + x2 * cos
            return jnp.stack([r1, r2], axis=-1).reshape(x.shape)

        def _rmsnorm(x, w):
            return x * jax.lax.rsqrt(jnp.mean(x * x, axis=-1, keepdims=True) + EPS) * w
        Bx, Tx, C = x.shape
        q = x @ wq.T
        kv = x @ wkv.T
        k, v = (kv[..., :N_KV * D_HEAD], kv[..., N_KV * D_HEAD:])
        q = q.reshape(Bx, Tx, QPG, N_KV, D_HEAD).transpose(0, 2, 3, 1, 4)
        k = k.reshape(Bx, Tx, 1, N_KV, D_HEAD).transpose(0, 2, 3, 1, 4)
        v = v.reshape(Bx, Tx, 1, N_KV, D_HEAD).transpose(0, 2, 3, 1, 4)
        q = _rmsnorm(_rope(q), q_norm_w)
        k = _rmsnorm(_rope(k), k_norm_w)
        rows = jnp.arange(Tx)[:, None]
        cols = jnp.arange(Tx)[None, :]
        mask = (cols <= rows) & (rows - cols <= WINDOW)
        scale = 1.0 / math.sqrt(D_HEAD)
        scores = jnp.einsum('bqgtd,bqgsd->bqgts', q, k) * scale
        scores = jnp.where(mask[None, None, None], scores, NEG)
        attn = jax.nn.softmax(scores, axis=-1)
        out = jnp.einsum('bqgts,bqgsd->bqgtd', attn, v)
        out = out.transpose(0, 3, 1, 2, 4).reshape(Bx, Tx, QPG * N_KV * D_HEAD)
        return out @ wo.T

    def _L1_ffn_ref(x, router_w, router_b, W1, b1, W2, b2):
        import jax, jax.numpy as jnp
        import numpy as np
        B, K, D = (128, 16, 64)
        E = 32
        H = int(D * 0.25)
        xf = x.reshape(-1, D)
        logits = xf @ router_w.T + router_b
        idx = jnp.argmax(logits, axis=-1)
        w1t = jnp.take(W1, idx, axis=0)
        h = jnp.einsum('nd,ndh->nh', xf, w1t) + jnp.take(b1, idx, axis=0)
        h = jax.nn.relu(h)
        w2t = jnp.take(W2, idx, axis=0)
        out = jnp.einsum('nh,nhd->nd', h, w2t) + jnp.take(b2, idx, axis=0)
        out = jax.nn.relu(out)
        return out.reshape(x.shape)

    def _L2_attn_ref(x, Wq_comp, Wkv_comp, Wqc, Wqr, Wkc, Wkr, Wv):
        import jax, jax.numpy as jnp
        import numpy as np
        HEAD_SIZE = 64
        HEAD_SIZE_R = HEAD_SIZE // 4
        HEAD_SIZE_C = HEAD_SIZE - HEAD_SIZE_R
        N_EMBD = 64

        def rope(x, start_pos=0):
            B, T, d = x.shape
            half = d // 2
            theta = 1.0 / 10000.0 ** (jnp.arange(half, dtype=x.dtype) / half)
            idx = jnp.arange(start_pos, start_pos + T, dtype=x.dtype)[:, None] * theta[None, :]
            sin, cos = (jnp.sin(idx), jnp.cos(idx))
            xs = x.reshape(B, T, half, 2)
            x1, x2 = (xs[..., 0], xs[..., 1])
            rot = jnp.stack([x1 * cos - x2 * sin, x1 * sin + x2 * cos], axis=-1)
            return rot.reshape(B, T, d)

        def _reference_tuple_inner(x, Wq_comp, Wkv_comp, Wqc, Wqr, Wkc, Wkr, Wv):
            c_q = x @ Wq_comp
            c_kv = x @ Wkv_comp
            q_c = c_q @ Wqc
            q_r = rope(c_q @ Wqr, start_pos=0)
            q = jnp.concatenate([q_c, q_r], axis=-1)
            k_c = c_kv @ Wkc
            k_r = rope(c_kv @ Wkr, start_pos=0)
            k = jnp.concatenate([k_c, k_r], axis=-1)
            v = c_kv @ Wv
            scale = 1.0 / jnp.sqrt(jnp.asarray(HEAD_SIZE, dtype=x.dtype))
            wei = jnp.einsum('bqd,bkd->bqk', q, k) * scale
            T_q = q.shape[1]
            mask = jnp.tril(jnp.ones((T_q, T_q), dtype=bool))
            wei = jnp.where(mask, wei, jnp.asarray(-jnp.inf, dtype=wei.dtype))
            wei = jax.nn.softmax(wei, axis=-1)
            out = jnp.einsum('bqk,bkd->bqd', wei, v)
            return (out, (k, v))
        return _reference_tuple_inner(x, Wq_comp, Wkv_comp, Wqc, Wqr, Wkc, Wkr, Wv)[0]

    def _L2_ffn_ref(h, gate_w, gate_b, w1, b1, w2, b2):
        import math
        import jax, jax.numpy as jnp
        import numpy as np
        CAPACITY_FACTOR = 1.25
        B, L, D = h.shape
        E = gate_w.shape[1]
        T = B * L
        C = max(1, math.ceil(CAPACITY_FACTOR * T / E))
        x = h.reshape(T, D)
        logits = x @ gate_w + gate_b
        probs = jax.nn.softmax(logits, axis=-1)
        idx = jnp.argmax(probs, axis=-1)
        prb = jnp.take_along_axis(probs, idx[:, None], axis=1)[:, 0]
        one_hot = jax.nn.one_hot(idx, E, dtype=jnp.float32)
        pos = (jnp.cumsum(one_hot, axis=0) * one_hot).sum(-1).astype(jnp.int32) - 1
        kept = pos < C
        pos_safe = jnp.where(kept, pos, C)
        buf = jnp.zeros((E, C, D), dtype=h.dtype).at[idx, pos_safe].set(x, mode='drop')
        hmid = jax.nn.relu(jnp.einsum('ecd,edf->ecf', buf, w1) + b1[:, None, :])
        ybuf = jnp.einsum('ecf,efd->ecd', hmid, w2) + b2[:, None, :]
        pos_g = jnp.minimum(pos, C - 1)
        y_tok = ybuf[idx, pos_g] * (prb * kept)[:, None]
        y = y_tok.reshape(B, L, D)
        y = jnp.nan_to_num(y, nan=0.0, posinf=10000.0, neginf=-10000.0)
        return y

    def _L3_attn_ref(x, Wq, bq, Wk, bk, Wv, bv):
        import jax, jax.numpy as jnp
        import numpy as np
        Q = jnp.einsum('bsd,de->bse', x, Wq) + bq
        K = jnp.einsum('bsd,de,->bse'.replace(',->', '->'), x, Wk) + bk
        V = jnp.einsum('bsd,de->bse', x, Wv) + bv
        scale = 1.0 / jnp.sqrt(jnp.asarray(Q.shape[-1], dtype=jnp.float32))
        scores = jnp.einsum('bqd,bkd->bqk', Q, K) * scale
        weights = jax.nn.softmax(scores, axis=-1)
        return jnp.einsum('bqk,bkd->bqd', weights, V)

    def _L3_ffn_ref(x, ln1_w, ln2_w, wq, wk, wv, wo, router_w, w1, w2, w3):
        import jax, jax.numpy as jnp
        import numpy as np
        B, T, C = (64, 96, 64)
        NH, NKV = (4, 2)
        HD = C // NH
        NREP = NH // NKV
        NE, TOPK = (8, 2)
        HID = int(8 / 3 * C)
        EPS_RMS = 1e-06

        def _rope_tables(t_len):
            inv_freq = 1.0 / 10000.0 ** (np.arange(0, HD, 2, dtype=np.float32) / HD)
            t = np.arange(t_len, dtype=np.float32)
            freqs = np.outer(t, inv_freq)
            emb = np.concatenate([freqs, freqs], axis=-1)
            return (jnp.asarray(np.cos(emb)), jnp.asarray(np.sin(emb)))

        def _rotate_half(x):
            h = x.shape[-1] // 2
            return jnp.concatenate([-x[..., h:], x[..., :h]], axis=-1)

        def _rmsnorm(v, w):
            return v * jax.lax.rsqrt(jnp.mean(v * v, axis=-1, keepdims=True) + EPS_RMS) * w
        Bx, Tx, Cx = x.shape
        h = _rmsnorm(x, ln1_w)
        q = (h @ wq.T).reshape(Bx, Tx, NH, HD).transpose(0, 2, 1, 3)
        k = (h @ wk.T).reshape(Bx, Tx, NKV, HD).transpose(0, 2, 1, 3)
        v = (h @ wv.T).reshape(Bx, Tx, NKV, HD).transpose(0, 2, 1, 3)
        cos, sin = _rope_tables(Tx)
        cos, sin = (cos[None, None], sin[None, None])
        q = q * cos + _rotate_half(q) * sin
        k = k * cos + _rotate_half(k) * sin
        k = jnp.repeat(k, NREP, axis=1)
        v = jnp.repeat(v, NREP, axis=1)
        scores = jnp.einsum('bhtd,bhsd->bhts', q, k) / jnp.sqrt(jnp.float32(HD))
        causal = jnp.tril(jnp.ones((Tx, Tx), dtype=bool))
        scores = jnp.where(causal[None, None], scores, jnp.float32(-1e+30))
        att = jax.nn.softmax(scores, axis=-1)
        y = jnp.einsum('bhts,bhsd->bhtd', att, v).transpose(0, 2, 1, 3).reshape(Bx, Tx, Cx)
        x = x + y @ wo.T
        flat = _rmsnorm(x, ln2_w).reshape(-1, Cx)
        probs = jax.nn.softmax(flat @ router_w.T, axis=-1)
        tp, ti = jax.lax.top_k(probs, TOPK)
        tp = tp / (jnp.sum(tp, axis=-1, keepdims=True) + 1e-09)
        weights = jnp.sum(tp[..., None] * jax.nn.one_hot(ti, NE, dtype=flat.dtype), axis=1)
        out = jnp.zeros_like(flat)
        for e in range(NE):
            hh = jax.nn.silu(flat @ w1[e].T) * (flat @ w3[e].T)
            out = out + weights[:, e:e + 1] * (hh @ w2[e].T)
        return x + out.reshape(Bx, Tx, Cx)
    h = _L0_tok_ref(x, L0_tok_embed, L0_tok_Wg, L0_tok_Wu, L0_tok_Wd, L0_tok_lm_head)
    h = h + _L0_attn_ref(_layernorm(h, axis=-1), L0_attn_edge_index, L0_attn_Wq, L0_attn_bq, L0_attn_Wk, L0_attn_bk, L0_attn_Wv, L0_attn_bv, L0_attn_Wo, L0_attn_bo, L0_attn_gamma, L0_attn_beta)
    h = h + _L0_ffn_ref(_layernorm(h, axis=-1), L0_ffn_gate_w, L0_ffn_lattice_weights, L0_ffn_out_w, L0_ffn_out_b, L0_ffn_ln_g, L0_ffn_ln_b)
    h = h + _L1_attn_ref(_layernorm(h, axis=-1), L1_attn_wq, L1_attn_wkv, L1_attn_wo, L1_attn_q_norm_w, L1_attn_k_norm_w)
    h = h + _L1_ffn_ref(_layernorm(h, axis=-1), L1_ffn_router_w, L1_ffn_router_b, L1_ffn_W1, L1_ffn_b1, L1_ffn_W2, L1_ffn_b2)
    h = h + _L2_attn_ref(_layernorm(h, axis=-1), L2_attn_Wq_comp, L2_attn_Wkv_comp, L2_attn_Wqc, L2_attn_Wqr, L2_attn_Wkc, L2_attn_Wkr, L2_attn_Wv)
    h = h + _L2_ffn_ref(_layernorm(h, axis=-1), L2_ffn_gate_w, L2_ffn_gate_b, L2_ffn_w1, L2_ffn_b1, L2_ffn_w2, L2_ffn_b2)
    h = h + _L3_attn_ref(_layernorm(h, axis=-1), L3_attn_Wq, L3_attn_bq, L3_attn_Wk, L3_attn_bk, L3_attn_Wv, L3_attn_bv)
    h = h + _L3_ffn_ref(_layernorm(h, axis=-1), L3_ffn_ln1_w, L3_ffn_ln2_w, L3_ffn_wq, L3_ffn_wk, L3_ffn_wv, L3_ffn_wo, L3_ffn_router_w, L3_ffn_w1, L3_ffn_w2, L3_ffn_w3)
    return h

_drawn_inputs = setup_inputs


def setup_inputs(seed=0):
    import zlib

    import numpy as np

    out = dict(_drawn_inputs(seed))
    spreads = {'L0_attn_bq': (0.0, 0.8),
     'L0_attn_bk': (0.0, 0.8),
     'L0_attn_bv': (0.0, 0.272),
     'L0_attn_bo': (0.0, 0.1),
     'L0_attn_gamma': (1.0, 0.2),
     'L0_attn_beta': (0.0, 0.1),
     'L0_ffn_out_b': (0.0, 0.1),
     'L0_ffn_ln_g': (1.0, 0.2),
     'L0_ffn_ln_b': (0.0, 0.1),
     'L1_attn_q_norm_w': (1.0, 0.6),
     'L1_attn_k_norm_w': (1.0, 0.6),
     'L2_ffn_gate_b': (0.0, 0.1),
     'L2_ffn_b1': (0.0, 0.8),
     'L2_ffn_b2': (0.0, 0.8),
     'L3_attn_bq': (0.0, 0.8),
     'L3_attn_bk': (0.0, 0.8),
     'L3_attn_bv': (0.0, 0.1),
     'L3_ffn_ln1_w': (1.0, 0.6),
     'L3_ffn_ln2_w': (1.0, 0.6)}
    factors = {'L0_tok_Wg': 8.0,
     'L0_tok_Wu': 8.0,
     'L0_tok_Wd': 8.0,
     'L0_attn_Wq': 8.0,
     'L0_attn_Wk': 8.0,
     'L0_attn_Wv': 4.512,
     'L0_ffn_gate_w': 6.874,
     'L0_ffn_lattice_weights': 5.981,
     'L0_ffn_out_w': 5.23,
     'L1_attn_wq': 3.622,
     'L1_attn_wo': 2.832,
     'L1_ffn_b1': 5.435,
     'L2_attn_Wq_comp': 8.0,
     'L2_attn_Wqc': 8.0,
     'L2_attn_Wqr': 8.0,
     'L2_attn_Wkc': 8.0,
     'L2_attn_Wkr': 8.0,
     'L3_attn_Wq': 8.0,
     'L3_attn_Wk': 8.0,
     'L3_attn_Wv': 3.558,
     'L3_ffn_wq': 8.0,
     'L3_ffn_wk': 8.0,
     'L3_ffn_wv': 8.0,
     'L3_ffn_wo': 8.0,
     'L3_ffn_router_w': 8.0,
     'L3_ffn_w1': 8.0,
     'L3_ffn_w2': 8.0,
     'L3_ffn_w3': 8.0}
    for name, (base, spread) in spreads.items():
        noise = np.random.default_rng([zlib.crc32(name.encode()), seed]).standard_normal(out[name].shape)
        drawn = base * np.exp(spread * noise) if base else spread * noise
        out[name] = jnp.asarray(drawn.astype(out[name].dtype))
    for name, factor in factors.items():
        out[name] = (out[name] * factor).astype(out[name].dtype)
    return out
```

```python
from contextlib import ExitStack

import numpy as np

import concourse.bass as bass
from concourse import mybir

F32 = mybir.dt.float32
BF16 = mybir.dt.bfloat16
I32 = mybir.dt.int32
ALU = mybir.AluOpType
ACT = mybir.ActivationFunctionType
AX = mybir.AxisListType

LAST_STAGE = 9
P = 128
D = 64
SEQS, T = 8, 256
CH = (0, 1)
TILES = (0, 1)
PASSES = SEQS // 2
NEG = -1e30
BIG = 3e38
EPS = 1e-5
HIDDEN3 = 170

TURN = {n: i for i, n in enumerate([
    "L0_attn_out", "L0_ffn_in", "L0_ffn_out", "L1_attn_in", "L1_ffn_in", "L2_attn_in", "L2_ffn_in",
    "L3_attn_in", "L3_qkv_in", "L3_attn_out", "L3_moe_in"])}
NORM = {n: i for i, n in enumerate([
    "L0_attn_post", "L0_ffn_pre", "L0_ffn_post", "L1_attn_pre", "L1_k", "L1_q0", "L1_q1", "L1_ffn_pre",
    "L2_attn_pre", "L2_ffn_pre", "L3_attn_pre", "L3_ffn_pre", "L3_rms1", "L3_rms2"])}
STEP = {"L1": 0, "L2": 8, "L3": 9, "L3f": 10}


def build(nc, dram, out, cols):
    with ExitStack() as ctx:
        def sb(name, shape, dt=F32):
            return ctx.enter_context(nc.sbuf_tensor(name, shape, dt))

        def sb2(name, shape, dt=F32):
            return [sb(f"{name}{c}", shape, dt) for c in CH]

        def sem(name):
            return ctx.enter_context(nc.semaphore(name))

        packs = {}
        for name, (arr, width) in cols["packs"].items():
            whole = sb("pack_" + name, [P if name == "early64" else arr, width])
            packs[name] = whole[0:arr, :]
            if name == "early64":
                h_all = whole[:, 0:2 * SEQS * D].rearrange("p (t d) -> p t d", d=D)

        def w(name, rows=None):
            pack, at, width, r = cols["pieces"][name]
            return packs[pack][0:(rows or r), at:at + width]

        ident = w("ident")
        cosq = w("cos_l1").rearrange("p (t f) -> p t f", t=2)
        sinq = w("sin_l1").rearrange("p (t f) -> p t f", t=2)
        cos2 = w("cos_l2").rearrange("p (t f) -> p t f", t=2)
        sin2 = w("sin_l2").rearrange("p (t f) -> p t f", t=2)
        cos3 = w("cos_l3").rearrange("p (t f) -> p t f", t=2)
        sin3 = w("sin_l3").rearrange("p (t f) -> p t f", t=2)
        vecs = sb("vecs", [P, 6, D])
        qk_norm = sb("qk_norm", [P, D])
        ident_b = sb("ident_b", [P, P], BF16)
        maskb = sb("maskb", [P, 3, P], BF16)
        tri_b = sb("tri_b", [P, P], BF16)
        ones_b = sb("ones_b", [P, P], BF16)
        sel_b = sb("sel_b", [8, 4, P], BF16)
        ones1 = sb("ones1", [1, P])
        half = sb("half", [P, 1])
        ids_bc = sb("ids_bc", [D, SEQS * T])
        ids_tok_i = sb("ids_tok_i", [P, 2 * SEQS], I32)
        ids_tok = sb("ids_tok", [P, 2 * SEQS])
        edges = sb("edges", [P, 2, P])
        iota_b = sb("iota_b", [P, T], BF16)
        diag_b = sb("diag_b", [P, 2, T], BF16)
        allow = sb("allow", [P, 2, T], BF16)

        tabT = sb("tabT", [D, D])
        tab_t = sb("tab_t", [P, 4, D])
        tab_a = sb("tab_a", [P, 4, D])
        tab_z = sb("tab_z", [P, 4, D])
        tabs = sb("tabs", [D, 2, D])
        tab_s = sb("tab_s", [D, 4])
        tab_q = sb("tab_q", [D, D])
        xtabT = sb("xtabT", [D + 1, 2, D])
        qtab = sb("qtab", [8, 8, D])
        ktab = sb("ktab", [8, 8, D])
        score_tab = sb("score_tab", [D, 8, D])
        vblk = sb("vblk", [P, 4, 2, 9])
        ln1w = w("ln1")
        ln2w = w("ln2")

        h = sb2("h", [P, 2, D])
        xn = sb2("xn", [P, 2, D])
        xd = sb2("xd", [P, 2, 2, D])
        xc = sb2("xc", [P, 2, D])
        sq = sb2("sq", [P, 2, D])
        st = sb2("st", [P, 4, 16])
        rstd = sb2("rstd", [P, 16])
        xT = sb2("xT", [D + 1, T])
        xT2 = sb2("xT2", [P, T])
        hotT = sb2("hotT", [D, T])
        hot = sb2("hot", [P, 2, D], BF16)
        pen = sb2("pen", [P, 2, D])
        sm = sb2("sm", [P, 2, 8, D])
        pT = sb2("pT", [P, 1024])
        lg = sb2("lg", [P, 2, 72])
        top = sb2("top", [P, 2, 8])
        pick = {k: sb2(f"pick{k}_", [P, 2, 8]) for k in (1, 2, 6)}
        rep = sb2("rep", [P, 2, 72])
        sel = sb2("sel", [P, 2, D])
        prob = sb2("prob", [P, 2, D])
        zb = [sb2(f"zb{j}", [P, 8, D]) for j in range(2)]
        zT = [sb2(f"zT{j}", [P, 512]) for j in range(2)]
        att = sb2("att", [P, 2, 1024])
        qT = sb2("qT", [P, 8, T])
        kk = sb2("kk", [P, 2, P])
        kkm = sb2("kkm", [P, 2, P])
        vv = sb2("vv", [P, 2, D])
        kd = sb2("kd", [P, 2, 2, D])
        kT = sb2("kT", [P, T])
        exs = sb2("exs", [P, 2, 16])
        mx = sb2("mx", [P, 4])
        nb = sb2("nb", [P, 4])
        rs = sb2("rs", [P, 4])
        rr = sb2("rr", [P, 16])
        pr = sb2("pr", [P, 768])
        prT = sb2("prT", [P, 768])
        mT = sb2("mT", [32, T])
        mTb = sb2("mTb", [8, T], BF16)
        mb = sb2("mb", [P, 2, 8], BF16)
        carry = sb("carry", [P, 8])
        gate = sb2("gate", [P, 2])
        keep = sb2("keep", [P, 2])
        fill = sb2("fill", [P, 2, D])
        bad = sb2("bad", [P, 2, D], I32)
        kd4 = sb2("kd4", [P, 2, 2, P])
        th = sb2("th", [P, 2, HIDDEN3])
        x3 = sb2("x3", [P, 2, D])

        ids_bc_i = att[0][0:D].rearrange("p a b -> p (a b)").bitcast(I32)
        edges_i = att[1][:, 0, 0:2 * P].bitcast(I32).rearrange("p (a b) -> p a b", a=2)
        hot_src, hot_dst = [qT[c][:].rearrange("p a b -> p (a b)").bitcast(BF16)
                            .rearrange("p (s u n) -> p s u n", s=2, u=8) for c in CH]
        qa = pT
        qb = [sm[c][:].rearrange("p t h v -> p (t h v)")[:, 0:1024] for c in CH]
        z1 = [att[c][:, :, 0:544] for c in CH]
        hid = [att[c][:].rearrange("p a b -> p (a b)")[:, 0:8 * HIDDEN3].rearrange("p (e f) -> p e f", e=8) for c in CH]

        ps = ctx.enter_context(nc.psum_tensor("ps", [P, 8, 512], F32))

        def bank(c, j):
            return ps[:, 4 * c + j, :]

        def banks2(c, j):
            return ps[:, 4 * c + j:4 * c + j + 2, :]

        early = sem("early_loaded")
        late = sem("late_loaded")
        vset = sem("vector_setup_step")
        iset = sem("iota_ready")
        edge_hot = sem("edge_hot_ready")
        edge_used = sem("edge_hot_used")
        tabmm = sem("table_product_ready")
        taba = sem("table_tanh_ready")
        tabv = sem("table_vector_ready")
        tabz = sem("table_hidden_ready")
        tabpow = sem("table_rstd_ready")
        consts = sem("constants_ready")
        ended = sem("pass_ended")
        opened = sem("pass_opened")
        stored = sem("stored")
        vstep = sem("vector_step")
        astep = sem("scalar_step")
        hotT_ready = sem("hotT_ready")
        hot_ready = sem("hot_ready")
        var_ready = sem("variance_ready")
        rstd_ready = sem("rstd_ready")
        rows_ready = sem("rows_ready")
        turned = sem("rows_turned")
        feat_ready = sem("features_ready")
        proj_ready = sem("projection_ready")
        a0_scores, a0_max, a0_exp, a0_probs, a0_probsT_ps, a0_probsT, a0_av = [
            sem("a0_" + n) for n in ("scores", "max", "exp", "probs", "probsT_ps", "probsT", "av")]
        shifted = sem("logits_shifted")
        expd = sem("logits_exp")
        z_ready, z_turned, zT_ready, zsum_ready = [sem("lattice_" + n) for n in ("z", "turned", "zT", "sum")]
        at_scores, at_bias, at_probs, at_turned, at_probsT, at_av, at_out = [
            sem("at_" + n) for n in ("scores", "bias", "probs", "turned", "probsT", "av", "out")]
        q_proj, q_used, q_sq_in, q_sq, q_roped, q_turned, qT_ready, k_turned, kT_ready = [
            sem("l1_" + n) for n in ("q_proj", "q_used", "sq_in", "sq", "roped", "turned", "qT", "k_turned", "kT")]
        ao_turned, ao_ready, ao_rows = [sem("l1_out_" + n) for n in ("turned", "ready", "rows")]
        f1_z, f1_turned, f1_zT = [sem("f1_" + n) for n in ("z", "turned", "zT")]
        c2_ready, c2_used = sem("l2_c_ready"), sem("l2_c_used")
        qk_rows, qk_turned, qk_ready = [sem("qk_" + n) for n in ("rows", "turned", "ready")]
        f2_count, f2_maskT, f2_mask, f2_bc, f2_xm, f2_hid, f2_relu, f2_y = [
            sem("f2_" + n) for n in ("count", "maskT_ps", "maskT", "bc", "xm", "hid", "relu", "y")]
        f2_hot = sem("f2_hot")
        f4_gu, f4_tanh, f4_h, f4_turned, f4_hT = [sem("f4_" + n) for n in ("gu", "tanh", "h", "turned", "hT")]
        loop_sems = [vstep, astep, hotT_ready, hot_ready, var_ready, rstd_ready, rows_ready, turned, feat_ready,
                     proj_ready, a0_scores, a0_max, a0_exp, a0_probs, a0_probsT_ps, a0_probsT, a0_av, shifted, expd,
                     z_ready, z_turned, zT_ready, zsum_ready, at_scores, at_bias, at_probs, at_turned, at_probsT,
                     at_av, at_out, q_proj, q_used, q_sq_in, q_sq, q_roped, q_turned, qT_ready, k_turned, kT_ready,
                     ao_turned, ao_ready, ao_rows, f1_z, f1_turned, f1_zT, c2_ready, c2_used, qk_rows, qk_turned,
                     qk_ready, f2_count, f2_maskT, f2_mask, f2_bc, f2_xm, f2_hid, f2_relu, f2_y, f2_hot, f4_gu,
                     f4_tanh, f4_h, f4_turned, f4_hT, ended]

        class Steps:
            def __init__(self, eng, s):
                self.eng, self.s, self.n = eng, s, 0

            def done(self, ins):
                ins.then_inc(self.s, 1)
                self.n += 1
                return self.n

            def after(self, n=None):
                self.eng.wait_ge(self.s, n or self.n)

        def nth(n, c):
            return 2 * n + c + 1

        def close_pass(eng, i):
            eng.drain().then_inc(ended, 1)
            eng.wait_ge(opened, i + 1)

        def blocks(full):
            return [(0, 0), (0, 1), (1, 0), (1, 1)] if full else [(0, 0), (1, 0), (1, 1)]

        block = ctx.enter_context(nc.Block())

        @block.sync
        def _(sp):
            sp.dma_start(edges_i, dram["edges"]).then_inc(early, 16)
            sp.dma_start(ids_bc_i, dram["ids"].rearrange("(a n) -> a n", a=1).to_broadcast([D, SEQS * T])
                         ).then_inc(early, 16)
            sp.dma_start(ids_tok_i[:], dram["ids_tok"]).then_inc(early, 16)
            sp.dma_start(vecs[:], dram["vecs"].rearrange("(a v) d -> a v d", a=1).to_broadcast([P, 6, D])
                         ).then_inc(early, 16)
            for name in ("early128", "early64", "early65"):
                sp.dma_start(packs[name], dram[name]).then_inc(early, 16)
            for name in cols["packs"]:
                if not name.startswith("early"):
                    sp.dma_start(packs[name], dram[name]).then_inc(late, 16)
            sp.wait_ge(opened, PASSES)
            sp.dma_start(out.rearrange("(t p) d -> p t d", p=P), h_all).then_inc(stored, 16)
            sp.wait_ge(stored, 16)

        EARLY = 16 * 7
        LATE = 16 * sum(not n.startswith("early") for n in cols["packs"])

        @block.gpsimd
        def _(pool):
            nc.gpsimd.iota(iota_b[:], [[1, T]], base=0, channel_multiplier=0,
                           allow_small_or_imprecise_dtypes=True).then_inc(iset, 1)
            nc.gpsimd.memset(half[:], -0.5).then_inc(iset, 1)
            nc.gpsimd.memset(carry[:], 0.0).then_inc(iset, 1)
            nc.gpsimd.memset(ones1[:], 1.0).then_inc(iset, 1)
            pool.wait_ge(iset, 4)
            pool.wait_ge(tabv, 1)
            nc.gpsimd.tensor_tensor(tab_s[:, 3:4], tab_s[:, 2:3], half[0:D, :], ALU.pow).then_inc(tabpow, 1)
            with pool.Fori(0, PASSES) as i:
                def rsqrt(n, width):
                    for c in CH:
                        pool.wait_ge(var_ready, nth(n, c))
                        nc.gpsimd.tensor_tensor(rstd[c][:, 0:width], st[c][:, 2, 0:width],
                                                half[:, 0:1].to_broadcast([P, width]),
                                                ALU.pow).then_inc(rstd_ready, 1)
                stages = [["L0_attn_post"], ["L0_ffn_pre", "L0_ffn_post"],
                          ["L1_attn_pre", "L1_k", "L1_q0", "L1_q1"], ["L1_ffn_pre"], ["L2_attn_pre"], ["L2_ffn_pre"],
                          ["L3_attn_pre"], ["L3_ffn_pre", "L3_rms1", "L3_rms2"]]
                for names in stages[0:LAST_STAGE - 1]:
                    for n in names:
                        rsqrt(NORM[n], 16 if n in ("L1_q0", "L1_q1") else 2)
                pool.wait_ge(ended, 3)
                for s in loop_sems:
                    pool.sem_clear(s)
                pool.nop().then_inc(opened, 1)

        @block.tensor
        def _(pe):
            def mm(o, l, r, start=True, stop=True, **k):
                return nc.tensor.matmul(o, l, r, start=start, stop=stop, **k)

            def turn(o, i):
                k = i.shape[0]
                return nc.tensor.transpose(o, i, ident[0:k, 0:k])

            pe.wait_ge(consts, 1)
            for j in TILES:
                mm(ps[:, j, 0:T], ident_b[:], diag_b[:, j, :], start=True, stop=False).then_inc(edge_used, 1)
            with pe.Fori(0, 8) as i:
                for half_ in range(2):
                    pe.wait_ge(edge_hot, i * 2 + half_ + 1)
                    for u in range(8):
                        for j in TILES:
                            last = mm(ps[:, j, 0:T], hot_dst[:, half_, u, j * P:(j + 1) * P], hot_src[:, half_, u, :],
                                      start=False, stop=False)
                    last.then_inc(edge_used, 1)
            for j in TILES:
                last = mm(ps[:, j, 0:T], ident_b[:], diag_b[:, j, :], start=False, stop=True)
            last.then_inc(tabmm, 1)

            WgT = w("WgT").rearrange("p (l e f) -> p l e f", l=2, e=4)
            WuT = w("WuT").rearrange("p (l e f) -> p l e f", l=2, e=4)
            WdT = w("WdT").rearrange("p (l e d) -> p l e d", l=2, e=4)
            for l in range(2):
                pe.wait_ge(consts, 2 + l)
                for e in range(4):
                    mm(ps[:, 2, e * D:(e + 1) * D], WgT[:, l, e, :], tabT[:])
                for e in range(4):
                    last = mm(ps[:, 3, e * D:(e + 1) * D], WuT[:, l, e, :], tabT[:])
                last.then_inc(tabmm, 1)
                pe.wait_ge(tabz, l + 1)
                for e in range(4):
                    last = mm(ps[0:D, 4, 0:D], WdT[:, l, e, :], tab_z[:, e, :], start=(e == 0), stop=(e == 3))
                last.then_inc(tabmm, 1)
            pe.wait_ge(consts, 4)
            mm(ps[0:D, 5, 0:D], tabT[:], w("lmT")).then_inc(tabmm, 1)
            pe.wait_ge(consts, 5)
            turn(ps[0:D, 6, 0:D], tabs[:, 1, :]).then_inc(tabmm, 1)
            pe.wait_ge(consts, 6)
            for hd in range(8):
                mm(ps[0:8, 2, hd * D:(hd + 1) * D], w("L0_Wq")[:, 8 * hd:8 * hd + 8], xtabT[:, 0, :])
                mm(ps[0:8, 3, hd * D:(hd + 1) * D], w("L0_Wk")[:, 8 * hd:8 * hd + 8], xtabT[:, 0, :])
            mm(ps[:, 4, 0:D], xtabT[:].rearrange("p a b -> p (a b)"), w("L0_Wv")).then_inc(tabmm, 1)
            pe.wait_ge(consts, 7)
            for hd in range(8):
                last = mm(ps[0:D, 5, hd * D:(hd + 1) * D], qtab[:, hd, :], ktab[:, hd, :])
            last.then_inc(tabmm, 1)
            pe.wait_ge(consts, 8)
            pe.wait_ge(late, LATE)

            def features(name, src, width=D):
                n = TURN[name]
                for c in CH:
                    pe.wait_ge(rows_ready, nth(n, c))
                    for t in TILES:
                        last = turn(bank(c, 3)[0:width, t * P:(t + 1) * P], src[c][:, t, 0:width])
                    last.then_inc(turned, 1)

            def project(n, lhs, weight, at=2):
                width = weight.shape[1]
                for c in CH:
                    pe.wait_ge(feat_ready, nth(n, c))
                    for t in TILES:
                        last = mm(bank(c, at)[:, t * width:(t + 1) * width], lhs[c][0:weight.shape[0], t * P:(t + 1) * P], weight)
                    last.then_inc(proj_ready, 1)

            def attention(step, q, k, v, heads, full, mask, dv):
                bl = blocks(full)
                for c in CH:
                    if step > 0:
                        pe.wait_ge(at_out, nth(step - 1, c))
                    for e in range(heads):
                        at = 0
                        for t in TILES:
                            wd = T if full or t == 1 else P
                            o = bank(c, e)[:, at:at + wd]
                            last = mm(o, q(c, e, t), k(c, e)[:, 0:wd], start=True, stop=(mask is None))
                            if mask is not None:
                                first = mask[t]
                                for (b0, m) in first:
                                    last = mm(bank(c, e)[:, at + b0 * P:at + b0 * P + m.shape[1]], ident_b[:], m,
                                              start=False, stop=True)
                            at += wd
                    last.then_inc(at_scores, 1)
                for c in CH:
                    pe.wait_ge(at_probs, nth(step, c))
                    for e in range(heads):
                        for b in range(len(bl)):
                            x = e * len(bl) + b
                            last = turn(ps[:, 4 * c + 2 + x // 4, (x % 4) * P:(x % 4 + 1) * P],
                                        pr[c][:, x * P:(x + 1) * P])
                    last.then_inc(at_turned, 1)
                for c in CH:
                    pe.wait_ge(at_probsT, nth(step, c))
                    for e in range(heads):
                        for t in TILES:
                            mine = [(b, kt_) for b, (qt_, kt_) in enumerate(bl) if qt_ == t]
                            for z, (b, kt_) in enumerate(mine):
                                x = e * len(bl) + b
                                o = 256 + (e * 2 + t) * dv
                                last = mm(bank(c, 3)[:, o:o + dv], prT[c][:, x * P:(x + 1) * P], v(c, e, kt_),
                                          start=(z == 0), stop=(z == len(mine) - 1))
                    last.then_inc(at_av, 1)

            causal = {0: [(0, maskb[:, 0, :])], 1: [(1, maskb[:, 0, :])]}
            window = {0: [(0, maskb[:, 0, :])], 1: [(0, maskb[:, 1:3, :].rearrange("p a b -> p (a b)"))]}

            with pe.Fori(0, PASSES) as i:
                for c in CH:
                    pe.wait_ge(hotT_ready, c + 1)
                    pe.wait_ge(hot_ready, c + 1)
                    for t in TILES:
                        mm(bank(c, t), hotT[c][:, t * P:(t + 1) * P], score_tab[:].rearrange("p a b -> p (a b)"))
                    for t in TILES:
                        mm(bank(c, 2)[:, t * P:(t + 1) * P], hotT[c][:, t * P:(t + 1) * P],
                           tabs[:].rearrange("p a b -> p (a b)"))
                    for t in TILES:
                        for j in TILES:
                            last = mm(bank(c, 3)[:, t * D:(t + 1) * D], allow[:, j, t * P:(t + 1) * P], hot[c][:, j, :],
                                      start=(j == 0), stop=(j == 1))
                    last.then_inc(a0_scores, 1)
                if LAST_STAGE >= 2:
                    for c in CH:
                        pe.wait_ge(a0_probs, c + 1)
                        for t in TILES:
                            for hp in range(4):
                                last = turn(bank(c, t)[:, hp * P:(hp + 1) * P],
                                            sm[c][:, t, 2 * hp:2 * hp + 2, :].rearrange("p a b -> p (a b)"))
                        last.then_inc(a0_probsT_ps, 1)
                    for c in CH:
                        pe.wait_ge(a0_probsT, c + 1)
                        for t in TILES:
                            for hp in range(4):
                                o = t * 72 + hp * 18
                                last = mm(bank(c, 2)[:, o:o + 18], pT[c][:, t * 512 + hp * P:t * 512 + (hp + 1) * P],
                                          vblk[:, hp, :, :].rearrange("p a b -> p (a b)"))
                        last.then_inc(a0_av, 1)
                    features("L0_attn_out", [att[c][:, :, 0:D] for c in CH])
                    project(TURN["L0_attn_out"], xT, w("L0_Wo"))
                if LAST_STAGE >= 3:
                    features("L0_ffn_in", xn)
                    project(TURN["L0_ffn_in"], xT, w("L0_gate"))
                    lat = w("lattice").rearrange("p (e o) -> p e o", o=D)
                    for x in range(16):
                        t, k8 = x // 8, x % 8
                        for c in CH:
                            pe.wait_ge(z_ready, nth(x, c))
                            if x >= 2:
                                pe.wait_ge(zT_ready, nth(x - 2, c))
                            for q in range(4):
                                last = turn(bank(c, x % 2)[:, q * P:(q + 1) * P],
                                            zb[x % 2][c][:, 2 * q:2 * q + 2, :].rearrange("p a b -> p (a b)"))
                            last.then_inc(z_turned, 1)
                        for c in CH:
                            pe.wait_ge(zT_ready, nth(x, c))
                            for q in range(4):
                                last = mm(bank(c, 2)[:, t * D:(t + 1) * D], zT[x % 2][c][:, q * P:(q + 1) * P],
                                          lat[:, k8 * 4 + q, :], start=(k8 == 0 and q == 0), stop=(k8 == 7 and q == 3))
                            last.then_inc(zsum_ready, 1)
                    features("L0_ffn_out", xc)
                    project(TURN["L0_ffn_out"], xT, w("L0_out"))
                if LAST_STAGE >= 4:
                    features("L1_attn_in", xn)
                    n = TURN["L1_attn_in"]
                    project(n, xT, w("L1_wkv"))
                    for c in CH:
                        for hf in range(2):
                            last = mm(bank(c, hf), xT[c][0:D, 0:P], w("L1_wq")[:, hf * 512:(hf + 1) * 512])
                        last.then_inc(q_proj, 1)
                    for c in CH:
                        pe.wait_ge(q_used, c + 1)
                        for hf in range(2):
                            last = mm(bank(c, hf), xT[c][0:D, P:T], w("L1_wq")[:, hf * 512:(hf + 1) * 512])
                        last.then_inc(q_proj, 1)
                    for c in CH:
                        pe.wait_ge(qk_rows, nth(0, c))
                        for t in TILES:
                            last = turn(bank(c, 3)[:, t * P:(t + 1) * P], kd[c][:, t].rearrange("p a b -> p (a b)"))
                        last.then_inc(qk_turned, 1)
                    for t in TILES:
                        for c in CH:
                            pe.wait_ge(q_roped, nth(t, c))
                            pe.wait_ge(q_used, nth(1, c))
                            pe.wait_ge(qk_ready, nth(0, c))
                            if t == 1:
                                pe.wait_ge(qT_ready, nth(0, c))
                            for hp in range(8):
                                last = turn(ps[:, 4 * c + 0 + hp // 4, (hp % 4) * P:(hp % 4 + 1) * P],
                                            att[c][:, t, hp * P:(hp + 1) * P])
                            last.then_inc(q_turned, 1)
                    for c in CH:
                        pe.wait_ge(qT_ready, nth(1, c))
                    for s in range(8):
                        attention(STEP["L1"] + s,
                                  lambda c, e, t: qT[c][D * e:D * e + D, s, t * P:(t + 1) * P],
                                  lambda c, e: kT[c][D * e:D * e + D, :],
                                  lambda c, e, kt_: vv[c][:, kt_, :], 2, False, window, D)
                    for t in TILES:
                        for c in CH:
                            pe.wait_ge(at_out, nth(STEP["L1"] + 7, c))
                            if t == 1:
                                pe.wait_ge(ao_ready, nth(0, c))
                            for hp in range(8):
                                last = turn(ps[:, 4 * c + hp // 4, (hp % 4) * P:(hp % 4 + 1) * P],
                                            att[c][:, t, hp * P:(hp + 1) * P])
                            last.then_inc(ao_turned, 1)
                    for t in TILES:
                        for c in CH:
                            pe.wait_ge(ao_ready, nth(t, c))
                            for hp in range(8):
                                last = mm(bank(c, 2)[:, t * D:(t + 1) * D], qT[c][:, hp, t * P:(t + 1) * P],
                                          w("L1_wo")[:, hp * D:(hp + 1) * D], start=(hp == 0), stop=(hp == 7))
                            last.then_inc(ao_rows, 1)
                if LAST_STAGE >= 5:
                    features("L1_ffn_in", xn)
                    project(TURN["L1_ffn_in"], xT, w("L1_router"))
                    for c in CH:
                        for t in TILES:
                            last = mm(bank(c, t), xT[c][:, t * P:(t + 1) * P], w("L1_W1"))
                        last.then_inc(q_proj, 1)
                    for c in CH:
                        pe.wait_ge(f1_z, c + 1)
                        for t in TILES:
                            for k4 in range(4):
                                turn(bank(c, t)[:, k4 * P:(k4 + 1) * P], z1[c][:, t, k4 * P:(k4 + 1) * P])
                            last = turn(bank(c, 3)[0:32, t * P:(t + 1) * P], z1[c][:, t, 512:544])
                        last.then_inc(f1_turned, 1)
                    for c in CH:
                        pe.wait_ge(f1_zT, c + 1)
                        for t in TILES:
                            for k4 in range(4):
                                mm(bank(c, 2)[:, t * D:(t + 1) * D], pT[c][:, t * 512 + k4 * P:t * 512 + (k4 + 1) * P],
                                   w("L1_W2")[:, k4 * D:(k4 + 1) * D], start=(k4 == 0), stop=False)
                            last = mm(bank(c, 2)[:, t * D:(t + 1) * D], mT[c][:, t * P:(t + 1) * P], w("L1_b2"),
                                      start=False, stop=True)
                        last.then_inc(ao_rows, 1)
                if LAST_STAGE >= 6:
                    features("L2_attn_in", xn)
                    for c in CH:
                        pe.wait_ge(feat_ready, nth(TURN["L2_attn_in"], c))
                        mm(bank(c, 2)[0:D, 0:T], w("L2_Wqcomp"), xT[c][0:D, :])
                        mm(bank(c, 2)[0:D, T:2 * T], w("L2_Wkvcomp"), xT[c][0:D, :]).then_inc(c2_ready, 1)
                    for c in CH:
                        pe.wait_ge(c2_used, c + 1)
                        for t in TILES:
                            mm(bank(c, 0)[:, t * 192:t * 192 + D], pT[c][0:D, t * P:(t + 1) * P], w("L2_Wq"))
                            last = mm(bank(c, 0)[:, t * 192 + D:(t + 1) * 192], pT[c][0:D, T + t * P:T + (t + 1) * P],
                                      w("L2_Wkv"))
                        last.then_inc(q_proj, 1)
                    for c in CH:
                        pe.wait_ge(qk_rows, nth(1, c))
                        for g in range(2):
                            for t in TILES:
                                last = turn(bank(c, 3)[0:D, g * T + t * P:g * T + (t + 1) * P], kk[c][:, t, g * D:(g + 1) * D])
                        last.then_inc(qk_turned, 1)
                    for c in CH:
                        pe.wait_ge(qk_ready, nth(1, c))
                    attention(STEP["L2"], lambda c, e, t: pT[c][0:D, t * P:(t + 1) * P],
                              lambda c, e: pT[c][0:D, T:2 * T], lambda c, e, kt_: vv[c][:, kt_, :],
                              1, False, causal, D)
                if LAST_STAGE >= 7:
                    features("L2_ffn_in", [xd[c][:].rearrange("p t a d -> p t (a d)") for c in CH], P)
                    for c in CH:
                        pe.wait_ge(feat_ready, nth(TURN["L2_ffn_in"], c))
                        for t in TILES:
                            mm(bank(c, 2)[:, t * 8:(t + 1) * 8], xT2[c][0:D, t * P:(t + 1) * P], w("L2_gate")[0:D, :],
                               start=True, stop=False)
                            last = mm(bank(c, 2)[:, t * 8:(t + 1) * 8], ones1[:], w("L2_gateb"), start=False, stop=True)
                        last.then_inc(proj_ready, 1)
                    for c in CH:
                        pe.wait_ge(f2_hot, c + 1)
                        mm(bank(c, 2)[:, 32:40], tri_b[:], mb[c][:, 0, :])
                        mm(bank(c, 2)[:, 40:48], ones_b[:], mb[c][:, 0, :], start=True, stop=False)
                        mm(bank(c, 2)[:, 40:48], tri_b[:], mb[c][:, 1, :], start=False, stop=True)
                        mm(bank(c, 2)[:, 48:56], ones_b[:], mb[c][:, 0, :], start=True, stop=False)
                        mm(bank(c, 2)[:, 48:56], ones_b[:], mb[c][:, 1, :], start=False, stop=True).then_inc(f2_count, 1)
                        for t in TILES:
                            last = turn(bank(c, 3)[0:8, t * P:(t + 1) * P], sel[c][:, t, 0:8])
                        last.then_inc(f2_maskT, 1)
                    for c in CH:
                        pe.wait_ge(f2_mask, c + 1)
                        for pr_ in range(4):
                            last = mm(ps[:, 4 * c + pr_ // 2, (pr_ % 2) * T:(pr_ % 2 + 1) * T], sel_b[:, pr_, :], mTb[c][:])
                        last.then_inc(f2_bc, 1)
                    for c in CH:
                        pe.wait_ge(f2_xm, c + 1)
                        for m in range(2):
                            o = bank(c, 2)[:, m * T:(m + 1) * T]
                            for pr_ in range(4):
                                mm(o, w("L2_W1")[:, pr_ * 256 + m * P:pr_ * 256 + (m + 1) * P],
                                   pT[c][:, pr_ * T:(pr_ + 1) * T], start=(pr_ == 0), stop=False)
                            last = mm(o, w("L2_b1")[:, m * P:(m + 1) * P], mT[c][0:8, :], start=False, stop=True)
                        last.then_inc(f2_hid, 1)
                    for c in CH:
                        pe.wait_ge(f2_relu, c + 1)
                        for t in TILES:
                            for m in range(2):
                                mm(bank(c, t), qT[c][:, m, t * P:(t + 1) * P], w("L2_W2")[:, m * 512:(m + 1) * 512],
                                   start=(m == 0), stop=False)
                            last = mm(bank(c, t), ones1[:], w("L2_b2"), start=False, stop=True)
                        last.then_inc(f2_y, 1)
                if LAST_STAGE >= 8:
                    features("L3_attn_in", xn)
                    for c in CH:
                        pe.wait_ge(feat_ready, nth(TURN["L3_attn_in"], c))
                        mm(bank(c, 2)[0:D, 0:T], w("L3_Wq"), xT[c][:])
                        mm(bank(c, 2)[0:D, T:2 * T], w("L3_Wk"), xT[c][:])
                        for t in TILES:
                            last = mm(bank(c, 1)[:, t * D:(t + 1) * D], xT[c][:, t * P:(t + 1) * P], w("L3_Wv"))
                        last.then_inc(c2_ready, 1)
                    for c in CH:
                        pe.wait_ge(c2_used, nth(1, c))
                    attention(STEP["L3"], lambda c, e, t: pT[c][0:D, t * P:(t + 1) * P],
                              lambda c, e: pT[c][0:D, T:2 * T], lambda c, e, kt_: vv[c][:, kt_, :],
                              1, True, None, D)
                if LAST_STAGE >= 9:
                    features("L3_qkv_in", xc)
                    project(TURN["L3_qkv_in"], xT, w("L3_wqkv"))
                    for c in CH:
                        pe.wait_ge(qk_rows, nth(2, c))
                        for g in range(2):
                            for t in TILES:
                                last = turn(bank(c, 3)[:, g * T + t * P:g * T + (t + 1) * P],
                                            kd4[c][:, g, t, :])
                        last.then_inc(qk_turned, 1)
                    for c in CH:
                        pe.wait_ge(qk_ready, nth(2, c))
                    for s in range(2):
                        attention(STEP["L3f"] + s,
                                  lambda c, e, t: pT[c][32 * (2 * s + e):32 * (2 * s + e) + 32, t * P:(t + 1) * P],
                                  lambda c, e: pT[c][32 * (2 * s + e):32 * (2 * s + e) + 32, T:2 * T],
                                  lambda c, e, kt_: kk[c][:, kt_, 96 + 16 * s:112 + 16 * s], 2, False, causal, 16)
                    features("L3_attn_out", [att[c][:, :, 0:D] for c in CH])
                    project(TURN["L3_attn_out"], xT, w("L3_wo"))
                    features("L3_moe_in", xc)
                    project(TURN["L3_moe_in"], xT, w("L3_router"))
                    w13 = w("L3_w13").rearrange("p (e f) -> p e f", e=8)
                    for t in TILES:
                        for e2 in range(4):
                            for c in CH:
                                x = t * 4 + e2
                                if x >= 1:
                                    pe.wait_ge(f4_h, nth(x - 1, c))
                                for u in range(2):
                                    last = mm(bank(c, u)[:, 0:2 * HIDDEN3], xT[c][0:D, t * P:(t + 1) * P], w13[:, 2 * e2 + u, :])
                                last.then_inc(f4_gu, 1)
                        for part in range(3):
                            n_ = (4, 4, 3)[part]
                            for c in CH:
                                pe.wait_ge(f4_h, nth(t * 4 + 3, c))
                                if t * 3 + part >= 1:
                                    pe.wait_ge(f4_hT, nth(t * 3 + part - 1, c))
                                for u in range(n_):
                                    kx = part * 4 + u
                                    kw = P if kx < 10 else 80
                                    last = turn(bank(c, 3)[0:kw, u * P:(u + 1) * P], hid[c].rearrange("p a b -> p (a b)")[:, kx * P:kx * P + kw])
                                last.then_inc(f4_turned, 1)
                            for c in CH:
                                pe.wait_ge(f4_hT, nth(t * 3 + part, c))
                                for u in range(n_):
                                    kx = part * 4 + u
                                    kw = P if kx < 10 else 80
                                    wt = w("L3_w2")[:, kx * D:(kx + 1) * D] if kx < 10 else w("L3_w2t")
                                    last = mm(bank(c, 2)[:, t * D:(t + 1) * D], pT[c][0:kw, u * P:(u + 1) * P], wt,
                                              start=(kx == 0), stop=(kx == 10))
                                if part == 2:
                                    last.then_inc(ao_rows, 1)
                close_pass(pe, i)

        @block.scalar
        def _(act):
            a = nc.scalar.activation
            for l in range(2):
                act.wait_ge(tabmm, 2 + 2 * l)
                a(tab_t[:], ps[:, 2, 0:4 * D].rearrange("p (e v) -> p e v", e=4), ACT.Tanh, scale=0.5).then_inc(taba, 1)

            def features(name, width=D):
                n = TURN[name]
                for c in CH:
                    act.wait_ge(turned, nth(n, c))
                    dst = xT[c][0:D, :] if width == D else xT2[c][:]
                    a(dst, bank(c, 3)[0:width, 0:T], ACT.Copy).then_inc(feat_ready, 1)

            def logits_exp(n, width):
                for c in CH:
                    act.wait_ge(shifted, nth(n, c))
                    a(prob[c][:, :, 0:width], prob[c][:, :, 0:width], ACT.Exp).then_inc(expd, 1)

            def attention(step, heads, full, scale):
                nb_ = len(blocks(full))
                for c in CH:
                    act.wait_ge(at_bias, nth(step, c))
                    for e in range(heads):
                        for t in TILES:
                            at = 0 if t == 0 else (T if full else P)
                            wd = T if full or t == 1 else P
                            x = e * nb_ * P + at
                            last = a(pr[c][:, x:x + wd], bank(c, e)[:, at:at + wd], ACT.Exp,
                                     bias=nb[c][:, 2 * t + e:2 * t + e + 1], scale=scale(c, e, t),
                                     accum_out=rs[c][:, 2 * t + e:2 * t + e + 1])
                    last.then_inc(at_probs, 1)
                for c in CH:
                    act.wait_ge(at_turned, nth(step, c))
                    wd = heads * nb_ * P
                    a(prT[c][:, 0:wd], ps[:, 4 * c + 2:4 * c + 4, :].rearrange("p a b -> p (a b)")[:, 0:wd],
                      ACT.Copy).then_inc(at_probsT, 1)

            with act.Fori(0, PASSES) as i:
                if LAST_STAGE >= 2:
                    for c in CH:
                        act.wait_ge(a0_max, c + 1)
                        a(sm[c][:], sm[c][:], ACT.Exp, scale=8 ** -0.5).then_inc(a0_exp, 1)
                    for c in CH:
                        act.wait_ge(a0_probsT_ps, c + 1)
                        a(pT[c][:], banks2(c, 0).rearrange("p a b -> p (a b)"), ACT.Copy).then_inc(a0_probsT, 1)
                    features("L0_attn_out")
                if LAST_STAGE >= 3:
                    features("L0_ffn_in")
                    logits_exp(0, D)
                    for x in range(16):
                        for c in CH:
                            act.wait_ge(z_turned, nth(x, c))
                            if x >= 2:
                                act.wait_ge(zsum_ready, nth(x - 2, c))
                            a(zT[x % 2][c][:], bank(c, x % 2), ACT.Copy).then_inc(zT_ready, 1)
                    features("L0_ffn_out")
                if LAST_STAGE >= 4:
                    features("L1_attn_in")
                    for t in TILES:
                        for c in CH:
                            act.wait_ge(q_roped, nth(t, c))
                            if t == 1:
                                act.wait_ge(var_ready, nth(NORM["L1_q0"], c))
                            a(qa[c][:], att[c][:, t, :], ACT.Square).then_inc(q_sq, 1)
                    for c in CH:
                        act.wait_ge(qk_turned, nth(0, c))
                        a(kT[c][:], bank(c, 3)[:, 0:T], ACT.Copy).then_inc(qk_ready, 1)
                    for t in TILES:
                        for c in CH:
                            act.wait_ge(q_turned, nth(t, c))
                            a(qT[c][:, :, t * P:(t + 1) * P], banks2(c, 0).rearrange("p a (b q) -> p (a b) q", q=P),
                              ACT.Copy).then_inc(qT_ready, 1)
                    for s in range(8):
                        attention(STEP["L1"] + s, 2, False,
                                  lambda c, e, t: exs[c][:, t, 2 * s + e:2 * s + e + 1])
                    for t in TILES:
                        for c in CH:
                            act.wait_ge(ao_turned, nth(t, c))
                            a(qT[c][:, :, t * P:(t + 1) * P], banks2(c, 0).rearrange("p a (b q) -> p (a b) q", q=P),
                              ACT.Copy).then_inc(ao_ready, 1)
                if LAST_STAGE >= 5:
                    features("L1_ffn_in")
                    for c in CH:
                        act.wait_ge(f1_turned, c + 1)
                        a(pT[c][:], banks2(c, 0).rearrange("p a b -> p (a b)"), ACT.Copy)
                        a(mT[c][:], bank(c, 3)[0:32, 0:T], ACT.Copy).then_inc(f1_zT, 1)
                if LAST_STAGE >= 6:
                    features("L2_attn_in")
                    for c in CH:
                        act.wait_ge(c2_ready, c + 1)
                        a(pT[c][0:D, 0:512], bank(c, 2)[0:D, :], ACT.Copy).then_inc(c2_used, 1)
                    for c in CH:
                        act.wait_ge(qk_turned, nth(1, c))
                        a(pT[c][0:D, 0:512], bank(c, 3)[0:D, :], ACT.Copy).then_inc(qk_ready, 1)
                    attention(STEP["L2"], 1, False, lambda c, e, t: 0.125)
                if LAST_STAGE >= 7:
                    features("L2_ffn_in", P)
                    logits_exp(1, 8)
                    for c in CH:
                        act.wait_ge(f2_maskT, c + 1)
                        a(mT[c][0:8, :], bank(c, 3)[0:8, 0:T], ACT.Copy)
                        a(mTb[c][:], bank(c, 3)[0:8, 0:T], ACT.Copy).then_inc(f2_mask, 1)
                    for c in CH:
                        act.wait_ge(f2_hid, c + 1)
                        a(qT[c][:, 0:2, :], bank(c, 2).rearrange("p (m t) -> p m t", m=2), ACT.Relu).then_inc(f2_relu, 1)
                if LAST_STAGE >= 8:
                    features("L3_attn_in")
                    for c in CH:
                        act.wait_ge(c2_ready, nth(1, c))
                        a(pT[c][0:D, 0:512], bank(c, 2)[0:D, :], ACT.Copy)
                        a(vv[c][:], bank(c, 1)[:, 0:P].rearrange("p (t d) -> p t d", t=2), ACT.Copy).then_inc(c2_used, 1)
                    attention(STEP["L3"], 1, True, lambda c, e, t: 0.125)
                if LAST_STAGE >= 9:
                    features("L3_qkv_in")
                    for c in CH:
                        act.wait_ge(qk_turned, nth(2, c))
                        a(pT[c][:, 0:512], bank(c, 3), ACT.Copy).then_inc(qk_ready, 1)
                    for s in range(2):
                        attention(STEP["L3f"] + s, 2, False, lambda c, e, t: 0.25)
                    features("L3_attn_out")
                    features("L3_moe_in")
                    logits_exp(2, 8)
                    for t in TILES:
                        for e2 in range(4):
                            x = t * 4 + e2
                            for c in CH:
                                act.wait_ge(f4_gu, nth(x, c))
                                a(th[c][:], banks2(c, 0)[:, :, 0:HIDDEN3], ACT.Tanh, scale=0.5).then_inc(f4_tanh, 1)
                        for part in range(3):
                            for c in CH:
                                act.wait_ge(f4_turned, nth(t * 3 + part, c))
                                if part < 2:
                                    a(pT[c][:, 0:512], bank(c, 3), ACT.Copy).then_inc(f4_hT, 1)
                                else:
                                    a(pT[c][:, 0:256], bank(c, 3)[:, 0:256], ACT.Copy)
                                    a(pT[c][0:80, 256:384], bank(c, 3)[0:80, 256:384], ACT.Copy).then_inc(f4_hT, 1)
                close_pass(act, i)

        @block.vector
        def _(dve):
            v = nc.vector
            setup = Steps(dve, vset)
            dve.wait_ge(iset, 4)
            dve.wait_ge(early, EARLY)
            setup.done(v.tensor_copy(ids_bc[:], ids_bc_i))
            setup.done(v.tensor_copy(ids_tok[:], ids_tok_i[:]))
            setup.done(v.tensor_copy(edges[:], edges_i))
            setup.done(v.tensor_copy(ident_b[:], ident))
            setup.done(v.memset(diag_b[:], 0.0))
            setup.after()
            for j in TILES:
                setup.done(v.tensor_copy(diag_b[:, j, j * P:(j + 1) * P], ident))
                setup.done(v.tensor_copy(maskb[:, 2 * j, :], w("causal")))
            setup.done(v.tensor_copy(maskb[:, 1, :], w("window")))
            setup.done(v.tensor_copy(tri_b[:], w("tri")))
            setup.done(v.memset(ones_b[:], 1.0))
            setup.done(v.tensor_tensor(qk_norm[:], vecs[:, 4, :], vecs[:, 5, :], ALU.mult))
            setup.done(v.memset(vblk[:], 0.0))
            setup.done(v.memset(xtabT[D:D + 1, :, :], 1.0))
            for c in CH:
                setup.done(v.memset(xT[c][D:D + 1, :], 1.0))
                setup.done(v.memset(lg[c][:], BIG))
                for k in (1, 2, 6):
                    setup.done(v.memset(pick[k][c][:], BIG))
                setup.done(v.memset(kd4[c][:], 0.0))
            setup.after()
            dve.drain().then_inc(consts, 1)
            with dve.Fori(0, 8) as i:
                for half_ in range(2):
                    dve.wait_ge(edge_used, i * 2 + half_ + 1)
                    for u in range(8):
                        v.tensor_scalar(hot_src[:, half_, u, :], iota_b[:],
                                        edges[:, 0, bass.ds(i * 16 + (half_ * 8 + u), 1)], None, ALU.is_equal)
                        last = v.tensor_scalar(hot_dst[:, half_, u, :], iota_b[:],
                                               edges[:, 1, bass.ds(i * 16 + (half_ * 8 + u), 1)], None, ALU.is_equal)
                    last.then_inc(edge_hot, 1)
            v.tensor_copy(tabT[:], w("embT")).then_inc(consts, 1)
            dve.wait_ge(tabmm, 1)
            setup.done(v.tensor_scalar(allow[:], ps[:, 0:2, 0:T], 0.5, None, ALU.is_gt))
            for l in range(2):
                dve.wait_ge(taba, l + 1)
                setup.done(v.scalar_tensor_tensor(tab_a[:], tab_t[:], 1.0,
                                                  ps[:, 2, 0:4 * D].rearrange("p (e v) -> p e v", e=4), ALU.add, ALU.mult))
                setup.after()
                v.scalar_tensor_tensor(tab_z[:], ps[:, 3, 0:4 * D].rearrange("p (e v) -> p e v", e=4), 0.125,
                                       tab_a[:], ALU.mult, ALU.mult).then_inc(tabz, 1)
                dve.wait_ge(tabmm, 3 + 2 * l)
                dve.wait_ge(consts, 2 + l)
                v.tensor_tensor(tabT[:], tabT[:], ps[0:D, 4, 0:D], ALU.add).then_inc(consts, 1)
            dve.wait_ge(tabmm, 6)
            setup.done(v.tensor_copy(tabs[:, 0, :], ps[0:D, 5, 0:D]))
            setup.after()
            setup.done(v.reduce_sum(tab_s[:, 0:1], tabs[:, 0, :], AX.X))
            setup.after()
            setup.done(v.scalar_tensor_tensor(tab_q[:], tab_s[:, 0:1].to_broadcast([D, D]), -1.0 / D, tabs[:, 0, :],
                                              ALU.mult, ALU.add))
            setup.after()
            setup.done(v.tensor_tensor(tabs[:, 1, :], tab_q[:], tab_q[:], ALU.mult))
            setup.after()
            setup.done(v.reduce_sum(tab_s[:, 1:2], tabs[:, 1, :], AX.X))
            setup.after()
            v.tensor_scalar(tab_s[:, 2:3], tab_s[:, 1:2], 1.0 / D, EPS, ALU.mult, ALU.add).then_inc(tabv, 1)
            dve.wait_ge(tabpow, 1)
            v.tensor_scalar(tabs[:, 1, :], tab_q[:], tab_s[:, 3:4], None, ALU.mult).then_inc(consts, 1)
            dve.wait_ge(tabmm, 7)
            v.tensor_copy(xtabT[0:D, 0, :], ps[0:D, 6, 0:D])
            v.tensor_copy(xtabT[0:D, 1, :], ps[0:D, 6, 0:D]).then_inc(consts, 1)
            dve.wait_ge(tabmm, 8)
            v.tensor_copy(qtab[:].rearrange("p a b -> p (a b)"), ps[0:8, 2, :])
            v.tensor_copy(ktab[:].rearrange("p a b -> p (a b)"), ps[0:8, 3, :]).then_inc(consts, 1)
            for g in range(2):
                r = slice(g * D, g * D + D)
                setup.done(v.memset(vblk[r, :, g, 8:9], 1.0))
                setup.done(v.tensor_copy(vblk[r, :, g, 0:8],
                                         ps[r, 4, 0:D].rearrange("p (a g d) -> p a g d", a=4, g=2)[:, :, g, :]))
            dve.wait_ge(late, LATE)
            setup.done(v.tensor_copy(sel_b[:], w("sel8").rearrange("p (a b) -> p a b", a=4)))
            setup.done(v.tensor_scalar(w("L3_wqkv"), w("L3_wqkv"), ln1w[:, 0:1], None, ALU.mult))
            setup.done(v.tensor_scalar(w("L3_router"), w("L3_router"), ln2w[:, 0:1], None, ALU.mult))
            setup.done(v.tensor_scalar(w("L3_w13"), w("L3_w13"), ln2w[:, 0:1], None, ALU.mult))
            dve.wait_ge(tabmm, 9)
            setup.done(v.tensor_copy(score_tab[:].rearrange("p a b -> p (a b)"), ps[0:D, 5, :]))
            setup.after()
            dve.drain().then_inc(consts, 1)

            def bcast(ap, n):
                return ap.unsqueeze(2).to_broadcast([ap.shape[0], ap.shape[1], n])

            def bcast_mid(ap, n):
                return ap.unsqueeze(2).to_broadcast([ap.shape[0], ap.shape[1], n, ap.shape[2]])

            def bcast_heads(ap, n):
                return ap.unsqueeze(1).to_broadcast([ap.shape[0], n, ap.shape[1]])

            def tv(ap, t=2):
                return ap.rearrange("p (t f) -> p t f", t=t)

            with dve.Fori(0, PASSES) as i:
                steps = Steps(dve, vstep)
                done, after = steps.done, steps.after
                last = [0, 0]

                def centre(src):
                    for c in CH:
                        after(last[c])
                        last[c] = done(v.reduce_sum(st[c][:, 0, 0:2], src[c][:], AX.X))
                    for c in CH:
                        after(last[c])
                        last[c] = done(v.scalar_tensor_tensor(xc[c][:], bcast(st[c][:, 0, 0:2], D), -1.0 / D, src[c][:],
                                                              ALU.mult, ALU.add))
                    squares(xc)

                def squares(src):
                    for c in CH:
                        after(last[c])
                        last[c] = done(v.tensor_tensor(sq[c][:], src[c][:], src[c][:], ALU.mult))
                    for c in CH:
                        after(last[c])
                        last[c] = done(v.reduce_sum(st[c][:, 1, 0:2], sq[c][:], AX.X))

                def inverse_root(name, eps, width=2):
                    n = NORM[name]
                    for c in CH:
                        after(last[c])
                        v.tensor_scalar(st[c][:, 2, 0:width], st[c][:, 1, 0:width], 1.0 / D, eps, ALU.mult,
                                        ALU.add).then_inc(var_ready, 1)

                def rooted(name, c):
                    dve.wait_ge(rstd_ready, nth(NORM[name], c))

                def norm_rows(name, src, dst=None):
                    centre(src)
                    inverse_root(name, EPS)
                    for c in CH:
                        rooted(name, c)
                        if dst is None:
                            v.tensor_tensor(xn[c][:], xc[c][:], bcast(rstd[c][:, 0:2], D), ALU.mult).then_inc(rows_ready, 1)
                        else:
                            for g in range(2):
                                q = v.tensor_tensor(xd[c][:, :, g, :], xc[c][:], bcast(rstd[c][:, 0:2], D), ALU.mult)
                            q.then_inc(rows_ready, 1)

                def post_norm(name, proj, turn_name, g):
                    for c in CH:
                        dve.wait_ge(proj_ready, nth(proj, c))
                        last[c] = done(v.tensor_tensor(xn[c][:], xn[c][:], tv(bank(c, 2)[:, 0:P]), ALU.add))
                    centre(xn)
                    inverse_root(name, EPS)
                    for c in CH:
                        rooted(name, c)
                        last[c] = done(v.tensor_tensor(sq[c][:], xc[c][:], bcast(rstd[c][:, 0:2], D), ALU.mult))
                    for c in CH:
                        after(last[c])
                        last[c] = done(v.tensor_tensor(sq[c][:], sq[c][:], bcast_heads(vecs[:, g, :], 2), ALU.mult))
                    for c in CH:
                        after(last[c])
                        last[c] = done(v.tensor_tensor(sq[c][:], sq[c][:], bcast_heads(vecs[:, g + 1, :], 2), ALU.add))
                    for c in CH:
                        after(last[c])
                        last[c] = done(v.tensor_tensor(h[c][:], h[c][:], sq[c][:], ALU.add))

                def route(proj, E, k, at=0):
                    lo = D - E
                    for c in CH:
                        dve.wait_ge(proj_ready, nth(proj, c))
                        last[c] = done(v.tensor_copy(lg[c][:, :, lo:D], tv(bank(c, 2)[:, 0:2 * E])))
                    for c in CH:
                        after(last[c])
                        for t in TILES:
                            last[c] = done(v.max(top[c][:, t, :], lg[c][:, t, lo:D]))
                    for c in CH:
                        after(last[c])
                        last[c] = done(v.tensor_copy(pick[k][c][:, :, 0:k], top[c][:, :, 0:k]))
                    for c in CH:
                        after(last[c])
                        for t in TILES:
                            last[c] = done(v.match_replace(rep[c][:, t, lo:D + 8 - k], pick[k][c][:, t, :],
                                                           lg[c][:, t, lo:D + 8 - k], -BIG))
                    for c in CH:
                        after(last[c])
                        last[c] = done(v.tensor_scalar(sel[c][:, :, 0:E], rep[c][:, :, lo:D], -0.5 * BIG, None, ALU.is_lt))

                def shift(E):
                    for c in CH:
                        v.tensor_tensor(prob[c][:, :, 0:E], lg[c][:, :, D - E:D], bcast(top[c][:, :, 0], E),
                                        ALU.subtract).then_inc(shifted, 1)

                def attention(step, heads, full, exp_scale, out_):
                    for c in CH:
                        dve.wait_ge(at_scores, nth(step, c))
                        for t in TILES:
                            at = 0 if t == 0 else (T if full else P)
                            wd = T if full or t == 1 else P
                            last[c] = done(v.tensor_reduce(mx[c][:, 2 * t:2 * t + heads],
                                                           ps[:, 4 * c:4 * c + heads, at:at + wd], AX.X, ALU.max))
                        after(last[c])
                        m, n_ = tv(mx[c][:])[:, :, 0:heads], tv(nb[c][:])[:, :, 0:heads]
                        if isinstance(exp_scale, float):
                            v.tensor_scalar(n_, m, -exp_scale, None, ALU.mult).then_inc(at_bias, 1)
                        else:
                            v.scalar_tensor_tensor(n_, m, -1.0, exp_scale(c), ALU.mult, ALU.mult).then_inc(at_bias, 1)
                    for c in CH:
                        dve.wait_ge(at_av, nth(step, c))
                        r = tv(rr[c][:, 0:4])[:, :, 0:heads]
                        last[c] = done(v.reciprocal(r, tv(rs[c][:])[:, :, 0:heads]))
                        dv = D if step < STEP["L3f"] else 16
                        after(last[c])
                        o = bank(c, 3)[:, 256:256 + heads * 2 * dv].rearrange("p (e t d) -> p t e d", t=2, d=dv)
                        v.tensor_tensor(out_(c), o, r.unsqueeze(3).to_broadcast([P, 2, heads, dv]),
                                        ALU.mult).then_inc(at_out, 1)

                def add_to_h(step):
                    for c in CH:
                        dve.wait_ge(at_out, nth(step, c))
                        last[c] = done(v.tensor_tensor(h[c][:], h[c][:], xc[c][:], ALU.add))

                for c in CH:
                    v.tensor_scalar(hotT[c][:], ids_bc[:, bass.ds((i * 2 + c) * T, T)], w("iota_col")[0:D, :], None,
                                    ALU.is_equal).then_inc(hotT_ready, 1)
                    v.tensor_tensor(hot[c][:], bcast_heads(iota_b[:, 0:D], 2),
                                    bcast(ids_tok[:, bass.ds(i * 4 + 2 * c, 2)], D), ALU.is_equal).then_inc(hot_ready, 1)
                for c in CH:
                    dve.wait_ge(a0_scores, c + 1)
                    g = bank(c, 2)[:, 0:2 * P].rearrange("p (t a d) -> p t a d", t=2, a=2)
                    last[c] = done(v.tensor_copy(h[c][:], g[:, :, 0, :]))
                    done(v.tensor_copy(xn[c][:], g[:, :, 1, :]))
                    last[c] = done(v.tensor_scalar(pen[c][:], tv(bank(c, 3)[:, 0:P]), 0.5, NEG, ALU.is_lt, ALU.mult))
                if LAST_STAGE >= 2:
                    for c in CH:
                        after(last[c])
                        last[c] = done(v.tensor_tensor(sm[c][:], banks2(c, 0).rearrange("p t (h v) -> p t h v", h=8),
                                                       bcast_mid(pen[c][:], 8), ALU.add))
                    for c in CH:
                        after(last[c])
                        last[c] = done(v.reduce_max(st[c][:, 0, :], sm[c][:].rearrange("p t h v -> p (t h) v"), AX.X))
                    for c in CH:
                        after(last[c])
                        s3 = sm[c][:].rearrange("p t h v -> p (t h) v")
                        v.tensor_tensor(s3, s3, bcast(st[c][:, 0, :], D), ALU.subtract).then_inc(a0_max, 1)
                    for c in CH:
                        dve.wait_ge(a0_exp, c + 1)
                        v.tensor_tensor(sm[c][:], sm[c][:], bcast_mid(tv(bank(c, 3)[:, 0:P]), 8),
                                        ALU.mult).then_inc(a0_probs, 1)
                    for c in CH:
                        dve.wait_ge(a0_av, c + 1)
                        o = bank(c, 2)[:, 0:144].rearrange("p (a b) -> p a b", b=9)
                        last[c] = done(v.reciprocal(rr[c][:], o[:, :, 8]))
                        after(last[c])
                        for t in TILES:
                            q = v.tensor_tensor(att[c][:, t, 0:D].rearrange("p (h d) -> p h d", h=8),
                                                o[:, 8 * t:8 * t + 8, 0:8], bcast(rr[c][:, 8 * t:8 * t + 8], 8), ALU.mult)
                        q.then_inc(rows_ready, 1)
                    post_norm("L0_attn_post", 0, "L0_attn_out", 0)
                if LAST_STAGE >= 3:
                    norm_rows("L0_ffn_pre", h)
                    route(1, D, 6)
                    shift(D)
                    for c in CH:
                        dve.wait_ge(expd, c + 1)
                        last[c] = done(v.tensor_tensor(prob[c][:], prob[c][:], sel[c][:], ALU.mult))
                    for c in CH:
                        after(last[c])
                        last[c] = done(v.reduce_sum(st[c][:, 0, 0:2], prob[c][:], AX.X))
                    for c in CH:
                        after(last[c])
                        last[c] = done(v.reciprocal(rr[c][:, 0:2], st[c][:, 0, 0:2]))
                    for c in CH:
                        after(last[c])
                        last[c] = done(v.tensor_tensor(prob[c][:], prob[c][:], bcast(rr[c][:, 0:2], D), ALU.mult))
                    for c in CH:
                        after(last[c])
                    for x in range(16):
                        t, k8 = x // 8, x % 8
                        for c in CH:
                            if x >= 2:
                                dve.wait_ge(z_turned, nth(x - 2, c))
                            v.tensor_tensor(zb[x % 2][c][:], bcast_heads(xn[c][:, t, :], 8),
                                            bcast(prob[c][:, t, 8 * k8:8 * k8 + 8], D), ALU.mult).then_inc(z_ready, 1)
                    for c in CH:
                        dve.wait_ge(zsum_ready, nth(15, c))
                        v.tensor_copy(xc[c][:], tv(bank(c, 2)[:, 0:P])).then_inc(rows_ready, 1)
                    post_norm("L0_ffn_post", 2, "L0_ffn_out", 2)
                if LAST_STAGE >= 4:
                    norm_rows("L1_attn_pre", h)
                    for c in CH:
                        dve.wait_ge(proj_ready, nth(3, c))
                        kv = tv(bank(c, 2)[:, 0:256])
                        done(v.tensor_copy(vv[c][:], kv[:, :, D:P]))
                        done(v.tensor_tensor(kk[c][:, :, 0:D], kv[:, :, 0:D], cosq, ALU.mult))
                        done(v.tensor_tensor(kkm[c][:, :, 0:32], kv[:, :, 32:64], sinq[:, :, 0:32], ALU.mult))
                        last[c] = done(v.tensor_tensor(kkm[c][:, :, 32:64], kv[:, :, 0:32], sinq[:, :, 32:64], ALU.mult))
                    for c in CH:
                        after(last[c])
                        last[c] = done(v.tensor_tensor(kk[c][:, :, 0:D], kk[c][:, :, 0:D], kkm[c][:, :, 0:D], ALU.add))
                    for c in CH:
                        after(last[c])
                        last[c] = done(v.tensor_tensor(sq[c][:], kk[c][:, :, 0:D], kk[c][:, :, 0:D], ALU.mult))
                    for c in CH:
                        after(last[c])
                        last[c] = done(v.reduce_sum(st[c][:, 1, 0:2], sq[c][:], AX.X))
                    inverse_root("L1_k", 1.1920929e-07)
                    for c in CH:
                        rooted("L1_k", c)
                        last[c] = done(v.tensor_tensor(kk[c][:, :, 0:D], kk[c][:, :, 0:D], bcast(rstd[c][:, 0:2], D), ALU.mult))
                    for c in CH:
                        after(last[c])
                        for t in TILES:
                            q = v.tensor_tensor(kd[c][:, t], bcast_heads(kk[c][:, t, 0:D], 2),
                                                bcast_heads(qk_norm[:], 2), ALU.mult)
                        q.then_inc(qk_rows, 1)
                    for t in TILES:
                        for c in CH:
                            dve.wait_ge(q_proj, nth(t, c))
                            qp = banks2(c, 0).rearrange("p a (h f) -> p (a h) f", f=D)
                            qo = att[c][:, t, :].rearrange("p (h f) -> p h f", f=D)
                            qs = qb[c].rearrange("p (h f) -> p h f", f=D)
                            if t == 1:
                                after(last[c])
                            done(v.tensor_tensor(qo, qp, bcast_heads(cosq[:, t, :], 16), ALU.mult))
                            v.tensor_tensor(qs[:, :, 0:32], qp[:, :, 32:64], bcast_heads(sinq[:, t, 0:32], 16), ALU.mult)
                            v.tensor_tensor(qs[:, :, 32:64], qp[:, :, 0:32], bcast_heads(sinq[:, t, 32:64], 16),
                                            ALU.mult).then_inc(q_used, 1)
                            dve.wait_ge(q_used, nth(t, c))
                            v.tensor_tensor(qo, qo, qs, ALU.add).then_inc(q_roped, 1)
                        for c in CH:
                            dve.wait_ge(q_sq, nth(t, c))
                            last[c] = done(v.reduce_sum(st[c][:, 1, :], qa[c][:].rearrange("p (h f) -> p h f", f=D), AX.X))
                        inverse_root(f"L1_q{t}", 1.1920929e-07, 16)
                        for c in CH:
                            rooted(f"L1_q{t}", c)
                            last[c] = done(v.tensor_scalar(exs[c][:, t, :], rstd[c][:], 0.125, None, ALU.mult))
                    for c in CH:
                        after(last[c])
                    for s in range(8):
                        attention(STEP["L1"] + s, 2, False, lambda c: exs[c][:, :, 2 * s:2 * s + 2],
                                  lambda c: att[c][:, :, 2 * s * D:2 * (s + 1) * D].rearrange("p t (e d) -> p t e d", e=2))
                    for c in CH:
                        dve.wait_ge(ao_rows, nth(1, c))
                        last[c] = done(v.tensor_tensor(h[c][:], h[c][:], tv(bank(c, 2)[:, 0:P]), ALU.add))
                if LAST_STAGE >= 5:
                    norm_rows("L1_ffn_pre", h)
                    route(4, 32, 1)
                    for c in CH:
                        after(last[c])
                        dve.wait_ge(q_proj, nth(2, c))
                        for t in TILES:
                            v.scalar_tensor_tensor(z1[c][:, t, 0:512].rearrange("p (e f) -> p e f", f=16),
                                                   bank(c, t).rearrange("p (e f) -> p e f", f=16), 0.0,
                                                   bcast(sel[c][:, t, 0:32], 16), ALU.max, ALU.mult)
                        v.tensor_copy(z1[c][:, :, 512:544], sel[c][:, :, 0:32]).then_inc(f1_z, 1)
                    for c in CH:
                        dve.wait_ge(ao_rows, nth(2, c))
                        last[c] = done(v.scalar_tensor_tensor(h[c][:], tv(bank(c, 2)[:, 0:P]), 0.0, h[c][:], ALU.max, ALU.add))
                if LAST_STAGE >= 6:
                    norm_rows("L2_attn_pre", h)
                    for c in CH:
                        dve.wait_ge(q_proj, nth(3, c))
                        x = bank(c, 0)[:, 0:384].rearrange("p (t g f) -> p t g f", t=2, g=3)
                        kq = kk[c][:].rearrange("p t (g f) -> p t g f", g=2)
                        km = kkm[c][:].rearrange("p t (g f) -> p t g f", g=2)
                        done(v.tensor_copy(vv[c][:], x[:, :, 2, :]))
                        done(v.tensor_copy(kq[:, :, :, 0:48], x[:, :, 0:2, 0:48]))
                        done(v.tensor_tensor(kq[:, :, :, 48:64], x[:, :, 0:2, 48:64], bcast_mid(cos2, 2), ALU.mult))
                        done(v.tensor_tensor(km[:, :, :, 0:8], x[:, :, 0:2, 56:64], bcast_mid(sin2[:, :, 0:8], 2), ALU.mult))
                        last[c] = done(v.tensor_tensor(km[:, :, :, 8:16], x[:, :, 0:2, 48:56],
                                                       bcast_mid(sin2[:, :, 8:16], 2), ALU.mult))
                        after(last[c])
                        v.tensor_tensor(kq[:, :, :, 48:64], kq[:, :, :, 48:64], km[:, :, :, 0:16], ALU.add).then_inc(qk_rows, 1)
                    attention(STEP["L2"], 1, False, 0.125, lambda c: xc[c][:].unsqueeze(2))
                    add_to_h(STEP["L2"])
                if LAST_STAGE >= 7:
                    CAP = -(-5 * SEQS * T // 4) // 8
                    norm_rows("L2_ffn_pre", h, xd)
                    route(5, 8, 1)
                    shift(8)
                    for c in CH:
                        after(last[c])
                        v.tensor_copy(mb[c][:], sel[c][:, :, 0:8]).then_inc(f2_hot, 1)
                    for c in CH:
                        dve.wait_ge(expd, nth(1, c))
                        last[c] = done(v.reduce_sum(st[c][:, 0, 0:2], prob[c][:, :, 0:8], AX.X))
                        after(last[c])
                        last[c] = done(v.reciprocal(rr[c][:, 0:2], st[c][:, 0, 0:2]))
                    for c in CH:
                        dve.wait_ge(f2_count, c + 1)
                        last[c] = done(v.tensor_tensor(pen[c][:, :, 0:8], tv(bank(c, 2)[:, 32:48]),
                                                       bcast_heads(carry[:], 2), ALU.add))
                        after(last[c])
                        last[c] = done(v.tensor_tensor(carry[:], carry[:], bank(c, 2)[:, 48:56], ALU.add))
                        last[c] = done(v.tensor_tensor(pen[c][:, :, 0:8], pen[c][:, :, 0:8], sel[c][:, :, 0:8], ALU.mult))
                        after(last[c])
                        last[c] = done(v.reduce_sum(keep[c][:], pen[c][:, :, 0:8], AX.X))
                        after(last[c])
                        last[c] = done(v.scalar_tensor_tensor(gate[c][:], keep[c][:], float(CAP) + 0.5, rr[c][:, 0:2],
                                                              ALU.is_lt, ALU.mult))
                    for c in CH:
                        dve.wait_ge(f2_bc, c + 1)
                        x4 = pT[c][:].rearrange("p (a q) -> p a q", a=4)
                        v.tensor_tensor(x4, banks2(c, 0).rearrange("p a (b q) -> p (a b) q", q=T),
                                        bcast_heads(xT2[c][:], 4), ALU.mult).then_inc(f2_xm, 1)
                    for c in CH:
                        dve.wait_ge(f2_y, c + 1)
                        for t in TILES:
                            y3 = bank(c, t).rearrange("p (e d) -> p e d", e=8)
                            s3 = sm[c][:, t]
                            last[c] = done(v.tensor_tensor(s3, y3, bcast(sel[c][:, t, 0:8], D), ALU.mult))
                    for c in CH:
                        after(last[c])
                        for t in TILES:
                            last[c] = done(v.reduce_sum(xc[c][:, t, :], sm[c][:, t].rearrange("p e d -> p d e"), AX.X))
                    for c in CH:
                        after(last[c])
                        last[c] = done(v.tensor_tensor(xc[c][:], xc[c][:], bcast(gate[c][:], D), ALU.mult))
                    for c in CH:
                        after(last[c])
                        done(v.memset(fill[c][:], 0.0))
                        last[c] = done(v.tensor_tensor(bad[c][:], xc[c][:], xc[c][:], ALU.is_equal))
                    for c in CH:
                        after(last[c])
                        last[c] = done(v.copy_predicated(fill[c][:], bad[c][:], xc[c][:]))
                    for value, op, lim in ((1e4, ALU.is_gt, 3.4e38), (-1e4, ALU.is_lt, -3.4e38)):
                        for c in CH:
                            after(last[c])
                            done(v.memset(sq[c][:], value))
                            last[c] = done(v.tensor_scalar(bad[c][:], xc[c][:], lim, None, op))
                        for c in CH:
                            after(last[c])
                            last[c] = done(v.copy_predicated(fill[c][:], bad[c][:], sq[c][:]))
                    for c in CH:
                        after(last[c])
                        last[c] = done(v.tensor_tensor(h[c][:], h[c][:], fill[c][:], ALU.add))
                if LAST_STAGE >= 8:
                    norm_rows("L3_attn_pre", h)
                    attention(STEP["L3"], 1, True, 0.125, lambda c: xc[c][:].unsqueeze(2))
                    add_to_h(STEP["L3"])
                if LAST_STAGE >= 9:
                    centre(h)
                    inverse_root("L3_ffn_pre", EPS)
                    for c in CH:
                        rooted("L3_ffn_pre", c)
                        last[c] = done(v.tensor_tensor(x3[c][:], xc[c][:], bcast(rstd[c][:, 0:2], D), ALU.mult))
                    squares(x3)
                    inverse_root("L3_rms1", 1e-6)
                    for c in CH:
                        rooted("L3_rms1", c)
                        v.tensor_tensor(xc[c][:], x3[c][:], bcast(rstd[c][:, 0:2], D), ALU.mult).then_inc(rows_ready, 1)
                    for c in CH:
                        dve.wait_ge(proj_ready, nth(6, c))
                        x = tv(bank(c, 2)[:, 0:256])
                        q6 = x[:, :, 0:96].rearrange("p t (h f) -> p t h f", f=16)
                        k6 = kk[c][:, :, 0:96].rearrange("p t (h f) -> p t h f", f=16)
                        m6 = kkm[c][:, :, 0:96].rearrange("p t (h f) -> p t h f", f=16)
                        done(v.tensor_copy(kk[c][:, :, 96:128], x[:, :, 96:128]))
                        done(v.tensor_tensor(k6, q6, bcast_mid(cos3, 6), ALU.mult))
                        done(v.tensor_tensor(m6[:, :, :, 0:8], q6[:, :, :, 8:16], bcast_mid(sin3[:, :, 0:8], 6), ALU.mult))
                        last[c] = done(v.tensor_tensor(m6[:, :, :, 8:16], q6[:, :, :, 0:8], bcast_mid(sin3[:, :, 8:16], 6), ALU.mult))
                        after(last[c])
                        pad = kd4[c][:].rearrange("p g t (h f) -> p g t h f", f=32)
                        v.tensor_tensor(pad[:, 0, :, :, 0:16], k6[:, :, 0:4, :], m6[:, :, 0:4, :], ALU.add)
                        for r in range(2):
                            q = v.tensor_tensor(pad[:, 1, :, r:4:2, 0:16], k6[:, :, 4:6, :], m6[:, :, 4:6, :], ALU.add)
                        q.then_inc(qk_rows, 1)
                    for s in range(2):
                        attention(STEP["L3f"] + s, 2, False, 0.25,
                                  lambda c: att[c][:, :, 32 * s:32 * s + 32].rearrange("p t (e d) -> p t e d", e=2))
                    for c in CH:
                        dve.wait_ge(at_out, nth(STEP["L3f"] + 1, c))
                        dve.drain().then_inc(rows_ready, 1)
                    for c in CH:
                        dve.wait_ge(proj_ready, nth(7, c))
                        last[c] = done(v.tensor_tensor(x3[c][:], x3[c][:], tv(bank(c, 2)[:, 0:P]), ALU.add))
                    squares(x3)
                    inverse_root("L3_rms2", 1e-6)
                    for c in CH:
                        rooted("L3_rms2", c)
                        v.tensor_tensor(xc[c][:], x3[c][:], bcast(rstd[c][:, 0:2], D), ALU.mult).then_inc(rows_ready, 1)
                    route(8, 8, 2)
                    shift(8)
                    for c in CH:
                        dve.wait_ge(expd, nth(2, c))
                        last[c] = done(v.reduce_sum(st[c][:, 0, 0:2], prob[c][:, :, 0:8], AX.X))
                        after(last[c])
                        last[c] = done(v.reciprocal(rr[c][:, 0:2], st[c][:, 0, 0:2]))
                        last[c] = done(v.tensor_tensor(prob[c][:, :, 0:8], prob[c][:, :, 0:8], sel[c][:, :, 0:8], ALU.mult))
                        after(last[c])
                        last[c] = done(v.tensor_tensor(prob[c][:, :, 0:8], prob[c][:, :, 0:8], bcast(rr[c][:, 0:2], 8), ALU.mult))
                        after(last[c])
                        last[c] = done(v.reduce_sum(st[c][:, 0, 0:2], prob[c][:, :, 0:8], AX.X))
                        after(last[c])
                        last[c] = done(v.tensor_scalar(st[c][:, 1, 0:2], st[c][:, 0, 0:2], 2.0, 2e-9, ALU.mult, ALU.add))
                        after(last[c])
                        last[c] = done(v.reciprocal(rr[c][:, 2:4], st[c][:, 1, 0:2]))
                        after(last[c])
                        last[c] = done(v.tensor_tensor(prob[c][:, :, 0:8], prob[c][:, :, 0:8], bcast(rr[c][:, 2:4], 8), ALU.mult))
                        done(v.tensor_tensor(h[c][:], h[c][:], x3[c][:], ALU.add))
                    for c in CH:
                        after(last[c])
                    for t in TILES:
                        for e2 in range(4):
                            x = t * 4 + e2
                            for c in CH:
                                dve.wait_ge(f4_tanh, nth(x, c))
                                g = banks2(c, 0)[:, :, 0:HIDDEN3]
                                last[c] = done(v.scalar_tensor_tensor(th[c][:], th[c][:], 1.0, g, ALU.add, ALU.mult))
                            for c in CH:
                                after(last[c])
                                for u in range(2):
                                    e = 2 * e2 + u
                                    q = v.scalar_tensor_tensor(hid[c][:, e, :], bank(c, u)[:, HIDDEN3:2 * HIDDEN3],
                                                               prob[c][:, t, e:e + 1], th[c][:, u, :], ALU.mult, ALU.mult)
                                q.then_inc(f4_h, 1)
                    for c in CH:
                        dve.wait_ge(ao_rows, nth(4, c))
                        last[c] = done(v.tensor_tensor(h[c][:], h[c][:], tv(bank(c, 2)[:, 0:P]), ALU.add))
                for c in CH:
                    after(last[c])
                    v.tensor_copy(h_all[:, bass.ds(i * 4 + 2 * c, 2), :], h[c][:])
                close_pass(dve, i)


def layout(x):
    f = np.float32

    def rows(a, b):
        return np.concatenate([a, b.reshape(1, -1)], 0)

    half_split = np.concatenate([np.arange(0, 64, 2), np.arange(1, 64, 2)])
    rope16 = np.concatenate([np.arange(0, 16, 2), np.arange(1, 16, 2)])
    i, j = np.arange(P)[:, None], np.arange(P)[None, :]

    def rope(freqs, signed):
        ang = (np.arange(T, dtype=f)[:, None] * freqs[None, :].astype(f)).astype(f)
        s, c = np.sin(ang).astype(f), np.cos(ang).astype(f)
        both = lambda a, b: np.concatenate([a, b], 1).reshape(2, P, -1).transpose(1, 0, 2).reshape(P, -1)
        return both(c, c), both(-s, s)

    cos1, sin1 = rope(np.power(f(10000.0), (-2.0 * np.arange(32, dtype=f) / 64).astype(f)), True)
    cos2, sin2 = rope((f(1.0) / np.power(f(10000.0), np.arange(8, dtype=f) / f(8))).astype(f), True)
    cos3, sin3 = rope((1.0 / 10000.0 ** (np.arange(0, 16, 2, dtype=f) / 16)).astype(f), True)
    sel8 = np.zeros((8, 4, P), f)
    for p in range(4):
        sel8[2 * p, p, 0:64] = 1
        sel8[2 * p + 1, p, 64:128] = 1
    wq = x["L1_attn_wq"].reshape(16, 64, 64)[:, half_split].reshape(1024, 64)
    wk, wv = x["L1_attn_wkv"][0:64][half_split], x["L1_attn_wkv"][64:128]
    w2 = x["L3_ffn_w2"].transpose(0, 2, 1).reshape(8 * HIDDEN3, D)
    pieces = {
        "ident": ("early128", np.eye(P, dtype=f)),
        "causal": ("early128", np.where(j <= i, 0, NEG).astype(f)),
        "window": ("early128", np.where(j >= i, 0, NEG).astype(f)),
        "tri": ("early128", (i <= j).astype(f)),
        "cos_l1": ("early128", cos1), "sin_l1": ("early128", sin1),
        "cos_l2": ("early128", cos2), "sin_l2": ("early128", sin2),
        "cos_l3": ("early128", cos3), "sin_l3": ("early128", sin3),
        "iota_col": ("early128", np.arange(P, dtype=f).reshape(P, 1)),
        "WdT": ("early128", x["L0_tok_Wd"].transpose(3, 0, 1, 2).reshape(P, -1)),
        "WgT": ("early64", x["L0_tok_Wg"].transpose(3, 0, 1, 2).reshape(D, -1)),
        "WuT": ("early64", x["L0_tok_Wu"].transpose(3, 0, 1, 2).reshape(D, -1)),
        "embT": ("early64", x["L0_tok_embed"].T),
        "lmT": ("early64", x["L0_tok_lm_head"].T),
        "L0_Wq": ("early65", rows(x["L0_attn_Wq"], x["L0_attn_bq"])),
        "L0_Wk": ("early65", rows(x["L0_attn_Wk"], x["L0_attn_bk"])),
        "L0_Wv": ("early65", rows(x["L0_attn_Wv"], x["L0_attn_bv"])),
        "L0_Wo": ("early65", rows(x["L0_attn_Wo"], x["L0_attn_bo"])),
        "L0_out": ("early65", rows(x["L0_ffn_out_w"].T, x["L0_ffn_out_b"])),
        "sel8": ("late8", sel8.reshape(8, -1)),
        "L0_gate": ("late64", x["L0_ffn_gate_w"].T),
        "L1_wq": ("late64", wq.T),
        "L1_wkv": ("late64", np.concatenate([wk, wv], 0).T),
        "L2_Wqcomp": ("late64", x["L2_attn_Wq_comp"]), "L2_Wkvcomp": ("late64", x["L2_attn_Wkv_comp"]),
        "L2_Wq": ("late64", np.concatenate([x["L2_attn_Wqc"], x["L2_attn_Wqr"][:, rope16]], 1)),
        "L2_Wkv": ("late64", np.concatenate([x["L2_attn_Wkc"], x["L2_attn_Wkr"][:, rope16], x["L2_attn_Wv"]], 1)),
        "L2_gate": ("late64", x["L2_ffn_gate_w"]),
        "ln1": ("late64", x["L3_ffn_ln1_w"].reshape(D, 1)), "ln2": ("late64", x["L3_ffn_ln2_w"].reshape(D, 1)),
        "L3_wqkv": ("late64", np.concatenate([x["L3_ffn_wq"], x["L3_ffn_wk"], x["L3_ffn_wv"]], 0).T),
        "L3_wo": ("late64", x["L3_ffn_wo"].T),
        "L3_router": ("late64", x["L3_ffn_router_w"].T),
        "L3_w13": ("late64", np.concatenate([x["L3_ffn_w1"], x["L3_ffn_w3"]], 1).transpose(2, 0, 1).reshape(D, -1)),
        "L1_router": ("late65", rows(x["L1_ffn_router_w"].T, x["L1_ffn_router_b"])),
        "L1_W1": ("late65", rows(x["L1_ffn_W1"].transpose(1, 0, 2).reshape(D, 512), x["L1_ffn_b1"])),
        "L3_Wq": ("late65", rows(x["L3_attn_Wq"], x["L3_attn_bq"])),
        "L3_Wk": ("late65", rows(x["L3_attn_Wk"], x["L3_attn_bk"])),
        "L3_Wv": ("late65", rows(x["L3_attn_Wv"], x["L3_attn_bv"])),
        "L1_b2": ("late32", x["L1_ffn_b2"]),
        "L2_b1": ("late8", x["L2_ffn_b1"]),
        "L2_gateb": ("late1", x["L2_ffn_gate_b"].reshape(1, 8)),
        "L2_b2": ("late1", x["L2_ffn_b2"].reshape(1, 512)),
        "lattice": ("late128", x["L0_ffn_lattice_weights"].reshape(32, P, D).transpose(1, 0, 2).reshape(P, -1)),
        "L1_wo": ("late128", x["L1_attn_wo"].T.reshape(8, P, D).transpose(1, 0, 2).reshape(P, -1)),
        "L1_W2": ("late128", x["L1_ffn_W2"].reshape(4, P, D).transpose(1, 0, 2).reshape(P, -1)),
        "L2_W1": ("late128", x["L2_ffn_w1"].reshape(4, P, 256).transpose(1, 0, 2).reshape(P, -1)),
        "L2_W2": ("late128", x["L2_ffn_w2"].reshape(8, 2, P, D).transpose(2, 1, 0, 3).reshape(P, -1)),
        "L3_w2": ("late128", w2[0:1280].reshape(10, P, D).transpose(1, 0, 2).reshape(P, -1)),
        "L3_w2t": ("late80", w2[1280:]),
    }
    packs, place = {}, {}
    for name, (pack, a) in pieces.items():
        at = sum(b.shape[1] for b in packs.get(pack, []))
        place[name] = (pack, at, a.shape[1], a.shape[0])
        packs.setdefault(pack, []).append(a)
    arrays = {k: np.ascontiguousarray(np.concatenate(b, 1)) for k, b in packs.items()}
    return arrays, place


def kernel(**inputs):
    import numpy as _np
    import concourse.bacc as _bacc
    from concourse import mybir as _mybir
    from concourse.bass_utils import run_bass_kernel_spmd as _run

    x = {k: _np.ascontiguousarray(a) for k, a in inputs.items()}
    arrays, place = layout(x)
    cols = {"packs": {k: a.shape for k, a in arrays.items()}, "pieces": place}
    ids = x["x"].reshape(-1)
    arrays["ids"] = ids
    arrays["ids_tok"] = _np.ascontiguousarray(ids.reshape(2 * SEQS, P).T)
    arrays["edges"] = _np.ascontiguousarray(x["L0_attn_edge_index"].reshape(2, P, P).transpose(1, 0, 2))
    arrays["vecs"] = _np.stack([x["L0_attn_gamma"], x["L0_attn_beta"], x["L0_ffn_ln_g"], x["L0_ffn_ln_b"],
                                _np.concatenate([x["L1_attn_q_norm_w"][0::2], x["L1_attn_q_norm_w"][1::2]]),
                                _np.concatenate([x["L1_attn_k_norm_w"][0::2], x["L1_attn_k_norm_w"][1::2]])])
    nc = _bacc.Bacc("TRN2", target_bir_lowering=False, num_devices=1)
    dram = {k: nc.dram_tensor("in_" + k, a.shape, _mybir.dt.from_np(a.dtype), kind="ExternalInput").ap()
            for k, a in arrays.items()}
    out = nc.dram_tensor("tower_out", (SEQS * T, D), F32, kind="ExternalOutput").ap()
    build(nc, dram, out, cols)
    r = _run(nc, [{"in_" + k: a for k, a in arrays.items()}], core_ids=[0])
    return r.results[0]["tower_out"].reshape(SEQS, T, D)
```

```python
from contextlib import ExitStack

import numpy as np

import concourse.bass as bass
from concourse import mybir

F32 = mybir.dt.float32
BF16 = mybir.dt.bfloat16
I32 = mybir.dt.int32
ALU = mybir.AluOpType
ACT = mybir.ActivationFunctionType
AX = mybir.AxisListType

LAST_STAGE = 9
P = 128
D = 64
SEQS, T = 8, 256
CH = (0, 1)
TILES = (0, 1)
PASSES = SEQS // 2
NEG = -1e30
BIG = 3e38
EPS = 1e-5
HIDDEN3 = 170

TURN = {n: i for i, n in enumerate([
    "L0_attn_out", "L0_ffn_in", "L0_ffn_out", "L1_attn_in", "L1_ffn_in", "L2_attn_in", "L2_ffn_in",
    "L3_attn_in", "L3_qkv_in", "L3_attn_out", "L3_moe_in"])}
NORM = {n: i for i, n in enumerate([
    "L0_attn_post", "L0_ffn_pre", "L0_ffn_post", "L1_attn_pre", "L1_k", "L1_ffn_pre",
    "L2_attn_pre", "L2_ffn_pre", "L3_attn_pre", "L3_ffn_pre", "L3_rms1", "L3_rms2"])}
PADDED = ("late64", "late65")
MOE_BANK = (0, 1, 3)
STEP = {"L1": 0, "L2": 8, "L3": 9, "L3f": 10}


def build(nc, dram, out, cols):
    with ExitStack() as ctx:
        def sb(name, shape, dt=F32):
            return ctx.enter_context(nc.sbuf_tensor(name, shape, dt))

        def sb2(name, shape, dt=F32):
            return [sb(f"{name}{c}", shape, dt) for c in CH]

        def sem(name):
            return ctx.enter_context(nc.semaphore(name))

        packs, padded = {}, {}
        for name, (arr, width) in cols["packs"].items():
            whole = sb("pack_" + name, [P if name in PADDED + ("early64",) else arr, width])
            packs[name] = whole[0:arr, :]
            padded[name] = whole
            if name == "early64":
                h_all = whole[:, 0:2 * SEQS * D].rearrange("p (t d) -> p t d", d=D)

        def w(name, rows=None):
            pack, at, width, r = cols["pieces"][name]
            return packs[pack][0:(rows or r), at:at + width]

        def wide(name):
            pack, at, width, r = cols["pieces"][name]
            return padded[pack][:, at:at + width]

        ident = w("ident")
        cosq = w("cos_l1").rearrange("p (t f) -> p t f", t=2)
        sinq = w("sin_l1").rearrange("p (t f) -> p t f", t=2)
        cos2 = w("cos_l2").rearrange("p (t f) -> p t f", t=2)
        sin2 = w("sin_l2").rearrange("p (t f) -> p t f", t=2)
        cos3 = w("cos_l3").rearrange("p (t f) -> p t f", t=2)
        sin3 = w("sin_l3").rearrange("p (t f) -> p t f", t=2)
        vecs = sb("vecs", [P, 6, D])
        qk_norm = sb("qk_norm", [P, D])
        ident_b = sb("ident_b", [P, P], BF16)
        maskb = sb("maskb", [P, 3, P], BF16)
        tri_b = sb("tri_b", [P, P], BF16)
        ones_b = sb("ones_b", [P, P], BF16)
        sel_b = sb("sel_b", [8, 4, P], BF16)
        ones1 = sb("ones1", [1, P])
        half = sb("half", [P, 1])
        ids_bc = sb("ids_bc", [D, SEQS * T])
        ids_tok_i = sb("ids_tok_i", [P, 2 * SEQS], I32)
        ids_tok = sb("ids_tok", [P, 2 * SEQS])
        edges = sb("edges", [P, 2, P])
        iota_b = sb("iota_b", [P, T], BF16)
        diag_b = sb("diag_b", [P, 2, T], BF16)
        allow = sb("allow", [P, 2, T], BF16)

        tabT = sb("tabT", [D, D])
        tab_t = sb("tab_t", [P, 4, D])
        tab_a = sb("tab_a", [P, 4, D])
        tab_z = sb("tab_z", [P, 4, D])
        tabs = sb("tabs", [D, 2, D])
        tab_s = sb("tab_s", [D, 4])
        tab_q = sb("tab_q", [D, D])
        xtabT = sb("xtabT", [D + 1, 2, D])
        qtab = sb("qtab", [8, 8, D])
        ktab = sb("ktab", [8, 8, D])
        score_tab = sb("score_tab", [P, 8, D])
        vblk = sb("vblk", [P, 4, 2, 9])
        ln1w = w("ln1")
        ln2w = w("ln2")

        h = sb2("h", [P, 2, D])
        xn = sb2("xn", [P, 2, D])
        xd = sb2("xd", [P, 2, 2, D])
        xc = sb2("xc", [P, 2, D])
        sq = sb2("sq", [P, 2, D])
        st = sb2("st", [P, 3, 16])
        qsum = sb2("qsum", [P, 2, 16])
        rstd = sb2("rstd", [P, 16])
        xT = sb2("xT", [P, T])
        xT2 = sb2("xT2", [P, T])
        hotT = sb2("hotT", [P, T])
        hot = sb2("hot", [P, 2, D], BF16)
        pen = sb2("pen", [P, 2, D])
        sm = sb2("sm", [P, 2, 8, D])
        pT = sb2("pT", [P, 1024])
        lg = sb2("lg", [P, 2, 72])
        top = sb2("top", [P, 2, 8])
        pick = {k: sb2(f"pick{k}_", [P, 2, 8]) for k in (1, 2, 6)}
        rep = sb2("rep", [P, 2, 72])
        sel = sb2("sel", [P, 2, D])
        prob = sb2("prob", [P, 2, D])
        zb = [sb2(f"zb{j}", [P, 8, D]) for j in range(2)]
        zT = [sb2(f"zT{j}", [P, 512]) for j in range(2)]
        att = sb2("att", [P, 2, 1024])
        qT = sb2("qT", [P, 8, T])
        kk = sb2("kk", [P, 2, P])
        kkm = sb2("kkm", [P, 2, P])
        vv = sb2("vv", [P, 2, D])
        kd = sb2("kd", [P, 2, 2, D])
        kT = sb2("kT", [P, 2, T])
        exs = sb2("exs", [P, 2, 16])
        mx = sb2("mx", [P, 4])
        nb = sb2("nb", [P, 4])
        rs = sb2("rs", [P, 2, 4])
        rr = sb2("rr", [P, 16])
        pr = sb2("pr", [P, 768])
        prT = sb2("prT", [P, 768])
        mT = sb2("mT", [32, T])
        mTb = sb2("mTb", [8, T], BF16)
        mb = sb2("mb", [P, 2, 8], BF16)
        carry = sb("carry", [P, 8])
        gate = sb2("gate", [P, 2])
        keep = sb2("keep", [P, 2])
        fill = sb2("fill", [P, 2, D])
        bad = sb2("bad", [P, 2, D], I32)
        kd4 = sb2("kd4", [P, 2, 2, P])
        x3 = sb2("x3", [P, 2, D])

        ids_bc_i = att[0][0:D].rearrange("p a b -> p (a b)").bitcast(I32)
        edges_i = att[1][:, 0, 0:2 * P].bitcast(I32).rearrange("p (a b) -> p a b", a=2)
        hot_src, hot_dst = [qT[c][:].rearrange("p a b -> p (a b)").bitcast(BF16)
                            .rearrange("p (s u n) -> p s u n", s=2, u=8) for c in CH]
        qa = pT
        qb = [sm[c][:].rearrange("p t h v -> p (t h v)")[:, 0:1024] for c in CH]
        z1 = [att[c][:, :, 0:544] for c in CH]
        th = [sm[c][:].rearrange("p t h v -> p (t h v)")[:, 0:3 * HIDDEN3].rearrange("p (b f) -> p b f", b=3) for c in CH]
        hid = [[b[c][:].rearrange("p a b -> p (a b)")[:, 0:8 * HIDDEN3] for c in CH] for b in (att, qT)]

        ps = ctx.enter_context(nc.psum_tensor("ps", [P, 8, 512], F32))

        def bank(c, j):
            return ps[:, 4 * c + j, :]

        def banks2(c, j):
            return ps[:, 4 * c + j:4 * c + j + 2, :]

        early = sem("early_loaded")
        late = sem("late_loaded")
        vset = sem("vector_setup_step")
        padding = sem("padding_zeroed")
        iset = sem("iota_ready")
        edge_hot = sem("edge_hot_ready")
        edge_used = sem("edge_hot_used")
        tabmm = sem("table_product_ready")
        taba = sem("table_tanh_ready")
        tabv = sem("table_vector_ready")
        tabz = sem("table_hidden_ready")
        tabpow = sem("table_rstd_ready")
        consts = sem("constants_ready")
        ended = sem("pass_ended")
        opened = sem("pass_opened")
        stored = sem("stored")
        vstep = sem("vector_step")
        astep = sem("scalar_step")
        hotT_ready = sem("hotT_ready")
        hot_ready = sem("hot_ready")
        var_ready = sem("variance_ready")
        rstd_ready = sem("rstd_ready")
        rows_ready = sem("rows_ready")
        turned = sem("rows_turned")
        feat_ready = sem("features_ready")
        proj_ready = sem("projection_ready")
        a0_scores, a0_max, a0_exp, a0_probs, a0_probsT_ps, a0_probsT, a0_av = [
            sem("a0_" + n) for n in ("scores", "max", "exp", "probs", "probsT_ps", "probsT", "av")]
        shifted = sem("logits_shifted")
        expd = sem("logits_exp")
        z_ready, z_turned, zT_ready, zsum_ready = [sem("lattice_" + n) for n in ("z", "turned", "zT", "sum")]
        at_scores, at_bias, at_probs, at_turned, at_probsT, at_av, at_out = [
            sem("at_" + n) for n in ("scores", "bias", "probs", "turned", "probsT", "av", "out")]
        q_proj, q_used, q_sq, q_var, scales_ready, q_roped, q_turned, qT_ready, k_turned, kT_ready = [
            sem("l1_" + n) for n in ("q_proj", "q_used", "sq", "var", "scales", "roped", "turned", "qT", "k_turned", "kT")]
        ao_turned, ao_ready, ao_rows = [sem("l1_out_" + n) for n in ("turned", "ready", "rows")]
        f1_z, f1_turned, f1_zT = [sem("f1_" + n) for n in ("z", "turned", "zT")]
        c2_ready, c2_used = sem("l2_c_ready"), sem("l2_c_used")
        qk_rows, qk_turned, qk_ready = [sem("qk_" + n) for n in ("rows", "turned", "ready")]
        f2_count, f2_maskT, f2_mask, f2_bc, f2_xm, f2_hid, f2_relu, f2_y = [
            sem("f2_" + n) for n in ("count", "maskT_ps", "maskT", "bc", "xm", "hid", "relu", "y")]
        f2_hot = sem("f2_hot")
        f4_gu, f4_tanh, f4_h, f4_turned, f4_hT = [sem("f4_" + n) for n in ("gu", "tanh", "h", "turned", "hT")]
        loop_sems = [vstep, astep, hotT_ready, hot_ready, var_ready, rstd_ready, rows_ready, turned, feat_ready,
                     proj_ready, a0_scores, a0_max, a0_exp, a0_probs, a0_probsT_ps, a0_probsT, a0_av, shifted, expd,
                     z_ready, z_turned, zT_ready, zsum_ready, at_scores, at_bias, at_probs, at_turned, at_probsT,
                     at_av, at_out, q_proj, q_used, q_sq, q_var, scales_ready, q_roped, q_turned, qT_ready, k_turned, kT_ready,
                     ao_turned, ao_ready, ao_rows, f1_z, f1_turned, f1_zT, c2_ready, c2_used, qk_rows, qk_turned,
                     qk_ready, f2_count, f2_maskT, f2_mask, f2_bc, f2_xm, f2_hid, f2_relu, f2_y, f2_hot, f4_gu,
                     f4_tanh, f4_h, f4_turned, f4_hT, ended]

        class Steps:
            def __init__(self, eng, s):
                self.eng, self.s, self.n = eng, s, 0

            def done(self, ins):
                ins.then_inc(self.s, 1)
                self.n += 1
                return self.n

            def after(self, n=None):
                self.eng.wait_ge(self.s, n or self.n)

        def nth(n, c):
            return 2 * n + c + 1

        def close_pass(eng, i):
            eng.drain().then_inc(ended, 1)
            eng.wait_ge(opened, i + 1)

        def blocks(full):
            return [(0, 0), (0, 1), (1, 0), (1, 1)] if full else [(0, 0), (1, 0), (1, 1)]

        block = ctx.enter_context(nc.Block())

        @block.sync
        def _(sp):
            sp.dma_start(edges_i, dram["edges"]).then_inc(early, 16)
            sp.dma_start(ids_bc_i, dram["ids"].rearrange("(a n) -> a n", a=1).to_broadcast([D, SEQS * T])
                         ).then_inc(early, 16)
            sp.dma_start(ids_tok_i[:], dram["ids_tok"]).then_inc(early, 16)
            sp.dma_start(vecs[:], dram["vecs"].rearrange("(a v) d -> a v d", a=1).to_broadcast([P, 6, D])
                         ).then_inc(early, 16)
            for name in ("early128", "early64", "early65"):
                sp.dma_start(packs[name], dram[name]).then_inc(early, 16)
            sp.wait_ge(padding, len(PADDED))
            for name in cols["packs"]:
                if not name.startswith("early"):
                    sp.dma_start(packs[name], dram[name]).then_inc(late, 16)
            sp.wait_ge(opened, PASSES)
            sp.dma_start(out.rearrange("(t p) d -> p t d", p=P), h_all).then_inc(stored, 16)
            sp.wait_ge(stored, 16)

        EARLY = 16 * 7
        LATE = 16 * sum(not n.startswith("early") for n in cols["packs"])

        @block.gpsimd
        def _(pool):
            for n, name in enumerate(PADDED):
                nc.gpsimd.memset(padded[name][D:P, :], 0.0).then_inc(padding, 1)
                pool.wait_ge(padding, n + 1)
            nc.gpsimd.iota(iota_b[:], [[1, T]], base=0, channel_multiplier=0,
                           allow_small_or_imprecise_dtypes=True).then_inc(iset, 1)
            nc.gpsimd.memset(half[:], -0.5).then_inc(iset, 1)
            nc.gpsimd.memset(carry[:], 0.0).then_inc(iset, 1)
            nc.gpsimd.memset(ones1[:], 1.0).then_inc(iset, 1)
            pool.wait_ge(iset, 4)
            pool.wait_ge(tabv, 1)
            nc.gpsimd.tensor_tensor(tab_s[:, 3:4], tab_s[:, 2:3], half[0:D, :], ALU.pow).then_inc(tabpow, 1)
            with pool.Fori(0, PASSES) as i:
                def rsqrt(n, width):
                    for c in CH:
                        pool.wait_ge(var_ready, nth(n, c))
                        nc.gpsimd.tensor_tensor(rstd[c][:, 0:width], st[c][:, 2, 0:width],
                                                half[:, 0:1].to_broadcast([P, width]),
                                                ALU.pow).then_inc(rstd_ready, 1)

                def q_scales(t, lo, hi):
                    for c in CH:
                        pool.wait_ge(q_var, nth(t, c))
                        nc.gpsimd.tensor_tensor(exs[c][:, t, lo:hi], qsum[c][:, t, lo:hi],
                                                half[:, 0:1].to_broadcast([P, hi - lo]), ALU.pow).then_inc(scales_ready, 1)

                stages = [["L0_attn_post"], ["L0_ffn_pre", "L0_ffn_post"],
                          ["L1_attn_pre", "L1_k"], ["L1_ffn_pre"], ["L2_attn_pre"], ["L2_ffn_pre"],
                          ["L3_attn_pre"], ["L3_ffn_pre", "L3_rms1", "L3_rms2"]]
                for names in stages[0:LAST_STAGE - 1]:
                    for n in names:
                        rsqrt(NORM[n], 2)
                        if n == "L1_k":
                            q_scales(0, 0, 16)
                            q_scales(1, 0, 4)
                            q_scales(1, 4, 16)
                pool.wait_ge(ended, 3)
                for s in loop_sems:
                    pool.sem_clear(s)
                pool.nop().then_inc(opened, 1)

        @block.tensor
        def _(pe):
            def mm(o, l, r, start=True, stop=True, **k):
                return nc.tensor.matmul(o, l, r, start=start, stop=stop, **k)

            def turn(o, i):
                k = i.shape[0]
                return nc.tensor.transpose(o, i, ident[0:k, 0:k])

            pe.wait_ge(consts, 1)
            for j in TILES:
                mm(ps[:, j, 0:T], ident_b[:], diag_b[:, j, :], start=True, stop=False).then_inc(edge_used, 1)
            with pe.Fori(0, 8) as i:
                for half_ in range(2):
                    pe.wait_ge(edge_hot, i * 2 + half_ + 1)
                    for u in range(8):
                        for j in TILES:
                            last = mm(ps[:, j, 0:T], hot_dst[:, half_, u, j * P:(j + 1) * P], hot_src[:, half_, u, :],
                                      start=False, stop=False)
                    last.then_inc(edge_used, 1)
            for j in TILES:
                last = mm(ps[:, j, 0:T], ident_b[:], diag_b[:, j, :], start=False, stop=True)
            last.then_inc(tabmm, 1)

            WgT = w("WgT").rearrange("p (l e f) -> p l e f", l=2, e=4)
            WuT = w("WuT").rearrange("p (l e f) -> p l e f", l=2, e=4)
            WdT = w("WdT").rearrange("p (l e d) -> p l e d", l=2, e=4)
            for l in range(2):
                pe.wait_ge(consts, 2 + l)
                for e in range(4):
                    mm(ps[:, 2, e * D:(e + 1) * D], WgT[:, l, e, :], tabT[:])
                for e in range(4):
                    last = mm(ps[:, 3, e * D:(e + 1) * D], WuT[:, l, e, :], tabT[:])
                last.then_inc(tabmm, 1)
                pe.wait_ge(tabz, l + 1)
                for e in range(4):
                    last = mm(ps[0:D, 4, 0:D], WdT[:, l, e, :], tab_z[:, e, :], start=(e == 0), stop=(e == 3))
                last.then_inc(tabmm, 1)
            pe.wait_ge(consts, 4)
            mm(ps[0:D, 5, 0:D], tabT[:], w("lmT")).then_inc(tabmm, 1)
            pe.wait_ge(consts, 5)
            turn(ps[0:D, 6, 0:D], tabs[:, 1, :]).then_inc(tabmm, 1)
            pe.wait_ge(consts, 6)
            for hd in range(8):
                mm(ps[0:8, 2, hd * D:(hd + 1) * D], w("L0_Wq")[:, 8 * hd:8 * hd + 8], xtabT[:, 0, :])
                mm(ps[0:8, 3, hd * D:(hd + 1) * D], w("L0_Wk")[:, 8 * hd:8 * hd + 8], xtabT[:, 0, :])
            mm(ps[:, 4, 0:D], xtabT[:].rearrange("p a b -> p (a b)"), w("L0_Wv")).then_inc(tabmm, 1)
            pe.wait_ge(consts, 7)
            for hd in range(8):
                last = mm(ps[0:D, 5, hd * D:(hd + 1) * D], qtab[:, hd, :], ktab[:, hd, :])
            last.then_inc(tabmm, 1)
            pe.wait_ge(consts, 8)
            pe.wait_ge(late, LATE)

            def features(name, src, width=D):
                n = TURN[name]
                for c in CH:
                    pe.wait_ge(rows_ready, nth(n, c))
                    for t in TILES:
                        last = turn(bank(c, 3)[0:width, t * P:(t + 1) * P], src[c][:, t, 0:width])
                    last.then_inc(turned, 1)

            def project(n, lhs, weight, at=2):
                width = weight.shape[1]
                for c in CH:
                    pe.wait_ge(feat_ready, nth(n, c))
                    for t in TILES:
                        last = mm(bank(c, at)[:, t * width:(t + 1) * width], lhs[c][0:weight.shape[0], t * P:(t + 1) * P], weight)
                    last.then_inc(proj_ready, 1)

            def attention(first, count, operands, ordinal, q, k, v, heads, full, mask, dv):
                bl = blocks(full)

                def scores(s, c):
                    for e in range(heads):
                        for t in TILES:
                            at, wd = (0 if t == 0 else (T if full else P)), (T if full or t == 1 else P)
                            last = mm(bank(c, e)[:, at:at + wd], q(s, c, e, t), k(s, c, e)[:, 0:wd],
                                      start=True, stop=(mask is None))
                            if mask is not None:
                                b0, m = mask[t]
                                last = mm(bank(c, e)[:, at + b0 * P:at + b0 * P + m.shape[1]], ident_b[:], m,
                                          start=False, stop=True)
                    last.then_inc(at_scores, 1)

                def values(s, c):
                    pe.wait_ge(at_probsT, nth(first + s, c))
                    for e in range(heads):
                        for t in TILES:
                            mine = [(b, kt_) for b, (qt_, kt_) in enumerate(bl) if qt_ == t]
                            for z, (b, kt_) in enumerate(mine):
                                x = e * len(bl) + b
                                o = 256 + (e * 2 + t) * dv
                                last = mm(bank(c, 3)[:, o:o + dv], prT[c][:, x * P:(x + 1) * P], v(s, c, e, kt_),
                                          start=(z == 0), stop=(z == len(mine) - 1))
                    last.then_inc(at_av, 1)

                for c in CH:
                    pe.wait_ge(operands, nth(ordinal, c))
                    scores(0, c)
                for u in range(2 * count):
                    s, c = u // 2, u % 2
                    pe.wait_ge(at_probs, nth(first + s, c))
                    for x in range(heads * len(bl)):
                        if x == 4 or x + 1 == heads * len(bl) < 5:
                            if s + 1 < count:
                                scores(s + 1, c)
                            if s > 0:
                                pe.wait_ge(at_out, nth(first + s - 1, c))
                        last = turn(ps[:, 4 * c + 2 + x // 4, (x % 4) * P:(x % 4 + 1) * P],
                                    pr[c][:, x * P:(x + 1) * P])
                    last.then_inc(at_turned, 1)
                    if u > 0:
                        values((u - 1) // 2, (u - 1) % 2)
                values(count - 1, 1)

            causal = {0: (0, maskb[:, 0, :]), 1: (1, maskb[:, 0, :])}
            window = {0: (0, maskb[:, 0, :]), 1: (0, maskb[:, 1:3, :].rearrange("p a b -> p (a b)"))}

            with pe.Fori(0, PASSES) as i:
                for c in CH:
                    pe.wait_ge(hotT_ready, c + 1)
                    pe.wait_ge(hot_ready, c + 1)
                    for t in TILES:
                        mm(bank(c, t), hotT[c][:, t * P:(t + 1) * P], score_tab[:].rearrange("p a b -> p (a b)"))
                    for t in TILES:
                        mm(bank(c, 2)[:, t * P:(t + 1) * P], hotT[c][0:D, t * P:(t + 1) * P],
                           tabs[:].rearrange("p a b -> p (a b)"))
                    for t in TILES:
                        for j in TILES:
                            last = mm(bank(c, 3)[:, t * D:(t + 1) * D], allow[:, j, t * P:(t + 1) * P], hot[c][:, j, :],
                                      start=(j == 0), stop=(j == 1))
                    last.then_inc(a0_scores, 1)
                if LAST_STAGE >= 2:
                    for c in CH:
                        pe.wait_ge(a0_probs, c + 1)
                        for t in TILES:
                            for hp in range(4):
                                last = turn(bank(c, t)[:, hp * P:(hp + 1) * P],
                                            sm[c][:, t, 2 * hp:2 * hp + 2, :].rearrange("p a b -> p (a b)"))
                        last.then_inc(a0_probsT_ps, 1)
                    for c in CH:
                        pe.wait_ge(a0_probsT, c + 1)
                        for t in TILES:
                            for hp in range(4):
                                o = t * 72 + hp * 18
                                last = mm(bank(c, 2)[:, o:o + 18], pT[c][:, t * 512 + hp * P:t * 512 + (hp + 1) * P],
                                          vblk[:, hp, :, :].rearrange("p a b -> p (a b)"))
                        last.then_inc(a0_av, 1)
                    features("L0_attn_out", [att[c][:, :, 0:D] for c in CH])
                    project(TURN["L0_attn_out"], xT, w("L0_Wo"))
                if LAST_STAGE >= 3:
                    features("L0_ffn_in", xn)
                    project(TURN["L0_ffn_in"], xT, wide("L0_gate"))
                    lat = w("lattice").rearrange("p (e o) -> p e o", o=D)
                    for x in range(17):
                        if x < 16:
                            for c in CH:
                                pe.wait_ge(z_ready, nth(x, c))
                                if x >= 2:
                                    pe.wait_ge(zT_ready, nth(x - 2, c))
                                for q in range(4):
                                    last = turn(bank(c, x % 2)[:, q * P:(q + 1) * P],
                                                zb[x % 2][c][:, 2 * q:2 * q + 2, :].rearrange("p a b -> p (a b)"))
                                last.then_inc(z_turned, 1)
                        if x >= 1:
                            y = x - 1
                            t, k8 = y // 8, y % 8
                            for c in CH:
                                pe.wait_ge(zT_ready, nth(y, c))
                                for q in range(4):
                                    last = mm(bank(c, 2)[:, t * D:(t + 1) * D], zT[y % 2][c][:, q * P:(q + 1) * P],
                                              lat[:, k8 * 4 + q, :], start=(k8 == 0 and q == 0), stop=(k8 == 7 and q == 3))
                                last.then_inc(zsum_ready, 1)
                    features("L0_ffn_out", xc)
                    project(TURN["L0_ffn_out"], xT, w("L0_out"))
                if LAST_STAGE >= 4:
                    features("L1_attn_in", xn)
                    n = TURN["L1_attn_in"]
                    project(n, xT, wide("L1_wkv"))
                    for c in CH:
                        for hf in range(2):
                            last = mm(bank(c, hf), xT[c][:, 0:P], wide("L1_wq")[:, hf * 512:(hf + 1) * 512])
                        last.then_inc(q_proj, 1)

                    def second_tile(c):
                        pe.wait_ge(q_used, c + 1)
                        for hf in range(2):
                            last = mm(bank(c, hf), xT[c][:, P:T], wide("L1_wq")[:, hf * 512:(hf + 1) * 512])
                        last.then_inc(q_proj, 1)

                    def turn_q(t, c):
                        pe.wait_ge(q_roped, nth(t, c))
                        if t == 0:
                            pe.wait_ge(qk_ready, nth(0, c))
                        else:
                            pe.wait_ge(qT_ready, nth(0, c))
                        for hp in range(8):
                            last = turn(ps[:, 4 * c + 2 + hp // 4, (hp % 4) * P:(hp % 4 + 1) * P],
                                        att[c][:, t, hp * P:(hp + 1) * P])
                        last.then_inc(q_turned, 1)

                    second_tile(0)
                    for c in CH:
                        pe.wait_ge(qk_rows, nth(0, c))
                        for t in TILES:
                            last = turn(bank(c, 3)[:, t * P:(t + 1) * P], kd[c][:, t].rearrange("p a b -> p (a b)"))
                        last.then_inc(qk_turned, 1)
                    turn_q(0, 0)
                    second_tile(1)
                    turn_q(0, 1)
                    for c in CH:
                        turn_q(1, c)
                    attention(STEP["L1"], 8, qT_ready, 1,
                              lambda s, c, e, t: qT[c][:, s, t * P:(t + 1) * P],
                              lambda s, c, e: kT[c][:, e, :],
                              lambda s, c, e, kt_: vv[c][:, kt_, :], 2, False, window, D)
                    for t in TILES:
                        for c in CH:
                            pe.wait_ge(at_out, nth(STEP["L1"] + 7, c))
                            if t == 1:
                                pe.wait_ge(ao_ready, nth(0, c))
                            for hp in range(8):
                                last = turn(ps[:, 4 * c + hp // 4, (hp % 4) * P:(hp % 4 + 1) * P],
                                            att[c][:, t, hp * P:(hp + 1) * P])
                            last.then_inc(ao_turned, 1)
                    for t in TILES:
                        for c in CH:
                            pe.wait_ge(ao_ready, nth(t, c))
                            for hp in range(8):
                                last = mm(bank(c, 2)[:, t * D:(t + 1) * D], qT[c][:, hp, t * P:(t + 1) * P],
                                          w("L1_wo")[:, hp * D:(hp + 1) * D], start=(hp == 0), stop=(hp == 7))
                            last.then_inc(ao_rows, 1)
                if LAST_STAGE >= 5:
                    features("L1_ffn_in", xn)
                    project(TURN["L1_ffn_in"], xT, wide("L1_router"))
                    for c in CH:
                        for t in TILES:
                            last = mm(bank(c, t), xT[c][:, t * P:(t + 1) * P], wide("L1_W1"))
                        last.then_inc(q_proj, 1)
                    for c in CH:
                        pe.wait_ge(f1_z, c + 1)
                        for t in TILES:
                            for k4 in range(4):
                                turn(bank(c, t)[:, k4 * P:(k4 + 1) * P], z1[c][:, t, k4 * P:(k4 + 1) * P])
                            last = turn(bank(c, 3)[0:32, t * P:(t + 1) * P], z1[c][:, t, 512:544])
                        last.then_inc(f1_turned, 1)
                    for c in CH:
                        pe.wait_ge(f1_zT, c + 1)
                        for t in TILES:
                            for k4 in range(4):
                                mm(bank(c, 2)[:, t * D:(t + 1) * D], pT[c][:, t * 512 + k4 * P:t * 512 + (k4 + 1) * P],
                                   w("L1_W2")[:, k4 * D:(k4 + 1) * D], start=(k4 == 0), stop=False)
                            last = mm(bank(c, 2)[:, t * D:(t + 1) * D], mT[c][:, t * P:(t + 1) * P], w("L1_b2"),
                                      start=False, stop=True)
                        last.then_inc(ao_rows, 1)
                if LAST_STAGE >= 6:
                    features("L2_attn_in", xn)
                    for c in CH:
                        pe.wait_ge(feat_ready, nth(TURN["L2_attn_in"], c))
                        mm(bank(c, 2)[0:D, 0:T], wide("L2_Wqcomp"), xT[c][:])
                        mm(bank(c, 2)[0:D, T:2 * T], wide("L2_Wkvcomp"), xT[c][:]).then_inc(c2_ready, 1)
                    for c in CH:
                        pe.wait_ge(c2_used, c + 1)
                        for t in TILES:
                            mm(bank(c, 0)[:, t * 192:t * 192 + D], pT[c][0:D, t * P:(t + 1) * P], w("L2_Wq"))
                            last = mm(bank(c, 0)[:, t * 192 + D:(t + 1) * 192], pT[c][0:D, T + t * P:T + (t + 1) * P],
                                      w("L2_Wkv"))
                        last.then_inc(q_proj, 1)
                    for c in CH:
                        pe.wait_ge(qk_rows, nth(1, c))
                        for g in range(2):
                            for t in TILES:
                                last = turn(bank(c, 3)[0:D, g * T + t * P:g * T + (t + 1) * P], kk[c][:, t, g * D:(g + 1) * D])
                        last.then_inc(qk_turned, 1)
                    attention(STEP["L2"], 1, qk_ready, 1, lambda s, c, e, t: pT[c][0:D, t * P:(t + 1) * P],
                              lambda s, c, e: pT[c][0:D, T:2 * T], lambda s, c, e, kt_: vv[c][:, kt_, :],
                              1, False, causal, D)
                if LAST_STAGE >= 7:
                    features("L2_ffn_in", [xd[c][:].rearrange("p t a d -> p t (a d)") for c in CH], P)
                    for c in CH:
                        pe.wait_ge(feat_ready, nth(TURN["L2_ffn_in"], c))
                        for t in TILES:
                            mm(bank(c, 2)[:, t * 8:(t + 1) * 8], xT2[c][0:D, t * P:(t + 1) * P], w("L2_gate")[0:D, :],
                               start=True, stop=False)
                            last = mm(bank(c, 2)[:, t * 8:(t + 1) * 8], ones1[:], w("L2_gateb"), start=False, stop=True)
                        last.then_inc(proj_ready, 1)
                    for c in CH:
                        pe.wait_ge(f2_hot, c + 1)
                        mm(bank(c, 2)[:, 32:40], tri_b[:], mb[c][:, 0, :])
                        mm(bank(c, 2)[:, 40:48], ones_b[:], mb[c][:, 0, :], start=True, stop=False)
                        mm(bank(c, 2)[:, 40:48], tri_b[:], mb[c][:, 1, :], start=False, stop=True)
                        mm(bank(c, 2)[:, 48:56], ones_b[:], mb[c][:, 0, :], start=True, stop=False)
                        mm(bank(c, 2)[:, 48:56], ones_b[:], mb[c][:, 1, :], start=False, stop=True).then_inc(f2_count, 1)
                        for t in TILES:
                            last = turn(bank(c, 3)[0:8, t * P:(t + 1) * P], sel[c][:, t, 0:8])
                        last.then_inc(f2_maskT, 1)
                    for c in CH:
                        pe.wait_ge(f2_mask, c + 1)
                        for pr_ in range(4):
                            last = mm(ps[:, 4 * c + pr_ // 2, (pr_ % 2) * T:(pr_ % 2 + 1) * T], sel_b[:, pr_, :], mTb[c][:])
                        last.then_inc(f2_bc, 1)
                    for c in CH:
                        pe.wait_ge(f2_xm, c + 1)
                        for m in range(2):
                            o = bank(c, 2)[:, m * T:(m + 1) * T]
                            for pr_ in range(4):
                                mm(o, w("L2_W1")[:, pr_ * 256 + m * P:pr_ * 256 + (m + 1) * P],
                                   pT[c][:, pr_ * T:(pr_ + 1) * T], start=(pr_ == 0), stop=False)
                            last = mm(o, w("L2_b1")[:, m * P:(m + 1) * P], mT[c][0:8, :], start=False, stop=True)
                        last.then_inc(f2_hid, 1)
                    for c in CH:
                        pe.wait_ge(f2_relu, c + 1)
                        for t in TILES:
                            for m in range(2):
                                mm(bank(c, t), qT[c][:, m, t * P:(t + 1) * P], w("L2_W2")[:, m * 512:(m + 1) * 512],
                                   start=(m == 0), stop=False)
                            last = mm(bank(c, t), ones1[:], w("L2_b2"), start=False, stop=True)
                        last.then_inc(f2_y, 1)
                if LAST_STAGE >= 8:
                    features("L3_attn_in", xn)
                    for c in CH:
                        pe.wait_ge(feat_ready, nth(TURN["L3_attn_in"], c))
                        mm(bank(c, 2)[0:D, 0:T], wide("L3_Wq"), xT[c][:])
                        mm(bank(c, 2)[0:D, T:2 * T], wide("L3_Wk"), xT[c][:])
                        for t in TILES:
                            last = mm(bank(c, 1)[:, t * D:(t + 1) * D], xT[c][:, t * P:(t + 1) * P], wide("L3_Wv"))
                        last.then_inc(c2_ready, 1)
                    attention(STEP["L3"], 1, c2_used, 1, lambda s, c, e, t: pT[c][0:D, t * P:(t + 1) * P],
                              lambda s, c, e: pT[c][0:D, T:2 * T], lambda s, c, e, kt_: vv[c][:, kt_, :],
                              1, True, None, D)
                if LAST_STAGE >= 9:
                    features("L3_qkv_in", xc)
                    project(TURN["L3_qkv_in"], xT, wide("L3_wqkv"))
                    for c in CH:
                        pe.wait_ge(qk_rows, nth(2, c))
                        for g in range(2):
                            for t in TILES:
                                last = turn(bank(c, 3)[:, g * T + t * P:g * T + (t + 1) * P],
                                            kd4[c][:, g, t, :])
                        last.then_inc(qk_turned, 1)
                    attention(STEP["L3f"], 2, qk_ready, 2,
                              lambda s, c, e, t: pT[c][32 * (2 * s + e):32 * (2 * s + e) + 32, t * P:(t + 1) * P],
                              lambda s, c, e: pT[c][32 * (2 * s + e):32 * (2 * s + e) + 32, T:2 * T],
                              lambda s, c, e, kt_: kk[c][:, kt_, 96 + 16 * s:112 + 16 * s], 2, False, causal, 16)
                    features("L3_attn_out", [att[c][:, :, 0:D] for c in CH])
                    project(TURN["L3_attn_out"], xT, wide("L3_wo"))
                    features("L3_moe_in", xc)
                    project(TURN["L3_moe_in"], xT, wide("L3_router"))
                    w13 = wide("L3_w13").rearrange("p (e f) -> p e f", e=8)
                    for x in range(16):
                        t, e = x // 8, x % 8
                        for c in CH:
                            if x >= 3:
                                pe.wait_ge(f4_h, nth(x - 3, c))
                            mm(bank(c, MOE_BANK[x % 3])[:, 0:2 * HIDDEN3], xT[c][:, t * P:(t + 1) * P],
                               w13[:, e, :]).then_inc(f4_gu, 1)
                    for t in TILES:
                        for part in range(3):
                            for c in CH:
                                if part == 0:
                                    pe.wait_ge(f4_h, nth(15, c))
                                if t == 1:
                                    pe.wait_ge(f4_hT, nth(part, c))
                                for kx in range(4 * part, min(4 * part + 4, 11)):
                                    kw = P if kx < 10 else 80
                                    u = kx - 4 * part
                                    last = turn(bank(c, MOE_BANK[part])[0:kw, u * P:(u + 1) * P],
                                                hid[t][c][:, kx * P:kx * P + kw])
                                last.then_inc(f4_turned, 1)
                        for c in CH:
                            for kx in range(11):
                                if kx % 4 == 0:
                                    pe.wait_ge(f4_hT, nth(3 * t + kx // 4, c))
                                kw = P if kx < 10 else 80
                                src = pT[c][:, kx * P:(kx + 1) * P] if kx < 8 else prT[c][0:kw, (kx - 8) * P:(kx - 7) * P]
                                wt = w("L3_w2")[:, kx * D:(kx + 1) * D] if kx < 10 else w("L3_w2t")
                                last = mm(bank(c, 2)[:, t * D:(t + 1) * D], src, wt, start=(kx == 0), stop=(kx == 10))
                            last.then_inc(ao_rows, 1)
                close_pass(pe, i)

        @block.scalar
        def _(act):
            a = nc.scalar.activation
            for l in range(2):
                act.wait_ge(tabmm, 2 + 2 * l)
                a(tab_t[:], ps[:, 2, 0:4 * D].rearrange("p (e v) -> p e v", e=4), ACT.Tanh, scale=0.5).then_inc(taba, 1)

            def features(name, width=D):
                n = TURN[name]
                for c in CH:
                    act.wait_ge(turned, nth(n, c))
                    dst = xT[c][0:D, :] if width == D else xT2[c][:]
                    a(dst, bank(c, 3)[0:width, 0:T], ACT.Copy).then_inc(feat_ready, 1)

            def logits_exp(n, width):
                for c in CH:
                    act.wait_ge(shifted, nth(n, c))
                    a(prob[c][:, :, 0:width], prob[c][:, :, 0:width], ACT.Exp).then_inc(expd, 1)

            def attention(first, count, heads, full, scale):
                nb_ = len(blocks(full))

                def copy_turned(s, c):
                    act.wait_ge(at_turned, nth(first + s, c))
                    wd = heads * nb_ * P
                    a(prT[c][:, 0:wd], ps[:, 4 * c + 2:4 * c + 4, :].rearrange("p a b -> p (a b)")[:, 0:wd],
                      ACT.Copy).then_inc(at_probsT, 1)

                for u in range(2 * count):
                    s, c = u // 2, u % 2
                    act.wait_ge(at_bias, nth(first + s, c))
                    for e in range(heads):
                        for t in TILES:
                            at, wd = (0 if t == 0 else (T if full else P)), (T if full or t == 1 else P)
                            x = e * nb_ * P + at
                            last = a(pr[c][:, x:x + wd], bank(c, e)[:, at:at + wd], ACT.Exp,
                                     bias=nb[c][:, 2 * t + e:2 * t + e + 1], scale=scale(s, c, e, t),
                                     accum_out=rs[c][:, s % 2, 2 * t + e:2 * t + e + 1])
                    last.then_inc(at_probs, 1)
                    if u > 0:
                        copy_turned((u - 1) // 2, (u - 1) % 2)
                copy_turned(count - 1, 1)

            with act.Fori(0, PASSES) as i:
                if LAST_STAGE >= 2:
                    for c in CH:
                        act.wait_ge(a0_max, c + 1)
                        a(sm[c][:], sm[c][:], ACT.Exp, scale=8 ** -0.5).then_inc(a0_exp, 1)
                    for c in CH:
                        act.wait_ge(a0_probsT_ps, c + 1)
                        a(pT[c][:], banks2(c, 0).rearrange("p a b -> p (a b)"), ACT.Copy).then_inc(a0_probsT, 1)
                    features("L0_attn_out")
                if LAST_STAGE >= 3:
                    features("L0_ffn_in")
                    logits_exp(0, D)
                    for x in range(16):
                        for c in CH:
                            act.wait_ge(z_turned, nth(x, c))
                            if x >= 2:
                                act.wait_ge(zsum_ready, nth(x - 2, c))
                            a(zT[x % 2][c][:], bank(c, x % 2), ACT.Copy).then_inc(zT_ready, 1)
                    features("L0_ffn_out")
                if LAST_STAGE >= 4:
                    features("L1_attn_in")
                    def q_squares(t, c):
                        act.wait_ge(q_roped, nth(t, c))
                        if t == 1:
                            act.wait_ge(q_var, nth(0, c))
                        a(qa[c][:], att[c][:, t, :], ACT.Square).then_inc(q_sq, 1)

                    def copy_q(t, c):
                        act.wait_ge(q_turned, nth(t, c))
                        a(qT[c][:, :, t * P:(t + 1) * P], banks2(c, 2).rearrange("p a (b q) -> p (a b) q", q=P),
                          ACT.Copy).then_inc(qT_ready, 1)

                    q_squares(0, 0)
                    for c in CH:
                        act.wait_ge(qk_turned, nth(0, c))
                        for e in range(2):
                            r = slice(D * e, D * e + D)
                            last = a(kT[c][r, e, :], bank(c, 3)[r, 0:T], ACT.Copy)
                        last.then_inc(qk_ready, 1)
                    copy_q(0, 0)
                    q_squares(0, 1)
                    copy_q(0, 1)
                    for c in CH:
                        q_squares(1, c)
                    for c in CH:
                        copy_q(1, c)
                    attention(STEP["L1"], 8, 2, False,
                              lambda s, c, e, t: exs[c][:, t, 2 * s + e:2 * s + e + 1])
                    for t in TILES:
                        for c in CH:
                            act.wait_ge(ao_turned, nth(t, c))
                            a(qT[c][:, :, t * P:(t + 1) * P], banks2(c, 0).rearrange("p a (b q) -> p (a b) q", q=P),
                              ACT.Copy).then_inc(ao_ready, 1)
                if LAST_STAGE >= 5:
                    features("L1_ffn_in")
                    for c in CH:
                        act.wait_ge(f1_turned, c + 1)
                        a(pT[c][:], banks2(c, 0).rearrange("p a b -> p (a b)"), ACT.Copy)
                        a(mT[c][:], bank(c, 3)[0:32, 0:T], ACT.Copy).then_inc(f1_zT, 1)
                if LAST_STAGE >= 6:
                    features("L2_attn_in")
                    for c in CH:
                        act.wait_ge(c2_ready, c + 1)
                        a(pT[c][0:D, 0:512], bank(c, 2)[0:D, :], ACT.Copy).then_inc(c2_used, 1)
                    for c in CH:
                        act.wait_ge(qk_turned, nth(1, c))
                        a(pT[c][0:D, 0:512], bank(c, 3)[0:D, :], ACT.Copy).then_inc(qk_ready, 1)
                    attention(STEP["L2"], 1, 1, False, lambda s, c, e, t: 0.125)
                if LAST_STAGE >= 7:
                    features("L2_ffn_in", P)
                    logits_exp(1, 8)
                    for c in CH:
                        act.wait_ge(f2_maskT, c + 1)
                        a(mT[c][0:8, :], bank(c, 3)[0:8, 0:T], ACT.Copy)
                        a(mTb[c][:], bank(c, 3)[0:8, 0:T], ACT.Copy).then_inc(f2_mask, 1)
                    for c in CH:
                        act.wait_ge(f2_hid, c + 1)
                        a(qT[c][:, 0:2, :], bank(c, 2).rearrange("p (m t) -> p m t", m=2), ACT.Relu).then_inc(f2_relu, 1)
                if LAST_STAGE >= 8:
                    features("L3_attn_in")
                    for c in CH:
                        act.wait_ge(c2_ready, nth(1, c))
                        a(pT[c][0:D, 0:512], bank(c, 2)[0:D, :], ACT.Copy)
                        a(vv[c][:], bank(c, 1)[:, 0:P].rearrange("p (t d) -> p t d", t=2), ACT.Copy).then_inc(c2_used, 1)
                    attention(STEP["L3"], 1, 1, True, lambda s, c, e, t: 0.125)
                if LAST_STAGE >= 9:
                    features("L3_qkv_in")
                    for c in CH:
                        act.wait_ge(qk_turned, nth(2, c))
                        a(pT[c][:, 0:512], bank(c, 3), ACT.Copy).then_inc(qk_ready, 1)
                    attention(STEP["L3f"], 2, 2, False, lambda s, c, e, t: 0.25)
                    features("L3_attn_out")
                    features("L3_moe_in")
                    logits_exp(2, 8)
                    for x in range(16):
                        for c in CH:
                            act.wait_ge(f4_gu, nth(x, c))
                            if x >= 3:
                                act.wait_ge(f4_h, nth(x - 3, c))
                            a(th[c][:, x % 3, :], bank(c, MOE_BANK[x % 3])[:, 0:HIDDEN3], ACT.Tanh, scale=0.5).then_inc(f4_tanh, 1)
                    for t in TILES:
                        for part in range(3):
                            for c in CH:
                                act.wait_ge(f4_turned, nth(t * 3 + part, c))
                                if t == 1:
                                    act.wait_ge(ao_rows, nth(3, c))
                                src = bank(c, MOE_BANK[part])
                                if part < 2:
                                    a(pT[c][:, part * 512:(part + 1) * 512], src, ACT.Copy).then_inc(f4_hT, 1)
                                else:
                                    a(prT[c][:, 0:256], src[:, 0:256], ACT.Copy)
                                    a(prT[c][0:80, 256:384], src[0:80, 256:384], ACT.Copy).then_inc(f4_hT, 1)
                close_pass(act, i)

        @block.vector
        def _(dve):
            v = nc.vector
            setup = Steps(dve, vset)
            dve.wait_ge(iset, 4)
            dve.wait_ge(early, EARLY)
            setup.done(v.tensor_copy(ids_bc[:], ids_bc_i))
            setup.done(v.tensor_copy(ids_tok[:], ids_tok_i[:]))
            setup.done(v.tensor_copy(edges[:], edges_i))
            setup.done(v.tensor_copy(ident_b[:], ident))
            setup.done(v.memset(diag_b[:], 0.0))
            setup.after()
            for j in TILES:
                setup.done(v.tensor_copy(diag_b[:, j, j * P:(j + 1) * P], ident))
                setup.done(v.tensor_copy(maskb[:, 2 * j, :], w("causal")))
            setup.done(v.tensor_copy(maskb[:, 1, :], w("window")))
            setup.done(v.tensor_copy(tri_b[:], w("tri")))
            setup.done(v.memset(ones_b[:], 1.0))
            setup.done(v.tensor_tensor(qk_norm[:], vecs[:, 4, :], vecs[:, 5, :], ALU.mult))
            setup.done(v.memset(vblk[:], 0.0))
            setup.done(v.memset(score_tab[:], 0.0))
            setup.done(v.memset(xtabT[D:D + 1, :, :], 1.0))
            for c in CH:
                setup.done(v.memset(xT[c][D:P, :], 0.0))
                setup.done(v.memset(hotT[c][:], 0.0))
                setup.done(v.memset(kT[c][:], 0.0))
                setup.after()
                setup.done(v.memset(xT[c][D:D + 1, :], 1.0))
                setup.done(v.memset(lg[c][:], BIG))
                for k in (1, 2, 6):
                    setup.done(v.memset(pick[k][c][:], BIG))
                setup.done(v.memset(kd4[c][:], 0.0))
            setup.after()
            dve.drain().then_inc(consts, 1)
            with dve.Fori(0, 8) as i:
                for half_ in range(2):
                    dve.wait_ge(edge_used, i * 2 + half_ + 1)
                    for u in range(8):
                        v.tensor_scalar(hot_src[:, half_, u, :], iota_b[:],
                                        edges[:, 0, bass.ds(i * 16 + (half_ * 8 + u), 1)], None, ALU.is_equal)
                        last = v.tensor_scalar(hot_dst[:, half_, u, :], iota_b[:],
                                               edges[:, 1, bass.ds(i * 16 + (half_ * 8 + u), 1)], None, ALU.is_equal)
                    last.then_inc(edge_hot, 1)
            v.tensor_copy(tabT[:], w("embT")).then_inc(consts, 1)
            dve.wait_ge(tabmm, 1)
            setup.done(v.tensor_scalar(allow[:], ps[:, 0:2, 0:T], 0.5, None, ALU.is_gt))
            for l in range(2):
                dve.wait_ge(taba, l + 1)
                setup.done(v.scalar_tensor_tensor(tab_a[:], tab_t[:], 1.0,
                                                  ps[:, 2, 0:4 * D].rearrange("p (e v) -> p e v", e=4), ALU.add, ALU.mult))
                setup.after()
                v.scalar_tensor_tensor(tab_z[:], ps[:, 3, 0:4 * D].rearrange("p (e v) -> p e v", e=4), 0.125,
                                       tab_a[:], ALU.mult, ALU.mult).then_inc(tabz, 1)
                dve.wait_ge(tabmm, 3 + 2 * l)
                dve.wait_ge(consts, 2 + l)
                v.tensor_tensor(tabT[:], tabT[:], ps[0:D, 4, 0:D], ALU.add).then_inc(consts, 1)
            dve.wait_ge(tabmm, 6)
            setup.done(v.tensor_copy(tabs[:, 0, :], ps[0:D, 5, 0:D]))
            setup.after()
            setup.done(v.reduce_sum(tab_s[:, 0:1], tabs[:, 0, :], AX.X))
            setup.after()
            setup.done(v.scalar_tensor_tensor(tab_q[:], tab_s[:, 0:1].to_broadcast([D, D]), -1.0 / D, tabs[:, 0, :],
                                              ALU.mult, ALU.add))
            setup.after()
            setup.done(v.tensor_tensor(tabs[:, 1, :], tab_q[:], tab_q[:], ALU.mult))
            setup.after()
            setup.done(v.reduce_sum(tab_s[:, 1:2], tabs[:, 1, :], AX.X))
            setup.after()
            v.tensor_scalar(tab_s[:, 2:3], tab_s[:, 1:2], 1.0 / D, EPS, ALU.mult, ALU.add).then_inc(tabv, 1)
            dve.wait_ge(tabpow, 1)
            v.tensor_scalar(tabs[:, 1, :], tab_q[:], tab_s[:, 3:4], None, ALU.mult).then_inc(consts, 1)
            dve.wait_ge(tabmm, 7)
            v.tensor_copy(xtabT[0:D, 0, :], ps[0:D, 6, 0:D])
            v.tensor_copy(xtabT[0:D, 1, :], ps[0:D, 6, 0:D]).then_inc(consts, 1)
            dve.wait_ge(tabmm, 8)
            v.tensor_copy(qtab[:].rearrange("p a b -> p (a b)"), ps[0:8, 2, :])
            v.tensor_copy(ktab[:].rearrange("p a b -> p (a b)"), ps[0:8, 3, :]).then_inc(consts, 1)
            for g in range(2):
                r = slice(g * D, g * D + D)
                setup.done(v.memset(vblk[r, :, g, 8:9], 1.0))
                setup.done(v.tensor_copy(vblk[r, :, g, 0:8],
                                         ps[r, 4, 0:D].rearrange("p (a g d) -> p a g d", a=4, g=2)[:, :, g, :]))
            dve.wait_ge(late, LATE)
            setup.done(v.tensor_copy(sel_b[:], w("sel8").rearrange("p (a b) -> p a b", a=4)))
            setup.done(v.tensor_scalar(w("L3_wqkv"), w("L3_wqkv"), ln1w[:, 0:1], None, ALU.mult))
            setup.done(v.tensor_scalar(w("L3_router"), w("L3_router"), ln2w[:, 0:1], None, ALU.mult))
            setup.done(v.tensor_scalar(w("L3_w13"), w("L3_w13"), ln2w[:, 0:1], None, ALU.mult))
            dve.wait_ge(tabmm, 9)
            setup.done(v.tensor_copy(score_tab[0:D].rearrange("p a b -> p (a b)"), ps[0:D, 5, :]))
            setup.after()
            dve.drain().then_inc(consts, 1)

            def bcast(ap, n):
                return ap.unsqueeze(2).to_broadcast([ap.shape[0], ap.shape[1], n])

            def bcast_mid(ap, n):
                return ap.unsqueeze(2).to_broadcast([ap.shape[0], ap.shape[1], n, ap.shape[2]])

            def bcast_heads(ap, n):
                return ap.unsqueeze(1).to_broadcast([ap.shape[0], n, ap.shape[1]])

            def tv(ap, t=2):
                return ap.rearrange("p (t f) -> p t f", t=t)

            with dve.Fori(0, PASSES) as i:
                steps = Steps(dve, vstep)
                done, after = steps.done, steps.after
                last = [0, 0]

                def centre(src):
                    for c in CH:
                        after(last[c])
                        last[c] = done(v.reduce_sum(st[c][:, 0, 0:2], src[c][:], AX.X))
                    for c in CH:
                        after(last[c])
                        last[c] = done(v.scalar_tensor_tensor(xc[c][:], bcast(st[c][:, 0, 0:2], D), -1.0 / D, src[c][:],
                                                              ALU.mult, ALU.add))
                    squares(xc)

                def squares(src):
                    for c in CH:
                        after(last[c])
                        last[c] = done(v.tensor_tensor(sq[c][:], src[c][:], src[c][:], ALU.mult))
                    for c in CH:
                        after(last[c])
                        last[c] = done(v.reduce_sum(st[c][:, 1, 0:2], sq[c][:], AX.X))

                def inverse_root(name, eps, width=2):
                    n = NORM[name]
                    for c in CH:
                        after(last[c])
                        v.tensor_scalar(st[c][:, 2, 0:width], st[c][:, 1, 0:width], 1.0 / D, eps, ALU.mult,
                                        ALU.add).then_inc(var_ready, 1)

                def rooted(name, c):
                    dve.wait_ge(rstd_ready, nth(NORM[name], c))

                def norm_rows(name, src, dst=None):
                    centre(src)
                    inverse_root(name, EPS)
                    for c in CH:
                        rooted(name, c)
                        if dst is None:
                            v.tensor_tensor(xn[c][:], xc[c][:], bcast(rstd[c][:, 0:2], D), ALU.mult).then_inc(rows_ready, 1)
                        else:
                            for g in range(2):
                                q = v.tensor_tensor(xd[c][:, :, g, :], xc[c][:], bcast(rstd[c][:, 0:2], D), ALU.mult)
                            q.then_inc(rows_ready, 1)

                def post_norm(name, proj, turn_name, g):
                    for c in CH:
                        dve.wait_ge(proj_ready, nth(proj, c))
                        last[c] = done(v.tensor_tensor(xn[c][:], xn[c][:], tv(bank(c, 2)[:, 0:P]), ALU.add))
                    centre(xn)
                    inverse_root(name, EPS)
                    for c in CH:
                        rooted(name, c)
                        last[c] = done(v.tensor_tensor(sq[c][:], xc[c][:], bcast(rstd[c][:, 0:2], D), ALU.mult))
                    for c in CH:
                        after(last[c])
                        last[c] = done(v.tensor_tensor(sq[c][:], sq[c][:], bcast_heads(vecs[:, g, :], 2), ALU.mult))
                    for c in CH:
                        after(last[c])
                        last[c] = done(v.tensor_tensor(sq[c][:], sq[c][:], bcast_heads(vecs[:, g + 1, :], 2), ALU.add))
                    for c in CH:
                        after(last[c])
                        last[c] = done(v.tensor_tensor(h[c][:], h[c][:], sq[c][:], ALU.add))

                def route(proj, E, k, at=0):
                    lo = D - E
                    for c in CH:
                        dve.wait_ge(proj_ready, nth(proj, c))
                        last[c] = done(v.tensor_copy(lg[c][:, :, lo:D], tv(bank(c, 2)[:, 0:2 * E])))
                    for c in CH:
                        after(last[c])
                        for t in TILES:
                            last[c] = done(v.max(top[c][:, t, :], lg[c][:, t, lo:D]))
                    for c in CH:
                        after(last[c])
                        last[c] = done(v.tensor_copy(pick[k][c][:, :, 0:k], top[c][:, :, 0:k]))
                    for c in CH:
                        after(last[c])
                        for t in TILES:
                            last[c] = done(v.match_replace(rep[c][:, t, lo:D + 8 - k], pick[k][c][:, t, :],
                                                           lg[c][:, t, lo:D + 8 - k], -BIG))
                    for c in CH:
                        after(last[c])
                        last[c] = done(v.tensor_scalar(sel[c][:, :, 0:E], rep[c][:, :, lo:D], -0.5 * BIG, None, ALU.is_lt))

                def shift(E):
                    for c in CH:
                        v.tensor_tensor(prob[c][:, :, 0:E], lg[c][:, :, D - E:D], bcast(top[c][:, :, 0], E),
                                        ALU.subtract).then_inc(shifted, 1)

                def attention(first, count, heads, full, exp_scale, out_, dv=D):
                    def bias(s, c):
                        if first == STEP["L1"] and s in (0, 2):
                            dve.wait_ge(scales_ready, nth(1 + s // 2, c))
                        dve.wait_ge(at_scores, nth(first + s, c))
                        for t in TILES:
                            at, wd = (0 if t == 0 else (T if full else P)), (T if full or t == 1 else P)
                            last[c] = done(v.tensor_reduce(mx[c][:, 2 * t:2 * t + heads],
                                                           ps[:, 4 * c:4 * c + heads, at:at + wd], AX.X, ALU.max))
                        after(last[c])
                        m, n_ = tv(mx[c][:])[:, :, 0:heads], tv(nb[c][:])[:, :, 0:heads]
                        if isinstance(exp_scale, float):
                            v.tensor_scalar(n_, m, -exp_scale, None, ALU.mult).then_inc(at_bias, 1)
                        else:
                            v.scalar_tensor_tensor(n_, m, -1.0, exp_scale(s, c), ALU.mult, ALU.mult).then_inc(at_bias, 1)

                    def divide(s, c):
                        dve.wait_ge(at_av, nth(first + s, c))
                        r = tv(rr[c][:, 0:4])[:, :, 0:heads]
                        last[c] = done(v.reciprocal(r, tv(rs[c][:, s % 2])[:, :, 0:heads]))
                        after(last[c])
                        o = bank(c, 3)[:, 256:256 + heads * 2 * dv].rearrange("p (e t d) -> p t e d", t=2, d=dv)
                        v.tensor_tensor(out_(s, c), o, r.unsqueeze(3).to_broadcast([P, 2, heads, dv]),
                                        ALU.mult).then_inc(at_out, 1)

                    for c in CH:
                        bias(0, c)
                    for u in range(2 * count):
                        s, c = u // 2, u % 2
                        if s + 1 < count:
                            bias(s + 1, c)
                        if u > 0:
                            divide((u - 1) // 2, (u - 1) % 2)
                    divide(count - 1, 1)

                def add_to_h(step):
                    for c in CH:
                        dve.wait_ge(at_out, nth(step, c))
                        last[c] = done(v.tensor_tensor(h[c][:], h[c][:], xc[c][:], ALU.add))

                for c in CH:
                    v.tensor_scalar(hotT[c][0:D, :], ids_bc[:, bass.ds((i * 2 + c) * T, T)], w("iota_col")[0:D, :], None,
                                    ALU.is_equal).then_inc(hotT_ready, 1)
                    v.tensor_tensor(hot[c][:], bcast_heads(iota_b[:, 0:D], 2),
                                    bcast(ids_tok[:, bass.ds(i * 4 + 2 * c, 2)], D), ALU.is_equal).then_inc(hot_ready, 1)
                for c in CH:
                    dve.wait_ge(a0_scores, c + 1)
                    g = bank(c, 2)[:, 0:2 * P].rearrange("p (t a d) -> p t a d", t=2, a=2)
                    last[c] = done(v.tensor_copy(h[c][:], g[:, :, 0, :]))
                    done(v.tensor_copy(xn[c][:], g[:, :, 1, :]))
                    last[c] = done(v.tensor_scalar(pen[c][:], tv(bank(c, 3)[:, 0:P]), 0.5, NEG, ALU.is_lt, ALU.mult))
                if LAST_STAGE >= 2:
                    for c in CH:
                        after(last[c])
                        last[c] = done(v.tensor_tensor(sm[c][:], banks2(c, 0).rearrange("p t (h v) -> p t h v", h=8),
                                                       bcast_mid(pen[c][:], 8), ALU.add))
                    for c in CH:
                        after(last[c])
                        last[c] = done(v.reduce_max(st[c][:, 0, :], sm[c][:].rearrange("p t h v -> p (t h) v"), AX.X))
                    for c in CH:
                        after(last[c])
                        s3 = sm[c][:].rearrange("p t h v -> p (t h) v")
                        v.tensor_tensor(s3, s3, bcast(st[c][:, 0, :], D), ALU.subtract).then_inc(a0_max, 1)
                    for c in CH:
                        dve.wait_ge(a0_exp, c + 1)
                        v.tensor_tensor(sm[c][:], sm[c][:], bcast_mid(tv(bank(c, 3)[:, 0:P]), 8),
                                        ALU.mult).then_inc(a0_probs, 1)
                    for c in CH:
                        dve.wait_ge(a0_av, c + 1)
                        o = bank(c, 2)[:, 0:144].rearrange("p (a b) -> p a b", b=9)
                        last[c] = done(v.reciprocal(rr[c][:], o[:, :, 8]))
                        after(last[c])
                        for t in TILES:
                            q = v.tensor_tensor(att[c][:, t, 0:D].rearrange("p (h d) -> p h d", h=8),
                                                o[:, 8 * t:8 * t + 8, 0:8], bcast(rr[c][:, 8 * t:8 * t + 8], 8), ALU.mult)
                        q.then_inc(rows_ready, 1)
                    post_norm("L0_attn_post", 0, "L0_attn_out", 0)
                if LAST_STAGE >= 3:
                    norm_rows("L0_ffn_pre", h)
                    route(1, D, 6)
                    shift(D)
                    for c in CH:
                        dve.wait_ge(expd, c + 1)
                        last[c] = done(v.tensor_tensor(prob[c][:], prob[c][:], sel[c][:], ALU.mult))
                    for c in CH:
                        after(last[c])
                        last[c] = done(v.reduce_sum(st[c][:, 0, 0:2], prob[c][:], AX.X))
                    for c in CH:
                        after(last[c])
                        last[c] = done(v.reciprocal(rr[c][:, 0:2], st[c][:, 0, 0:2]))
                    for c in CH:
                        after(last[c])
                        last[c] = done(v.tensor_tensor(prob[c][:], prob[c][:], bcast(rr[c][:, 0:2], D), ALU.mult))
                    for c in CH:
                        after(last[c])
                    for x in range(16):
                        t, k8 = x // 8, x % 8
                        for c in CH:
                            if x >= 2:
                                dve.wait_ge(z_turned, nth(x - 2, c))
                            v.tensor_tensor(zb[x % 2][c][:], bcast_heads(xn[c][:, t, :], 8),
                                            bcast(prob[c][:, t, 8 * k8:8 * k8 + 8], D), ALU.mult).then_inc(z_ready, 1)
                    for c in CH:
                        dve.wait_ge(zsum_ready, nth(15, c))
                        v.tensor_copy(xc[c][:], tv(bank(c, 2)[:, 0:P])).then_inc(rows_ready, 1)
                    post_norm("L0_ffn_post", 2, "L0_ffn_out", 2)
                if LAST_STAGE >= 4:
                    norm_rows("L1_attn_pre", h)
                    for c in CH:
                        dve.wait_ge(proj_ready, nth(3, c))
                        kv = tv(bank(c, 2)[:, 0:256])
                        done(v.tensor_copy(vv[c][:], kv[:, :, D:P]))
                        done(v.tensor_tensor(kk[c][:, :, 0:D], kv[:, :, 0:D], cosq, ALU.mult))
                        done(v.tensor_tensor(kkm[c][:, :, 0:32], kv[:, :, 32:64], sinq[:, :, 0:32], ALU.mult))
                        last[c] = done(v.tensor_tensor(kkm[c][:, :, 32:64], kv[:, :, 0:32], sinq[:, :, 32:64], ALU.mult))
                    for c in CH:
                        after(last[c])
                        last[c] = done(v.tensor_tensor(kk[c][:, :, 0:D], kk[c][:, :, 0:D], kkm[c][:, :, 0:D], ALU.add))
                    squares([kk[c][:, :, 0:D] for c in CH])
                    inverse_root("L1_k", 1.1920929e-07)

                    def rope_q(t, c):
                        dve.wait_ge(q_proj, nth(t, c))
                        qp = banks2(c, 0).rearrange("p a (h f) -> p (a h) f", f=D)
                        qo = att[c][:, t, :].rearrange("p (h f) -> p h f", f=D)
                        qs = qb[c].rearrange("p (h f) -> p h f", f=D)
                        if t == 1:
                            dve.wait_ge(q_roped, c + 1)
                        v.tensor_tensor(qo, qp, bcast_heads(cosq[:, t, :], 16), ALU.mult)
                        v.tensor_tensor(qs[:, :, 0:32], qp[:, :, 32:64], bcast_heads(sinq[:, t, 0:32], 16), ALU.mult)
                        v.tensor_tensor(qs[:, :, 32:64], qp[:, :, 0:32], bcast_heads(sinq[:, t, 32:64], 16),
                                        ALU.mult).then_inc(q_used, 1)
                        dve.wait_ge(q_used, nth(t, c))
                        v.tensor_tensor(qo, qo, qs, ALU.add).then_inc(q_roped, 1)

                    def q_variance(t, c):
                        dve.wait_ge(q_sq, nth(t, c))
                        last[c] = done(v.reduce_sum(qsum[c][:, t, :], qa[c][:].rearrange("p (h f) -> p h f", f=D), AX.X))
                        after(last[c])
                        v.tensor_scalar(qsum[c][:, t, :], qsum[c][:, t, :], D * 1.1920929e-07, None,
                                        ALU.add).then_inc(q_var, 1)

                    rope_q(0, 0)
                    for c in CH:
                        rooted("L1_k", c)
                        last[c] = done(v.tensor_tensor(kk[c][:, :, 0:D], kk[c][:, :, 0:D], bcast(rstd[c][:, 0:2], D), ALU.mult))
                    for c in CH:
                        after(last[c])
                        for t in TILES:
                            q = v.tensor_tensor(kd[c][:, t], bcast_heads(kk[c][:, t, 0:D], 2),
                                                bcast_heads(qk_norm[:], 2), ALU.mult)
                        q.then_inc(qk_rows, 1)
                    rope_q(0, 1)
                    q_variance(0, 0)
                    rope_q(1, 0)
                    q_variance(0, 1)
                    rope_q(1, 1)
                    for c in CH:
                        q_variance(1, c)
                    attention(STEP["L1"], 8, 2, False, lambda s, c: exs[c][:, :, 2 * s:2 * s + 2],
                              lambda s, c: att[c][:, :, 2 * s * D:2 * (s + 1) * D].rearrange("p t (e d) -> p t e d", e=2))
                    for c in CH:
                        dve.wait_ge(ao_rows, nth(1, c))
                        last[c] = done(v.tensor_tensor(h[c][:], h[c][:], tv(bank(c, 2)[:, 0:P]), ALU.add))
                if LAST_STAGE >= 5:
                    norm_rows("L1_ffn_pre", h)
                    route(4, 32, 1)
                    for c in CH:
                        after(last[c])
                        dve.wait_ge(q_proj, nth(2, c))
                        for t in TILES:
                            v.scalar_tensor_tensor(z1[c][:, t, 0:512].rearrange("p (e f) -> p e f", f=16),
                                                   bank(c, t).rearrange("p (e f) -> p e f", f=16), 0.0,
                                                   bcast(sel[c][:, t, 0:32], 16), ALU.max, ALU.mult)
                        v.tensor_copy(z1[c][:, :, 512:544], sel[c][:, :, 0:32]).then_inc(f1_z, 1)
                    for c in CH:
                        dve.wait_ge(ao_rows, nth(2, c))
                        last[c] = done(v.scalar_tensor_tensor(h[c][:], tv(bank(c, 2)[:, 0:P]), 0.0, h[c][:], ALU.max, ALU.add))
                if LAST_STAGE >= 6:
                    norm_rows("L2_attn_pre", h)
                    for c in CH:
                        dve.wait_ge(q_proj, nth(3, c))
                        x = bank(c, 0)[:, 0:384].rearrange("p (t g f) -> p t g f", t=2, g=3)
                        kq = kk[c][:].rearrange("p t (g f) -> p t g f", g=2)
                        km = kkm[c][:].rearrange("p t (g f) -> p t g f", g=2)
                        done(v.tensor_copy(vv[c][:], x[:, :, 2, :]))
                        done(v.tensor_copy(kq[:, :, :, 0:48], x[:, :, 0:2, 0:48]))
                        done(v.tensor_tensor(kq[:, :, :, 48:64], x[:, :, 0:2, 48:64], bcast_mid(cos2, 2), ALU.mult))
                        done(v.tensor_tensor(km[:, :, :, 0:8], x[:, :, 0:2, 56:64], bcast_mid(sin2[:, :, 0:8], 2), ALU.mult))
                        last[c] = done(v.tensor_tensor(km[:, :, :, 8:16], x[:, :, 0:2, 48:56],
                                                       bcast_mid(sin2[:, :, 8:16], 2), ALU.mult))
                        after(last[c])
                        v.tensor_tensor(kq[:, :, :, 48:64], kq[:, :, :, 48:64], km[:, :, :, 0:16], ALU.add).then_inc(qk_rows, 1)
                    attention(STEP["L2"], 1, 1, False, 0.125, lambda s, c: xc[c][:].unsqueeze(2))
                    add_to_h(STEP["L2"])
                if LAST_STAGE >= 7:
                    CAP = -(-5 * SEQS * T // 4) // 8
                    norm_rows("L2_ffn_pre", h, xd)
                    route(5, 8, 1)
                    shift(8)
                    for c in CH:
                        after(last[c])
                        v.tensor_copy(mb[c][:], sel[c][:, :, 0:8]).then_inc(f2_hot, 1)
                    for c in CH:
                        dve.wait_ge(expd, nth(1, c))
                        last[c] = done(v.reduce_sum(st[c][:, 0, 0:2], prob[c][:, :, 0:8], AX.X))
                        after(last[c])
                        last[c] = done(v.reciprocal(rr[c][:, 0:2], st[c][:, 0, 0:2]))
                    for c in CH:
                        dve.wait_ge(f2_count, c + 1)
                        last[c] = done(v.tensor_tensor(pen[c][:, :, 0:8], tv(bank(c, 2)[:, 32:48]),
                                                       bcast_heads(carry[:], 2), ALU.add))
                        after(last[c])
                        last[c] = done(v.tensor_tensor(carry[:], carry[:], bank(c, 2)[:, 48:56], ALU.add))
                        last[c] = done(v.tensor_tensor(pen[c][:, :, 0:8], pen[c][:, :, 0:8], sel[c][:, :, 0:8], ALU.mult))
                        after(last[c])
                        last[c] = done(v.reduce_sum(keep[c][:], pen[c][:, :, 0:8], AX.X))
                        after(last[c])
                        last[c] = done(v.scalar_tensor_tensor(gate[c][:], keep[c][:], float(CAP) + 0.5, rr[c][:, 0:2],
                                                              ALU.is_lt, ALU.mult))
                    for c in CH:
                        dve.wait_ge(f2_bc, c + 1)
                        x4 = pT[c][:].rearrange("p (a q) -> p a q", a=4)
                        v.tensor_tensor(x4, banks2(c, 0).rearrange("p a (b q) -> p (a b) q", q=T),
                                        bcast_heads(xT2[c][:], 4), ALU.mult).then_inc(f2_xm, 1)
                    for c in CH:
                        dve.wait_ge(f2_y, c + 1)
                        for t in TILES:
                            y3 = bank(c, t).rearrange("p (e d) -> p e d", e=8)
                            s3 = sm[c][:, t]
                            last[c] = done(v.tensor_tensor(s3, y3, bcast(sel[c][:, t, 0:8], D), ALU.mult))
                    for c in CH:
                        after(last[c])
                        for t in TILES:
                            last[c] = done(v.reduce_sum(xc[c][:, t, :], sm[c][:, t].rearrange("p e d -> p d e"), AX.X))
                    for c in CH:
                        after(last[c])
                        last[c] = done(v.tensor_tensor(xc[c][:], xc[c][:], bcast(gate[c][:], D), ALU.mult))
                    for c in CH:
                        after(last[c])
                        done(v.memset(fill[c][:], 0.0))
                        last[c] = done(v.tensor_tensor(bad[c][:], xc[c][:], xc[c][:], ALU.is_equal))
                    for c in CH:
                        after(last[c])
                        last[c] = done(v.copy_predicated(fill[c][:], bad[c][:], xc[c][:]))
                    for value, op, lim in ((1e4, ALU.is_gt, 3.4e38), (-1e4, ALU.is_lt, -3.4e38)):
                        for c in CH:
                            after(last[c])
                            done(v.memset(sq[c][:], value))
                            last[c] = done(v.tensor_scalar(bad[c][:], xc[c][:], lim, None, op))
                        for c in CH:
                            after(last[c])
                            last[c] = done(v.copy_predicated(fill[c][:], bad[c][:], sq[c][:]))
                    for c in CH:
                        after(last[c])
                        last[c] = done(v.tensor_tensor(h[c][:], h[c][:], fill[c][:], ALU.add))
                if LAST_STAGE >= 8:
                    norm_rows("L3_attn_pre", h)
                    attention(STEP["L3"], 1, 1, True, 0.125, lambda s, c: xc[c][:].unsqueeze(2))
                    add_to_h(STEP["L3"])
                if LAST_STAGE >= 9:
                    centre(h)
                    inverse_root("L3_ffn_pre", EPS)
                    for c in CH:
                        rooted("L3_ffn_pre", c)
                        last[c] = done(v.tensor_tensor(x3[c][:], xc[c][:], bcast(rstd[c][:, 0:2], D), ALU.mult))
                    squares(x3)
                    inverse_root("L3_rms1", 1e-6)
                    for c in CH:
                        rooted("L3_rms1", c)
                        v.tensor_tensor(xc[c][:], x3[c][:], bcast(rstd[c][:, 0:2], D), ALU.mult).then_inc(rows_ready, 1)
                    for c in CH:
                        dve.wait_ge(proj_ready, nth(6, c))
                        x = tv(bank(c, 2)[:, 0:256])
                        q6 = x[:, :, 0:96].rearrange("p t (h f) -> p t h f", f=16)
                        k6 = kk[c][:, :, 0:96].rearrange("p t (h f) -> p t h f", f=16)
                        m6 = kkm[c][:, :, 0:96].rearrange("p t (h f) -> p t h f", f=16)
                        done(v.tensor_copy(kk[c][:, :, 96:128], x[:, :, 96:128]))
                        done(v.tensor_tensor(k6, q6, bcast_mid(cos3, 6), ALU.mult))
                        done(v.tensor_tensor(m6[:, :, :, 0:8], q6[:, :, :, 8:16], bcast_mid(sin3[:, :, 0:8], 6), ALU.mult))
                        last[c] = done(v.tensor_tensor(m6[:, :, :, 8:16], q6[:, :, :, 0:8], bcast_mid(sin3[:, :, 8:16], 6), ALU.mult))
                        after(last[c])
                        pad = kd4[c][:].rearrange("p g t (h f) -> p g t h f", f=32)
                        v.tensor_tensor(pad[:, 0, :, :, 0:16], k6[:, :, 0:4, :], m6[:, :, 0:4, :], ALU.add)
                        for r in range(2):
                            q = v.tensor_tensor(pad[:, 1, :, r:4:2, 0:16], k6[:, :, 4:6, :], m6[:, :, 4:6, :], ALU.add)
                        q.then_inc(qk_rows, 1)
                    attention(STEP["L3f"], 2, 2, False, 0.25,
                              lambda s, c: att[c][:, :, 32 * s:32 * s + 32].rearrange("p t (e d) -> p t e d", e=2), 16)
                    for c in CH:
                        dve.wait_ge(at_out, nth(STEP["L3f"] + 1, c))
                        dve.drain().then_inc(rows_ready, 1)
                    for c in CH:
                        dve.wait_ge(proj_ready, nth(7, c))
                        last[c] = done(v.tensor_tensor(x3[c][:], x3[c][:], tv(bank(c, 2)[:, 0:P]), ALU.add))
                    squares(x3)
                    inverse_root("L3_rms2", 1e-6)
                    for c in CH:
                        rooted("L3_rms2", c)
                        v.tensor_tensor(xc[c][:], x3[c][:], bcast(rstd[c][:, 0:2], D), ALU.mult).then_inc(rows_ready, 1)
                    route(8, 8, 2)
                    shift(8)
                    for c in CH:
                        dve.wait_ge(expd, nth(2, c))
                        last[c] = done(v.reduce_sum(st[c][:, 0, 0:2], prob[c][:, :, 0:8], AX.X))
                        after(last[c])
                        last[c] = done(v.reciprocal(rr[c][:, 0:2], st[c][:, 0, 0:2]))
                        last[c] = done(v.tensor_tensor(prob[c][:, :, 0:8], prob[c][:, :, 0:8], sel[c][:, :, 0:8], ALU.mult))
                        after(last[c])
                        last[c] = done(v.tensor_tensor(prob[c][:, :, 0:8], prob[c][:, :, 0:8], bcast(rr[c][:, 0:2], 8), ALU.mult))
                        after(last[c])
                        last[c] = done(v.reduce_sum(st[c][:, 0, 0:2], prob[c][:, :, 0:8], AX.X))
                        after(last[c])
                        last[c] = done(v.tensor_scalar(st[c][:, 1, 0:2], st[c][:, 0, 0:2], 2.0, 2e-9, ALU.mult, ALU.add))
                        after(last[c])
                        last[c] = done(v.reciprocal(rr[c][:, 2:4], st[c][:, 1, 0:2]))
                        after(last[c])
                        last[c] = done(v.tensor_tensor(prob[c][:, :, 0:8], prob[c][:, :, 0:8], bcast(rr[c][:, 2:4], 8), ALU.mult))
                        done(v.tensor_tensor(h[c][:], h[c][:], x3[c][:], ALU.add))
                    for c in CH:
                        after(last[c])
                    for x in range(16):
                        t, e = x // 8, x % 8
                        for c in CH:
                            dve.wait_ge(f4_tanh, nth(x, c))
                            last[c] = done(v.scalar_tensor_tensor(th[c][:, x % 3, :], th[c][:, x % 3, :], 1.0,
                                                                  bank(c, MOE_BANK[x % 3])[:, 0:HIDDEN3], ALU.add, ALU.mult))
                        for c in CH:
                            after(last[c])
                            v.scalar_tensor_tensor(hid[t][c][:, e * HIDDEN3:(e + 1) * HIDDEN3],
                                                   bank(c, MOE_BANK[x % 3])[:, HIDDEN3:2 * HIDDEN3],
                                                   prob[c][:, t, e:e + 1], th[c][:, x % 3, :], ALU.mult, ALU.mult).then_inc(f4_h, 1)
                    for c in CH:
                        dve.wait_ge(ao_rows, nth(4, c))
                        last[c] = done(v.tensor_tensor(h[c][:], h[c][:], tv(bank(c, 2)[:, 0:P]), ALU.add))
                for c in CH:
                    after(last[c])
                    v.tensor_copy(h_all[:, bass.ds(i * 4 + 2 * c, 2), :], h[c][:])
                close_pass(dve, i)


def layout(x):
    f = np.float32

    def rows(a, b):
        return np.concatenate([a, b.reshape(1, -1)], 0)

    half_split = np.concatenate([np.arange(0, 64, 2), np.arange(1, 64, 2)])
    rope16 = np.concatenate([np.arange(0, 16, 2), np.arange(1, 16, 2)])
    i, j = np.arange(P)[:, None], np.arange(P)[None, :]

    def rope(freqs, signed):
        ang = (np.arange(T, dtype=f)[:, None] * freqs[None, :].astype(f)).astype(f)
        s, c = np.sin(ang).astype(f), np.cos(ang).astype(f)
        both = lambda a, b: np.concatenate([a, b], 1).reshape(2, P, -1).transpose(1, 0, 2).reshape(P, -1)
        return both(c, c), both(-s, s)

    cos1, sin1 = rope(np.power(f(10000.0), (-2.0 * np.arange(32, dtype=f) / 64).astype(f)), True)
    cos2, sin2 = rope((f(1.0) / np.power(f(10000.0), np.arange(8, dtype=f) / f(8))).astype(f), True)
    cos3, sin3 = rope((1.0 / 10000.0 ** (np.arange(0, 16, 2, dtype=f) / 16)).astype(f), True)
    sel8 = np.zeros((8, 4, P), f)
    for p in range(4):
        sel8[2 * p, p, 0:64] = 1
        sel8[2 * p + 1, p, 64:128] = 1
    wq = x["L1_attn_wq"].reshape(16, 64, 64)[:, half_split].reshape(1024, 64)
    wk, wv = x["L1_attn_wkv"][0:64][half_split], x["L1_attn_wkv"][64:128]
    w2 = x["L3_ffn_w2"].transpose(0, 2, 1).reshape(8 * HIDDEN3, D)
    pieces = {
        "ident": ("early128", np.eye(P, dtype=f)),
        "causal": ("early128", np.where(j <= i, 0, NEG).astype(f)),
        "window": ("early128", np.where(j >= i, 0, NEG).astype(f)),
        "tri": ("early128", (i <= j).astype(f)),
        "cos_l1": ("early128", cos1), "sin_l1": ("early128", sin1),
        "cos_l2": ("early128", cos2), "sin_l2": ("early128", sin2),
        "cos_l3": ("early128", cos3), "sin_l3": ("early128", sin3),
        "iota_col": ("early128", np.arange(P, dtype=f).reshape(P, 1)),
        "WdT": ("early128", x["L0_tok_Wd"].transpose(3, 0, 1, 2).reshape(P, -1)),
        "WgT": ("early64", x["L0_tok_Wg"].transpose(3, 0, 1, 2).reshape(D, -1)),
        "WuT": ("early64", x["L0_tok_Wu"].transpose(3, 0, 1, 2).reshape(D, -1)),
        "embT": ("early64", x["L0_tok_embed"].T),
        "lmT": ("early64", x["L0_tok_lm_head"].T),
        "L0_Wq": ("early65", rows(x["L0_attn_Wq"], x["L0_attn_bq"])),
        "L0_Wk": ("early65", rows(x["L0_attn_Wk"], x["L0_attn_bk"])),
        "L0_Wv": ("early65", rows(x["L0_attn_Wv"], x["L0_attn_bv"])),
        "L0_Wo": ("early65", rows(x["L0_attn_Wo"], x["L0_attn_bo"])),
        "L0_out": ("early65", rows(x["L0_ffn_out_w"].T, x["L0_ffn_out_b"])),
        "sel8": ("late8", sel8.reshape(8, -1)),
        "L0_gate": ("late64", x["L0_ffn_gate_w"].T),
        "L1_wq": ("late64", wq.T),
        "L1_wkv": ("late64", np.concatenate([wk, wv], 0).T),
        "L2_Wqcomp": ("late64", x["L2_attn_Wq_comp"]), "L2_Wkvcomp": ("late64", x["L2_attn_Wkv_comp"]),
        "L2_Wq": ("late64", np.concatenate([x["L2_attn_Wqc"], x["L2_attn_Wqr"][:, rope16]], 1)),
        "L2_Wkv": ("late64", np.concatenate([x["L2_attn_Wkc"], x["L2_attn_Wkr"][:, rope16], x["L2_attn_Wv"]], 1)),
        "L2_gate": ("late64", x["L2_ffn_gate_w"]),
        "ln1": ("late64", x["L3_ffn_ln1_w"].reshape(D, 1)), "ln2": ("late64", x["L3_ffn_ln2_w"].reshape(D, 1)),
        "L3_wqkv": ("late64", np.concatenate([x["L3_ffn_wq"], x["L3_ffn_wk"], x["L3_ffn_wv"]], 0).T),
        "L3_wo": ("late64", x["L3_ffn_wo"].T),
        "L3_router": ("late64", x["L3_ffn_router_w"].T),
        "L3_w13": ("late64", np.concatenate([x["L3_ffn_w1"], x["L3_ffn_w3"]], 1).transpose(2, 0, 1).reshape(D, -1)),
        "L1_router": ("late65", rows(x["L1_ffn_router_w"].T, x["L1_ffn_router_b"])),
        "L1_W1": ("late65", rows(x["L1_ffn_W1"].transpose(1, 0, 2).reshape(D, 512), x["L1_ffn_b1"])),
        "L3_Wq": ("late65", rows(x["L3_attn_Wq"], x["L3_attn_bq"])),
        "L3_Wk": ("late65", rows(x["L3_attn_Wk"], x["L3_attn_bk"])),
        "L3_Wv": ("late65", rows(x["L3_attn_Wv"], x["L3_attn_bv"])),
        "L1_b2": ("late32", x["L1_ffn_b2"]),
        "L2_b1": ("late8", x["L2_ffn_b1"]),
        "L2_gateb": ("late1", x["L2_ffn_gate_b"].reshape(1, 8)),
        "L2_b2": ("late1", x["L2_ffn_b2"].reshape(1, 512)),
        "lattice": ("late128", x["L0_ffn_lattice_weights"].reshape(32, P, D).transpose(1, 0, 2).reshape(P, -1)),
        "L1_wo": ("late128", x["L1_attn_wo"].T.reshape(8, P, D).transpose(1, 0, 2).reshape(P, -1)),
        "L1_W2": ("late128", x["L1_ffn_W2"].reshape(4, P, D).transpose(1, 0, 2).reshape(P, -1)),
        "L2_W1": ("late128", x["L2_ffn_w1"].reshape(4, P, 256).transpose(1, 0, 2).reshape(P, -1)),
        "L2_W2": ("late128", x["L2_ffn_w2"].reshape(8, 2, P, D).transpose(2, 1, 0, 3).reshape(P, -1)),
        "L3_w2": ("late128", w2[0:1280].reshape(10, P, D).transpose(1, 0, 2).reshape(P, -1)),
        "L3_w2t": ("late80", w2[1280:]),
    }
    packs, place = {}, {}
    for name, (pack, a) in pieces.items():
        at = sum(b.shape[1] for b in packs.get(pack, []))
        place[name] = (pack, at, a.shape[1], a.shape[0])
        packs.setdefault(pack, []).append(a)
    arrays = {k: np.ascontiguousarray(np.concatenate(b, 1)) for k, b in packs.items()}
    return arrays, place


def kernel(**inputs):
    import numpy as _np
    import concourse.bacc as _bacc
    from concourse import mybir as _mybir
    from concourse.bass_utils import run_bass_kernel_spmd as _run

    x = {k: _np.ascontiguousarray(a) for k, a in inputs.items()}
    arrays, place = layout(x)
    cols = {"packs": {k: a.shape for k, a in arrays.items()}, "pieces": place}
    ids = x["x"].reshape(-1)
    arrays["ids"] = ids
    arrays["ids_tok"] = _np.ascontiguousarray(ids.reshape(2 * SEQS, P).T)
    arrays["edges"] = _np.ascontiguousarray(x["L0_attn_edge_index"].reshape(2, P, P).transpose(1, 0, 2))
    arrays["vecs"] = _np.stack([x["L0_attn_gamma"], x["L0_attn_beta"], x["L0_ffn_ln_g"], x["L0_ffn_ln_b"],
                                _np.concatenate([x["L1_attn_q_norm_w"][0::2], x["L1_attn_q_norm_w"][1::2]]),
                                _np.concatenate([x["L1_attn_k_norm_w"][0::2], x["L1_attn_k_norm_w"][1::2]])])
    nc = _bacc.Bacc("TRN2", target_bir_lowering=False, num_devices=1)
    dram = {k: nc.dram_tensor("in_" + k, a.shape, _mybir.dt.from_np(a.dtype), kind="ExternalInput").ap()
            for k, a in arrays.items()}
    out = nc.dram_tensor("tower_out", (SEQS * T, D), F32, kind="ExternalOutput").ap()
    build(nc, dram, out, cols)
    r = _run(nc, [{"in_" + k: a for k, a in arrays.items()}], core_ids=[0])
    return r.results[0]["tower_out"].reshape(SEQS, T, D)
```

```python
from contextlib import ExitStack

import numpy as np

import concourse.bass as bass
from concourse import mybir

F32 = mybir.dt.float32
BF16 = mybir.dt.bfloat16
I32 = mybir.dt.int32
ALU = mybir.AluOpType
ACT = mybir.ActivationFunctionType
AX = mybir.AxisListType

P = 128
D = 64
SEQS, T = 8, 256
CH = (0, 1)
TILES = (0, 1)
PASSES = SEQS // 2
NEG = -1e30
BIG = 3e38
EPS = 1e-5
HIDDEN3 = 170

TURN = {n: i for i, n in enumerate([
    "L0_attn_out", "L0_ffn_in", "L1_attn_in", "L1_ffn_in", "L2_attn_in", "L2_ffn_in",
    "L3_attn_in", "L3_qkv_in", "L3_attn_out", "L3_moe_in"])}
NORM = {n: i for i, n in enumerate([
    "L0_attn_post", "L0_ffn_pre", "L0_ffn_post", "L1_attn_pre", "L1_k", "L1_ffn_pre",
    "L2_attn_pre", "L2_ffn_pre", "L3_attn_pre", "L3_ffn_pre", "L3_rms1", "L3_rms2"])}
STEP = {"L1": 0, "L2": 8, "L3": 9, "L3f": 10}
PADDED = ("late64", "late65")
MOE_BANK = (0, 1, 3)


def build(nc, dram, out, cols):
    with ExitStack() as ctx:
        def sb(name, shape, dt=F32):
            return ctx.enter_context(nc.sbuf_tensor(name, shape, dt))

        def sb2(name, shape, dt=F32):
            return [sb(f"{name}{c}", shape, dt) for c in CH]

        def sem(name):
            return ctx.enter_context(nc.semaphore(name))

        packs, padded = {}, {}
        for name, (arr, width) in cols["packs"].items():
            whole = sb("pack_" + name, [P if name in PADDED + ("early64",) else arr, width])
            packs[name] = whole[0:arr, :]
            padded[name] = whole
            if name == "early64":
                h_all = whole[:, 0:2 * SEQS * D].rearrange("p (t d) -> p t d", d=D)

        def w(name, rows=None):
            pack, at, width, r = cols["pieces"][name]
            return packs[pack][0:(rows or r), at:at + width]

        def wide(name):
            pack, at, width, r = cols["pieces"][name]
            return padded[pack][:, at:at + width]

        ident = w("ident")
        w_pair = packs["early128"][:, cols["pieces"]["window"][1]:cols["pieces"]["window"][1] + 2 * P]
        cosq = w("cos_l1").rearrange("p (t f) -> p t f", t=2)
        sinq = w("sin_l1").rearrange("p (t f) -> p t f", t=2)
        cos2 = w("cos_l2").rearrange("p (t f) -> p t f", t=2)
        sin2 = w("sin_l2").rearrange("p (t f) -> p t f", t=2)
        cos3 = w("cos_l3").rearrange("p (t f) -> p t f", t=2)
        sin3 = w("sin_l3").rearrange("p (t f) -> p t f", t=2)
        vecs = sb("vecs", [P, 7, D])
        qk_norm = sb("qk_norm", [P, D])
        ident_b = sb("ident_b", [P, P], BF16)
        maskb = sb("maskb", [P, P], BF16)
        tri_b = sb("tri_b", [P, P], BF16)
        ones_b = sb("ones_b", [P, P], BF16)
        sel_b = sb("sel_b", [8, 4, P], BF16)
        half = sb("half", [P, 1])
        ids_bc = sb("ids_bc", [D, SEQS * T])
        ids_tok_i = sb("ids_tok_i", [P, 2 * SEQS], I32)
        ids_tok = sb("ids_tok", [P, 2 * SEQS])
        edges = sb("edges", [P, 2, P])
        iota_b = sb("iota_b", [P, T], BF16)
        diag_b = sb("diag_b", [P, 2, T], BF16)
        allow = sb("allow", [P, 2, T], BF16)

        tabT = sb("tabT", [D, D])
        tab_t = sb("tab_t", [P, 4, D])
        tab_a = sb("tab_a", [P, 4, D])
        tab_z = sb("tab_z", [P, 4, D])
        tabs = sb("tabs", [D, 2, D])
        tab_s = sb("tab_s", [D, 4])
        tab_q = sb("tab_q", [D, D])
        xtabT = sb("xtabT", [D + 1, 2, D])
        qtab = sb("qtab", [8, 8, D])
        ktab = sb("ktab", [8, 8, D])
        score_tab = sb("score_tab", [P, 8, D])
        vblk = sb("vblk", [P, 4, 2, 9])
        ln1w = w("ln1")
        ln2w = w("ln2")

        h = sb2("h", [P, 2, D])
        xn = sb2("xn", [P, 2, D])
        xd = sb2("xd", [P, 2, 2, D])
        xc = sb2("xc", [P, 2, D])
        sq = sb2("sq", [P, 2, D])
        st = sb2("st", [P, 3, 16])
        parts = sb2("parts", [P, 2, 6])
        mv = sb2("mv", [P, 2, 2])
        qsum = sb2("qsum", [P, 2, 16])
        rstd = sb2("rstd", [P, 16])
        xT = sb2("xT", [P, T])
        xT2 = sb2("xT2", [P, T])
        hotT = sb2("hotT", [P, T])
        hot = sb2("hot", [P, 2, D], BF16)
        penT = sb2("penT", [D, T], BF16)
        pen = sb2("pen", [P, 2, D])
        sm = sb2("sm", [P, 2, 8, D])
        pT = sb2("pT", [P, 1024])
        lg = sb2("lg", [P, 2, 72])
        top = sb2("top", [P, 2, 8])
        pick = {k: sb2(f"pick{k}_", [P, 2, 8]) for k in (1, 2, 6)}
        rep = sb2("rep", [P, 2, 72])
        sel = sb2("sel", [P, 2, D])
        prob = sb2("prob", [P, 2, D])
        zb = [sb2(f"zb{j}", [P, 8, D]) for j in range(2)]
        zT = [sb2(f"zT{j}", [P, 512]) for j in range(2)]
        att = sb2("att", [P, 2, 1024])
        qT = sb2("qT", [P, 8, T])
        kk = sb2("kk", [P, 2, P])
        kkm = sb2("kkm", [P, 2, P])
        vv = sb2("vv", [P, 2, D])
        kd = sb2("kd", [P, 2, 2, D])
        kT = sb2("kT", [P, 2, T])
        exs = sb2("exs", [P, 2, 16])
        mx = sb2("mx", [P, 4])
        nb = sb2("nb", [P, 4])
        rs = sb2("rs", [P, 2, 4])
        rr = sb2("rr", [P, 16])
        pr = sb2("pr", [P, 768])
        prT = sb2("prT", [P, 768])
        mT = sb2("mT", [32, T])
        mTb = sb2("mTb", [8, T], BF16)
        mb = sb2("mb", [P, 2, 8], BF16)
        carry = sb("carry", [P, 8])
        gate = sb2("gate", [P, 2])
        keep = sb2("keep", [P, 2])
        fill = sb2("fill", [P, 2, D])
        bad = sb2("bad", [P, 2, D], I32)
        finite = sb2("finite", [P, 2, D], I32)
        zero = sb("zero", [P, 1])
        kd4 = sb2("kd4", [P, 2, 2, P])
        x3 = sb2("x3", [P, 2, D])

        ids_bc_i = att[0][0:D].rearrange("p a b -> p (a b)").bitcast(I32)
        edges_i = att[1][:, 0, 0:2 * P].bitcast(I32).rearrange("p (a b) -> p a b", a=2)
        hot_src, hot_dst = [qT[c][:].rearrange("p a b -> p (a b)").bitcast(BF16)
                            .rearrange("p (s u n) -> p s u n", s=2, u=8) for c in CH]
        qa = pT
        qb = [sm[c][:].rearrange("p t h v -> p (t h v)")[:, 0:1024] for c in CH]
        z1 = [att[c][:, :, 0:544] for c in CH]
        masked_s = [[zb[0][c][:].rearrange("p a b -> p (a b)")[:, 0:2 * P].rearrange("p (e x) -> p e x", e=2),
                     zb[1][c][:].rearrange("p a b -> p (a b)").rearrange("p (e x) -> p e x", e=2)] for c in CH]
        kz = [qT[c][:, 0:4, :] for c in CH]
        th = [sm[c][:].rearrange("p t h v -> p (t h v)")[:, 0:3 * HIDDEN3].rearrange("p (b f) -> p b f", b=3) for c in CH]
        hid = [[b[c][:].rearrange("p a b -> p (a b)")[:, 0:8 * HIDDEN3] for c in CH] for b in (att, qT)]

        ps = ctx.enter_context(nc.psum_tensor("ps", [P, 8, 512], F32))

        def bank(c, j):
            return ps[:, 4 * c + j, :]

        def banks2(c, j):
            return ps[:, 4 * c + j:4 * c + j + 2, :]

        early = sem("early_loaded")
        late = sem("late_loaded")
        vset = sem("vector_setup_step")
        padding = sem("padding_zeroed")
        iset = sem("iota_ready")
        edge_hot = sem("edge_hot_ready")
        edge_used = sem("edge_hot_used")
        edge_total = sem("edge_counts_ready")
        tabmm = sem("table_product_ready")
        taba = sem("table_tanh_ready")
        tabv = sem("table_vector_ready")
        tabz = sem("table_hidden_ready")
        tabpow = sem("table_rstd_ready")
        consts = sem("constants_ready")
        opened = sem("pass_opened")
        stored = sem("stored")
        ended = sem("pass_ended")
        vstep = sem("vector_step")
        hotT_ready = sem("hotT_ready")
        hot_ready = sem("hot_ready")
        var_ready = sem("variance_ready")
        rstd_ready = sem("rstd_ready")
        rows_ready = sem("rows_ready")
        turned = sem("rows_turned")
        feat_ready = sem("features_ready")
        proj_ready = sem("projection_ready")
        a0_counts, a0_pen, a0_scores, a0_max, a0_exp, a0_probs, a0_probsT_ps, a0_probsT, a0_av = [
            sem("a0_" + n) for n in ("counts", "pen", "scores", "max", "exp", "probs", "probsT_ps", "probsT", "av")]
        shifted = sem("logits_shifted")
        expd = sem("logits_exp")
        z_ready, z_turned, zT_ready, zsum_ready, lattice_out = [
            sem("lattice_" + n) for n in ("z", "turned", "zT", "sum", "out")]
        at_scores, at_bias, at_probs, at_turned, at_probsT, at_av, at_out = [
            sem("at_" + n) for n in ("scores", "bias", "probs", "turned", "probsT", "av", "out")]
        q_proj, q_used, q_sq, q_var, scales_ready, q_roped, q_turned, qT_ready = [
            sem("l1_" + n) for n in ("q_proj", "q_used", "sq", "var", "scales", "roped", "turned", "qT")]
        ao_turned, ao_ready, ao_rows = [sem("l1_out_" + n) for n in ("turned", "ready", "rows")]
        f1_z, f1_turned, f1_zT = [sem("f1_" + n) for n in ("z", "turned", "zT")]
        c2_ready, c2_used = sem("l2_c_ready"), sem("l2_c_used")
        qk_rows, qk_turned, qk_ready = [sem("qk_" + n) for n in ("rows", "turned", "ready")]
        f2_count, f2_maskT, f2_mask, f2_bc, f2_xm, f2_hid, f2_relu, f2_y = [
            sem("f2_" + n) for n in ("count", "maskT_ps", "maskT", "bc", "xm", "hid", "relu", "y")]
        f2_hot = sem("f2_hot")
        kz_zeroed = sem("kz_zeroed")
        f4_gu, f4_tanh, f4_h, f4_turned, f4_hT = [sem("f4_" + n) for n in ("gu", "tanh", "h", "turned", "hT")]
        loop_nums = range(ended.num, f4_hT.num + 1)

        class Steps:
            def __init__(self, eng, s):
                self.eng, self.s, self.n = eng, s, 0

            def done(self, ins):
                ins.then_inc(self.s, 1)
                self.n += 1
                return self.n

            def after(self, n=None):
                self.eng.wait_ge(self.s, n or self.n)

        def nth(n, c):
            return 2 * n + c + 1

        def close_pass(eng, i):
            eng.drain().then_inc(ended, 1)
            eng.wait_ge(opened, i + 1)

        def blocks(full):
            return [(0, 0), (0, 1), (1, 0), (1, 1)] if full else [(0, 0), (1, 0), (1, 1)]

        block = ctx.enter_context(nc.Block())

        @block.sync
        def _(sp):
            sp.dma_start(edges_i, dram["edges"]).then_inc(early, 16)
            sp.dma_start(ids_bc_i, dram["ids"].rearrange("(a n) -> a n", a=1).to_broadcast([D, SEQS * T])
                         ).then_inc(early, 16)
            sp.dma_start(ids_tok_i[:], dram["ids_tok"]).then_inc(early, 16)
            sp.dma_start(vecs[:], dram["vecs"].rearrange("(a v) d -> a v d", a=1).to_broadcast([P, 7, D])
                         ).then_inc(early, 16)
            for name in ("early128", "early64", "early65"):
                sp.dma_start(packs[name], dram[name]).then_inc(early, 16)
            sp.wait_ge(padding, len(PADDED))
            for name in cols["packs"]:
                if not name.startswith("early"):
                    sp.dma_start(packs[name], dram[name]).then_inc(late, 16)
            sp.wait_ge(opened, PASSES)
            sp.dma_start(out.rearrange("(t p) d -> p t d", p=P), h_all).then_inc(stored, 16)
            sp.wait_ge(stored, 16)

        EARLY = 16 * 7
        LATE = 16 * sum(not n.startswith("early") for n in cols["packs"])

        @block.gpsimd
        def _(pool):
            for n, name in enumerate(PADDED):
                nc.gpsimd.memset(padded[name][D:P, :], 0.0).then_inc(padding, 1)
                pool.wait_ge(padding, n + 1)
            nc.gpsimd.iota(iota_b[:], [[1, T]], base=0, channel_multiplier=0,
                           allow_small_or_imprecise_dtypes=True).then_inc(iset, 1)
            nc.gpsimd.memset(half[:], -0.5).then_inc(iset, 1)
            nc.gpsimd.memset(carry[:], 0.0).then_inc(iset, 1)
            nc.gpsimd.memset(zero[:], 0.0).then_inc(iset, 1)
            pool.wait_ge(iset, 4)
            pool.wait_ge(tabv, 1)
            nc.gpsimd.tensor_tensor(tab_s[:, 3:4], tab_s[:, 2:3], half[0:D, :], ALU.pow).then_inc(tabpow, 1)
            with pool.Fori(0, PASSES) as i:
                def rsqrt(n):
                    for c in CH:
                        pool.wait_ge(var_ready, nth(n, c))
                        nc.gpsimd.tensor_tensor(rstd[c][:, 0:2], st[c][:, 2, 0:2],
                                                half[:, 0:1].to_broadcast([P, 2]),
                                                ALU.pow).then_inc(rstd_ready, 1)

                def q_scales(t, c, lo, hi):
                    pool.wait_ge(q_var, nth(t, c))
                    nc.gpsimd.tensor_tensor(exs[c][:, t, lo:hi], qsum[c][:, t, lo:hi],
                                            half[:, 0:1].to_broadcast([P, hi - lo]), ALU.pow).then_inc(scales_ready, 1)

                def add_turned(t, c):
                    pool.wait_ge(q_used, nth(t, c))
                    nc.gpsimd.tensor_tensor(att[c][:, t, :], att[c][:, t, :], qb[c], ALU.add).then_inc(q_roped, 1)

                for n in ("L0_attn_post", "L0_ffn_pre", "L0_ffn_post", "L1_attn_pre", "L1_k", "L1_ffn_pre",
                          "L2_attn_pre", "L2_ffn_pre", "L3_attn_pre", "L3_ffn_pre", "L3_rms1", "L3_rms2"):
                    rsqrt(NORM[n])
                    if n == "L3_attn_pre":
                        for c in CH:
                            pool.wait_ge(f2_y, c + 1)
                            nc.gpsimd.memset(kz[c], 0.0).then_inc(kz_zeroed, 1)
                            pool.wait_ge(kz_zeroed, c + 1)
                    if n == "L1_k":
                        add_turned(0, 0)
                        add_turned(0, 1)
                        q_scales(0, 0, 0, 4)
                        add_turned(1, 0)
                        q_scales(0, 1, 0, 4)
                        for c in CH:
                            q_scales(1, c, 0, 4)
                        for c in CH:
                            for t in TILES:
                                q_scales(t, c, 4, 16)
                pool.wait_ge(ended, 3)
                pool.sem_clear(loop_nums)
                pool.nop().then_inc(opened, 1)

        @block.tensor
        def _(pe):
            def mm(o, l, r, start=True, stop=True, **k):
                return nc.tensor.matmul(o, l, r, start=start, stop=stop, **k)

            def turn(o, i):
                k = i.shape[0]
                return nc.tensor.transpose(o, i, ident[0:k, 0:k])

            pe.wait_ge(consts, 1)
            for j in TILES:
                mm(ps[:, j, 0:T], ident_b[:], diag_b[:, j, :], start=True, stop=False).then_inc(edge_used, 1)

            def edge_counts(lo, hi):
                with pe.Fori(lo, hi) as i:
                    for half_ in range(2):
                        pe.wait_ge(edge_hot, i * 2 + half_ + 1)
                        for u in range(8):
                            for j in TILES:
                                last = mm(ps[:, j, 0:T], hot_dst[:, half_, u, j * P:(j + 1) * P], hot_src[:, half_, u, :],
                                          start=False, stop=False)
                        last.then_inc(edge_used, 1)

            WgT = w("WgT").rearrange("p (l e f) -> p l e f", l=2, e=4)
            WuT = w("WuT").rearrange("p (l e f) -> p l e f", l=2, e=4)
            WdT = w("WdT").rearrange("p (l e d) -> p l e d", l=2, e=4)

            def table_gates(l):
                pe.wait_ge(consts, 2 + l)
                for e in range(4):
                    mm(ps[:, 2, e * D:(e + 1) * D], WgT[:, l, e, :], tabT[:])
                for e in range(4):
                    last = mm(ps[:, 3, e * D:(e + 1) * D], WuT[:, l, e, :], tabT[:])
                last.then_inc(tabmm, 1)

            def table_down(l):
                pe.wait_ge(tabz, l + 1)
                for e in range(4):
                    last = mm(ps[0:D, 4, 0:D], WdT[:, l, e, :], tab_z[:, e, :], start=(e == 0), stop=(e == 3))
                last.then_inc(tabmm, 1)

            table_gates(0)
            edge_counts(0, 2)
            table_down(0)
            table_gates(1)
            edge_counts(2, 4)
            table_down(1)
            pe.wait_ge(consts, 4)
            mm(ps[0:D, 5, 0:D], tabT[:], w("lmT")).then_inc(tabmm, 1)
            edge_counts(4, 6)
            pe.wait_ge(consts, 5)
            turn(ps[0:D, 6, 0:D], tabs[:, 1, :]).then_inc(tabmm, 1)
            pe.wait_ge(consts, 6)
            for hd in range(8):
                mm(ps[0:8, 2, hd * D:(hd + 1) * D], w("L0_Wq")[:, 8 * hd:8 * hd + 8], xtabT[:, 0, :])
                mm(ps[0:8, 3, hd * D:(hd + 1) * D], w("L0_Wk")[:, 8 * hd:8 * hd + 8], xtabT[:, 0, :])
            mm(ps[:, 4, 0:D], xtabT[:].rearrange("p a b -> p (a b)"), w("L0_Wv")).then_inc(tabmm, 1)
            edge_counts(6, 8)
            for j in TILES:
                last = mm(ps[:, j, 0:T], ident_b[:], diag_b[:, j, :], start=False, stop=True)
            last.then_inc(edge_total, 1)
            pe.wait_ge(consts, 7)
            for hd in range(8):
                last = mm(ps[0:D, 5, hd * D:(hd + 1) * D], qtab[:, hd, :], ktab[:, hd, :])
            last.then_inc(tabmm, 1)
            pe.wait_ge(consts, 8)
            pe.wait_ge(late, LATE)

            def features(name, src, width=D):
                n = TURN[name]
                for c in CH:
                    pe.wait_ge(rows_ready, nth(n, c))
                    for t in TILES:
                        last = turn(bank(c, 3)[0:width, t * P:(t + 1) * P], src[c][:, t, 0:width])
                    last.then_inc(turned, 1)

            def project(n, lhs, weight, at=2, ready=feat_ready):
                width = weight.shape[1]
                for c in CH:
                    pe.wait_ge(ready, nth(n, c))
                    for t in TILES:
                        last = mm(bank(c, at)[:, t * width:(t + 1) * width], lhs[c][0:weight.shape[0], t * P:(t + 1) * P], weight)
                    last.then_inc(proj_ready, 1)

            def attention(first, count, operands, ordinal, q, k, v, heads, full, mask, dv):
                bl = blocks(full)

                def scores(s, c):
                    for e in range(heads):
                        for t in TILES:
                            at, wd = (0 if t == 0 else (T if full else P)), (T if full or t == 1 else P)
                            last = mm(bank(c, e)[:, at:at + wd], q(s, c, e, t), k(s, c, e)[:, 0:wd],
                                      start=True, stop=(mask is None))
                            if mask is not None:
                                b0, m = mask[t]
                                last = mm(bank(c, e)[:, at + b0 * P:at + b0 * P + m.shape[1]], ident_b[:], m,
                                          start=False, stop=True)
                    last.then_inc(at_scores, 1)

                def values(s, c):
                    pe.wait_ge(at_probsT, nth(first + s, c))
                    for e in range(heads):
                        for t in TILES:
                            mine = [(b, kt_) for b, (qt_, kt_) in enumerate(bl) if qt_ == t]
                            for z, (b, kt_) in enumerate(mine):
                                x = e * len(bl) + b
                                o = 256 + (e * 2 + t) * dv
                                last = mm(bank(c, 3)[:, o:o + dv], prT[c][:, x * P:(x + 1) * P], v(s, c, e, kt_),
                                          start=(z == 0), stop=(z == len(mine) - 1))
                    last.then_inc(at_av, 1)

                for c in CH:
                    pe.wait_ge(operands, nth(ordinal, c))
                    scores(0, c)
                for u in range(2 * count):
                    s, c = u // 2, u % 2
                    early_scores = first == STEP["L1"]
                    if early_scores and s + 1 < count:
                        pe.wait_ge(at_bias, nth(first + s, c))
                        scores(s + 1, c)
                    pe.wait_ge(at_probs, nth(first + s, c))
                    for x in range(heads * len(bl)):
                        if x == 4 or x + 1 == heads * len(bl) < 5:
                            if s + 1 < count and not early_scores:
                                scores(s + 1, c)
                            if s > 0:
                                pe.wait_ge(at_out, nth(first + s - 1, c))
                        last = turn(ps[:, 4 * c + 2 + x // 4, (x % 4) * P:(x % 4 + 1) * P],
                                    pr[c][:, x * P:(x + 1) * P])
                    last.then_inc(at_turned, 1)
                    if u > 0:
                        values((u - 1) // 2, (u - 1) % 2)
                values(count - 1, 1)

            causal = {0: (0, maskb[:]), 1: (1, maskb[:])}

            with pe.Fori(0, PASSES) as i:
                for c in CH:
                    pe.wait_ge(hotT_ready, c + 1)
                    pe.wait_ge(hot_ready, c + 1)
                    for j in TILES:
                        last = mm(bank(c, 3)[0:D, P:P + T], hot[c][:, j, :], allow[:, j, :], start=(j == 0), stop=(j == 1))
                    last.then_inc(a0_counts, 1)
                    for t in TILES:
                        mm(bank(c, t), hotT[c][:, t * P:(t + 1) * P], score_tab[:].rearrange("p a b -> p (a b)"),
                           start=True, stop=False)
                    for t in TILES:
                        mm(bank(c, 2)[:, t * P:(t + 1) * P], hotT[c][0:D, t * P:(t + 1) * P],
                           tabs[:].rearrange("p a b -> p (a b)"))
                    pe.wait_ge(a0_pen, c + 1)
                    for t in TILES:
                        for j in TILES:
                            mm(bank(c, 3)[:, t * D:(t + 1) * D], allow[:, j, t * P:(t + 1) * P], hot[c][:, j, :],
                               start=(j == 0), stop=(j == 1))
                    for t in TILES:
                        last = mm(bank(c, t).rearrange("p (h v) -> p h v", h=8), penT[c][:, t * P:(t + 1) * P],
                                  ident_b[0:D, 0:D].unsqueeze(1).to_broadcast([D, 8, D]), start=False, stop=True)
                    last.then_inc(a0_scores, 1)
                for c in CH:
                    pe.wait_ge(a0_probs, c + 1)
                    for t in TILES:
                        for hp in range(4):
                            last = turn(bank(c, t)[:, hp * P:(hp + 1) * P],
                                        sm[c][:, t, 2 * hp:2 * hp + 2, :].rearrange("p a b -> p (a b)"))
                    last.then_inc(a0_probsT_ps, 1)
                for c in CH:
                    pe.wait_ge(a0_probsT, c + 1)
                    for t in TILES:
                        for hp in range(4):
                            o = t * 72 + hp * 18
                            last = mm(bank(c, 2)[:, o:o + 18], pT[c][:, t * 512 + hp * P:t * 512 + (hp + 1) * P],
                                      vblk[:, hp, :, :].rearrange("p a b -> p (a b)"))
                    last.then_inc(a0_av, 1)
                features("L0_attn_out", [att[c][:, :, 0:D] for c in CH])
                project(TURN["L0_attn_out"], xT, w("L0_Wo"))
                features("L0_ffn_in", xn)
                project(TURN["L0_ffn_in"], xT, wide("L0_gate"))
                lat = w("lattice").rearrange("p (e o) -> p e o", o=D)
                for x in range(17):
                    if x < 16:
                        for c in CH:
                            pe.wait_ge(z_ready, nth(x, c))
                            if x >= 2:
                                pe.wait_ge(zT_ready, nth(x - 2, c))
                            for q in range(4):
                                last = turn(bank(c, x % 2)[:, q * P:(q + 1) * P],
                                            zb[x % 2][c][:, 2 * q:2 * q + 2, :].rearrange("p a b -> p (a b)"))
                            last.then_inc(z_turned, 1)
                    if x >= 1:
                        y = x - 1
                        t, k8 = y // 8, y % 8
                        for c in CH:
                            pe.wait_ge(zT_ready, nth(y, c))
                            for q in range(4):
                                last = mm(bank(c, 2)[0:D, t * P:(t + 1) * P], lat[:, k8 * 4 + q, :],
                                          zT[y % 2][c][:, q * P:(q + 1) * P],
                                          start=(k8 == 0 and q == 0), stop=(k8 == 7 and q == 3))
                            last.then_inc(zsum_ready, 1)
                project(0, xT, w("L0_out"), ready=lattice_out)
                features("L1_attn_in", xn)
                n = TURN["L1_attn_in"]
                project(n, xT, wide("L1_wkv"))
                for c in CH:
                    for hf in range(2):
                        last = mm(bank(c, hf), xT[c][:, 0:P], wide("L1_wq")[:, hf * 512:(hf + 1) * 512])
                    last.then_inc(q_proj, 1)

                def second_tile(c):
                    pe.wait_ge(q_used, c + 1)
                    for hf in range(2):
                        last = mm(bank(c, hf), xT[c][:, P:T], wide("L1_wq")[:, hf * 512:(hf + 1) * 512])
                    last.then_inc(q_proj, 1)

                def turn_q(t, c):
                    pe.wait_ge(q_roped, nth(t, c))
                    if t == 0:
                        pe.wait_ge(qk_ready, nth(0, c))
                    else:
                        pe.wait_ge(qT_ready, nth(0, c))
                    for hp in range(8):
                        last = turn(ps[:, 4 * c + 2 + hp // 4, (hp % 4) * P:(hp % 4 + 1) * P],
                                    att[c][:, t, hp * P:(hp + 1) * P])
                    last.then_inc(q_turned, 1)

                second_tile(0)
                for c in CH:
                    pe.wait_ge(qk_rows, nth(0, c))
                    for t in TILES:
                        last = turn(bank(c, 3)[:, t * P:(t + 1) * P], kd[c][:, t].rearrange("p a b -> p (a b)"))
                    last.then_inc(qk_turned, 1)
                turn_q(0, 0)
                second_tile(1)
                turn_q(0, 1)
                for c in CH:
                    turn_q(1, c)
                attention(STEP["L1"], 8, qT_ready, 1,
                          lambda s, c, e, t: qT[c][:, s, t * P:(t + 1) * P],
                          lambda s, c, e: kT[c][:, e, :],
                          lambda s, c, e, kt_: vv[c][:, kt_, :], 2, False, None, D)
                for t in TILES:
                    for c in CH:
                        pe.wait_ge(at_out, nth(STEP["L1"] + 7, c))
                        if t == 1:
                            pe.wait_ge(ao_ready, nth(0, c))
                        for hp in range(8):
                            last = turn(ps[:, 4 * c + hp // 4, (hp % 4) * P:(hp % 4 + 1) * P],
                                        att[c][:, t, hp * P:(hp + 1) * P])
                        last.then_inc(ao_turned, 1)
                for t in TILES:
                    for c in CH:
                        pe.wait_ge(ao_ready, nth(t, c))
                        for hp in range(8):
                            last = mm(bank(c, 2)[:, t * D:(t + 1) * D], qT[c][:, hp, t * P:(t + 1) * P],
                                      w("L1_wo")[:, hp * D:(hp + 1) * D], start=(hp == 0), stop=(hp == 7))
                        last.then_inc(ao_rows, 1)
                features("L1_ffn_in", xn)
                project(TURN["L1_ffn_in"], xT, wide("L1_router"))
                for c in CH:
                    for t in TILES:
                        last = mm(bank(c, t), xT[c][:, t * P:(t + 1) * P], wide("L1_W1"))
                    last.then_inc(q_proj, 1)
                for c in CH:
                    pe.wait_ge(f1_z, c + 1)
                    for t in TILES:
                        for k4 in range(4):
                            turn(bank(c, t)[:, k4 * P:(k4 + 1) * P], z1[c][:, t, k4 * P:(k4 + 1) * P])
                        last = turn(bank(c, 3)[0:32, t * P:(t + 1) * P], z1[c][:, t, 512:544])
                    last.then_inc(f1_turned, 1)
                for c in CH:
                    pe.wait_ge(f1_zT, c + 1)
                    for t in TILES:
                        for k4 in range(4):
                            mm(bank(c, 2)[:, t * D:(t + 1) * D], pT[c][:, t * 512 + k4 * P:t * 512 + (k4 + 1) * P],
                               w("L1_W2")[:, k4 * D:(k4 + 1) * D], start=(k4 == 0), stop=False)
                        last = mm(bank(c, 2)[:, t * D:(t + 1) * D], mT[c][:, t * P:(t + 1) * P], w("L1_b2"),
                                  start=False, stop=True)
                    last.then_inc(ao_rows, 1)
                features("L2_attn_in", xn)
                for c in CH:
                    pe.wait_ge(feat_ready, nth(TURN["L2_attn_in"], c))
                    mm(bank(c, 2)[0:D, 0:T], wide("L2_Wqcomp"), xT[c][:])
                    mm(bank(c, 2)[0:D, T:2 * T], wide("L2_Wkvcomp"), xT[c][:]).then_inc(c2_ready, 1)
                for c in CH:
                    pe.wait_ge(c2_used, c + 1)
                    for t in TILES:
                        mm(bank(c, 0)[:, t * 192:t * 192 + D], pT[c][0:D, t * P:(t + 1) * P], w("L2_Wq"))
                        last = mm(bank(c, 0)[:, t * 192 + D:(t + 1) * 192], pT[c][0:D, T + t * P:T + (t + 1) * P],
                                  w("L2_Wkv"))
                    last.then_inc(q_proj, 1)
                for c in CH:
                    pe.wait_ge(qk_rows, nth(1, c))
                    for g in range(2):
                        for t in TILES:
                            last = turn(bank(c, 3)[0:D, g * T + t * P:g * T + (t + 1) * P], kk[c][:, t, g * D:(g + 1) * D])
                    last.then_inc(qk_turned, 1)
                attention(STEP["L2"], 1, qk_ready, 1, lambda s, c, e, t: pT[c][0:D, t * P:(t + 1) * P],
                          lambda s, c, e: pT[c][0:D, T:2 * T], lambda s, c, e, kt_: vv[c][:, kt_, :],
                          1, False, causal, D)
                features("L2_ffn_in", [xd[c][:].rearrange("p t a d -> p t (a d)") for c in CH], P)
                for c in CH:
                    pe.wait_ge(feat_ready, nth(TURN["L2_ffn_in"], c))
                    for t in TILES:
                        last = mm(bank(c, 2)[:, t * 8:(t + 1) * 8], xT2[c][0:D, t * P:(t + 1) * P], w("L2_gate"))
                    last.then_inc(proj_ready, 1)
                for c in CH:
                    pe.wait_ge(f2_hot, c + 1)
                    mm(bank(c, 2)[:, 32:40], tri_b[:], mb[c][:, 0, :])
                    mm(bank(c, 2)[:, 40:48], ones_b[:], mb[c][:, 0, :], start=True, stop=False)
                    mm(bank(c, 2)[:, 40:48], tri_b[:], mb[c][:, 1, :], start=False, stop=True)
                    mm(bank(c, 2)[:, 48:56], ones_b[:], mb[c][:, 0, :], start=True, stop=False)
                    mm(bank(c, 2)[:, 48:56], ones_b[:], mb[c][:, 1, :], start=False, stop=True).then_inc(f2_count, 1)
                    for t in TILES:
                        last = turn(bank(c, 3)[0:8, t * P:(t + 1) * P], sel[c][:, t, 0:8])
                    last.then_inc(f2_maskT, 1)
                for c in CH:
                    pe.wait_ge(f2_mask, c + 1)
                    for pr_ in range(4):
                        last = mm(ps[:, 4 * c + pr_ // 2, (pr_ % 2) * T:(pr_ % 2 + 1) * T], sel_b[:, pr_, :], mTb[c][:])
                    last.then_inc(f2_bc, 1)
                for c in CH:
                    pe.wait_ge(f2_xm, c + 1)
                    for m in range(2):
                        o = bank(c, 2)[:, m * T:(m + 1) * T]
                        for pr_ in range(4):
                            mm(o, w("L2_W1")[:, pr_ * 256 + m * P:pr_ * 256 + (m + 1) * P],
                               pT[c][:, pr_ * T:(pr_ + 1) * T], start=(pr_ == 0), stop=False)
                        last = mm(o, w("L2_b1")[:, m * P:(m + 1) * P], mT[c][0:8, :], start=False, stop=True)
                    last.then_inc(f2_hid, 1)
                for c in CH:
                    pe.wait_ge(f2_relu, c + 1)
                    for t in TILES:
                        mm(bank(c, 2)[:, t * D:(t + 1) * D], mT[c][0:8, t * P:(t + 1) * P], w("L2_b2"))
                        for m in range(2):
                            last = mm(bank(c, t), qT[c][:, m, t * P:(t + 1) * P], w("L2_W2")[:, m * 512:(m + 1) * 512],
                                      start=(m == 0), stop=(m == 1))
                    last.then_inc(f2_y, 1)
                features("L3_attn_in", xn)
                for c in CH:
                    pe.wait_ge(feat_ready, nth(TURN["L3_attn_in"], c))
                    mm(bank(c, 2)[0:D, 0:T], wide("L3_Wq"), xT[c][:])
                    mm(bank(c, 2)[0:D, T:2 * T], wide("L3_Wk"), xT[c][:])
                    for t in TILES:
                        last = mm(bank(c, 1)[:, t * D:(t + 1) * D], xT[c][:, t * P:(t + 1) * P], wide("L3_Wv"))
                    last.then_inc(c2_ready, 1)
                attention(STEP["L3"], 1, c2_used, 1, lambda s, c, e, t: pT[c][0:D, t * P:(t + 1) * P],
                          lambda s, c, e: pT[c][0:D, T:2 * T], lambda s, c, e, kt_: vv[c][:, kt_, :],
                          1, True, None, D)
                features("L3_qkv_in", xc)
                project(TURN["L3_qkv_in"], xT, wide("L3_wqkv"))
                for c in CH:
                    pe.wait_ge(qk_rows, nth(2, c))
                    for g in range(2):
                        for t in TILES:
                            last = turn(bank(c, 3)[:, g * T + t * P:g * T + (t + 1) * P],
                                        kd4[c][:, g, t, :])
                    last.then_inc(qk_turned, 1)
                attention(STEP["L3f"], 2, qk_ready, 2,
                          lambda s, c, e, t: pT[c][:, t * P:(t + 1) * P], lambda s, c, e: kz[c][:, 2 * s + e, :],
                          lambda s, c, e, kt_: kk[c][:, kt_, 96 + 16 * s:112 + 16 * s], 2, False, causal, 16)
                features("L3_attn_out", [att[c][:, :, 0:D] for c in CH])
                project(TURN["L3_attn_out"], xT, wide("L3_wo"))
                features("L3_moe_in", xc)
                project(TURN["L3_moe_in"], xT, wide("L3_router"))
                w13 = wide("L3_w13").rearrange("p (e f) -> p e f", e=8)
                for x in range(16):
                    t, e = x // 8, x % 8
                    for c in CH:
                        if x >= 3:
                            pe.wait_ge(f4_h, nth(x - 3, c))
                        mm(bank(c, MOE_BANK[x % 3])[:, 0:2 * HIDDEN3], xT[c][:, t * P:(t + 1) * P],
                           w13[:, e, :]).then_inc(f4_gu, 1)
                for t in TILES:
                    for part in range(3):
                        for c in CH:
                            if part == 0:
                                pe.wait_ge(f4_h, nth(15, c))
                            if t == 1:
                                pe.wait_ge(f4_hT, nth(part, c))
                            for kx in range(4 * part, min(4 * part + 4, 11)):
                                kw = P if kx < 10 else 80
                                u = kx - 4 * part
                                last = turn(bank(c, MOE_BANK[part])[0:kw, u * P:(u + 1) * P],
                                            hid[t][c][:, kx * P:kx * P + kw])
                            last.then_inc(f4_turned, 1)
                    for c in CH:
                        for kx in range(11):
                            if kx % 4 == 0:
                                pe.wait_ge(f4_hT, nth(3 * t + kx // 4, c))
                            kw = P if kx < 10 else 80
                            src = pT[c][:, kx * P:(kx + 1) * P] if kx < 8 else prT[c][0:kw, (kx - 8) * P:(kx - 7) * P]
                            wt = w("L3_w2")[:, kx * D:(kx + 1) * D] if kx < 10 else w("L3_w2t")
                            last = mm(bank(c, 2)[:, t * D:(t + 1) * D], src, wt, start=(kx == 0), stop=(kx == 10))
                        last.then_inc(ao_rows, 1)
                close_pass(pe, i)

        @block.scalar
        def _(act):
            a = nc.scalar.activation
            for l in range(2):
                act.wait_ge(tabmm, 1 + 2 * l)
                a(tab_t[:], ps[:, 2, 0:4 * D].rearrange("p (e v) -> p e v", e=4), ACT.Tanh, scale=0.5).then_inc(taba, 1)

            def features(name, width=D):
                n = TURN[name]
                for c in CH:
                    act.wait_ge(turned, nth(n, c))
                    dst = xT[c][0:D, :] if width == D else xT2[c][:]
                    a(dst, bank(c, 3)[0:width, 0:T], ACT.Copy).then_inc(feat_ready, 1)

            def logits_exp(n, width):
                for c in CH:
                    act.wait_ge(shifted, nth(n, c))
                    a(prob[c][:, :, 0:width], prob[c][:, :, 0:width], ACT.Exp).then_inc(expd, 1)

            def attention(first, count, heads, full, scale, masked=False):
                nb_ = len(blocks(full))

                def copy_turned(s, c):
                    act.wait_ge(at_turned, nth(first + s, c))
                    wd = heads * nb_ * P
                    a(prT[c][:, 0:wd], ps[:, 4 * c + 2:4 * c + 4, :].rearrange("p a b -> p (a b)")[:, 0:wd],
                      ACT.Copy).then_inc(at_probsT, 1)

                for u in range(2 * count):
                    s, c = u // 2, u % 2
                    act.wait_ge(at_bias, nth(first + s, c))
                    for e in range(heads):
                        for t in TILES:
                            at, wd = (0 if t == 0 else (T if full else P)), (T if full or t == 1 else P)
                            x = e * nb_ * P + at
                            src = masked_s[c][t][:, e, :] if masked else bank(c, e)[:, at:at + wd]
                            last = a(pr[c][:, x:x + wd], src, ACT.Exp,
                                     bias=nb[c][:, 2 * t + e:2 * t + e + 1], scale=scale(s, c, e, t),
                                     accum_out=rs[c][:, s % 2, 2 * t + e:2 * t + e + 1])
                    last.then_inc(at_probs, 1)
                    if u > 0:
                        copy_turned((u - 1) // 2, (u - 1) % 2)
                copy_turned(count - 1, 1)

            with act.Fori(0, PASSES) as i:
                for c in CH:
                    act.wait_ge(a0_max, c + 1)
                    a(sm[c][:], sm[c][:], ACT.Exp, scale=8 ** -0.5).then_inc(a0_exp, 1)
                for c in CH:
                    act.wait_ge(a0_probsT_ps, c + 1)
                    a(pT[c][:], banks2(c, 0).rearrange("p a b -> p (a b)"), ACT.Copy).then_inc(a0_probsT, 1)
                features("L0_attn_out")
                features("L0_ffn_in")
                logits_exp(0, D)
                for x in range(16):
                    for c in CH:
                        act.wait_ge(z_turned, nth(x, c))
                        if x >= 2:
                            act.wait_ge(zsum_ready, nth(x - 2, c))
                        a(zT[x % 2][c][:], bank(c, x % 2), ACT.Copy).then_inc(zT_ready, 1)
                for c in CH:
                    act.wait_ge(zsum_ready, nth(15, c))
                    a(xT[c][0:D, :], bank(c, 2)[0:D, 0:T], ACT.Copy).then_inc(lattice_out, 1)
                features("L1_attn_in")
                def q_squares(t, c):
                    act.wait_ge(q_roped, nth(t, c))
                    if t == 1:
                        act.wait_ge(q_var, nth(0, c))
                    a(qa[c][:], att[c][:, t, :], ACT.Square).then_inc(q_sq, 1)

                def copy_q(t, c):
                    act.wait_ge(q_turned, nth(t, c))
                    a(qT[c][:, :, t * P:(t + 1) * P], banks2(c, 2).rearrange("p a (b q) -> p (a b) q", q=P),
                      ACT.Copy).then_inc(qT_ready, 1)

                q_squares(0, 0)
                for c in CH:
                    act.wait_ge(qk_turned, nth(0, c))
                    for e in range(2):
                        r = slice(D * e, D * e + D)
                        last = a(kT[c][r, e, :], bank(c, 3)[r, 0:T], ACT.Copy)
                    last.then_inc(qk_ready, 1)
                copy_q(0, 0)
                q_squares(0, 1)
                copy_q(0, 1)
                for c in CH:
                    q_squares(1, c)
                for c in CH:
                    copy_q(1, c)
                attention(STEP["L1"], 8, 2, False,
                          lambda s, c, e, t: exs[c][:, t, 2 * s + e:2 * s + e + 1], masked=True)
                for t in TILES:
                    for c in CH:
                        act.wait_ge(ao_turned, nth(t, c))
                        a(qT[c][:, :, t * P:(t + 1) * P], banks2(c, 0).rearrange("p a (b q) -> p (a b) q", q=P),
                          ACT.Copy).then_inc(ao_ready, 1)
                features("L1_ffn_in")
                for c in CH:
                    act.wait_ge(f1_turned, c + 1)
                    a(pT[c][:], banks2(c, 0).rearrange("p a b -> p (a b)"), ACT.Copy)
                    a(mT[c][:], bank(c, 3)[0:32, 0:T], ACT.Copy).then_inc(f1_zT, 1)
                features("L2_attn_in")
                for c in CH:
                    act.wait_ge(c2_ready, c + 1)
                    a(pT[c][0:D, 0:512], bank(c, 2)[0:D, :], ACT.Copy).then_inc(c2_used, 1)
                for c in CH:
                    act.wait_ge(qk_turned, nth(1, c))
                    a(pT[c][0:D, 0:512], bank(c, 3)[0:D, :], ACT.Copy).then_inc(qk_ready, 1)
                attention(STEP["L2"], 1, 1, False, lambda s, c, e, t: 0.125)
                features("L2_ffn_in", P)
                logits_exp(1, 8)
                for c in CH:
                    act.wait_ge(f2_maskT, c + 1)
                    a(mT[c][0:8, :], bank(c, 3)[0:8, 0:T], ACT.Copy)
                    a(mTb[c][:], bank(c, 3)[0:8, 0:T], ACT.Copy).then_inc(f2_mask, 1)
                for c in CH:
                    act.wait_ge(f2_hid, c + 1)
                    a(qT[c][:, 0:2, :], bank(c, 2).rearrange("p (m t) -> p m t", m=2), ACT.Relu).then_inc(f2_relu, 1)
                features("L3_attn_in")
                for c in CH:
                    act.wait_ge(c2_ready, nth(1, c))
                    a(pT[c][0:D, 0:512], bank(c, 2)[0:D, :], ACT.Copy)
                    a(vv[c][:], bank(c, 1)[:, 0:P].rearrange("p (t d) -> p t d", t=2), ACT.Copy).then_inc(c2_used, 1)
                attention(STEP["L3"], 1, 1, True, lambda s, c, e, t: 0.125)
                features("L3_qkv_in")
                for c in CH:
                    act.wait_ge(qk_turned, nth(2, c))
                    act.wait_ge(kz_zeroed, c + 1)
                    a(pT[c][:, 0:T], bank(c, 3)[:, 0:T], ACT.Copy)
                    for hd in range(4):
                        r = slice(32 * hd, 32 * hd + 32)
                        last = a(kz[c][r, hd, :], bank(c, 3)[r, T:2 * T], ACT.Copy)
                    last.then_inc(qk_ready, 1)
                attention(STEP["L3f"], 2, 2, False, lambda s, c, e, t: 0.25)
                features("L3_attn_out")
                features("L3_moe_in")
                logits_exp(2, 8)
                for x in range(16):
                    for c in CH:
                        act.wait_ge(f4_gu, nth(x, c))
                        if x >= 3:
                            act.wait_ge(f4_h, nth(x - 3, c))
                        a(th[c][:, x % 3, :], bank(c, MOE_BANK[x % 3])[:, 0:HIDDEN3], ACT.Tanh, scale=0.5).then_inc(f4_tanh, 1)
                for t in TILES:
                    for part in range(3):
                        for c in CH:
                            act.wait_ge(f4_turned, nth(t * 3 + part, c))
                            if t == 1:
                                act.wait_ge(ao_rows, nth(3, c))
                            src = bank(c, MOE_BANK[part])
                            if part < 2:
                                a(pT[c][:, part * 512:(part + 1) * 512], src, ACT.Copy).then_inc(f4_hT, 1)
                            else:
                                a(prT[c][:, 0:256], src[:, 0:256], ACT.Copy)
                                a(prT[c][0:80, 256:384], src[0:80, 256:384], ACT.Copy).then_inc(f4_hT, 1)
                close_pass(act, i)

        @block.vector
        def _(dve):
            v = nc.vector
            setup = Steps(dve, vset)
            dve.wait_ge(iset, 4)
            dve.wait_ge(early, EARLY)
            setup.done(v.tensor_copy(ids_bc[:], ids_bc_i))
            setup.done(v.tensor_copy(ids_tok[:], ids_tok_i[:]))
            setup.done(v.tensor_copy(edges[:], edges_i))
            setup.done(v.tensor_copy(ident_b[:], ident))
            setup.done(v.memset(diag_b[:], 0.0))
            setup.after()
            for j in TILES:
                setup.done(v.tensor_copy(diag_b[:, j, j * P:(j + 1) * P], ident))
            setup.done(v.tensor_copy(maskb[:], w("causal")))
            setup.done(v.tensor_copy(tri_b[:], w("tri")))
            setup.done(v.memset(ones_b[:], 1.0))
            setup.done(v.tensor_tensor(qk_norm[:], vecs[:, 4, :], vecs[:, 5, :], ALU.mult))
            setup.done(v.memset(vblk[:], 0.0))
            setup.done(v.memset(score_tab[:], 0.0))
            setup.done(v.memset(xtabT[D:D + 1, :, :], 1.0))
            for c in CH:
                setup.done(v.memset(xT[c][D:P, :], 0.0))
                setup.done(v.memset(hotT[c][:], 0.0))
                setup.done(v.memset(kT[c][:], 0.0))
                setup.after()
                setup.done(v.memset(xT[c][D:D + 1, :], 1.0))
                setup.done(v.memset(lg[c][:], BIG))
                for k in (1, 2, 6):
                    setup.done(v.memset(pick[k][c][:], BIG))
                setup.done(v.memset(kd4[c][:], 0.0))
            setup.after()
            dve.drain().then_inc(consts, 1)
            def edge_rows(lo, hi):
                with dve.Fori(lo, hi) as i:
                    for half_ in range(2):
                        dve.wait_ge(edge_used, i * 2 + half_ + 1)
                        for u in range(8):
                            v.tensor_scalar(hot_src[:, half_, u, :], iota_b[:],
                                            edges[:, 0, bass.ds(i * 16 + (half_ * 8 + u), 1)], None, ALU.is_equal)
                            last = v.tensor_scalar(hot_dst[:, half_, u, :], iota_b[:],
                                                   edges[:, 1, bass.ds(i * 16 + (half_ * 8 + u), 1)], None, ALU.is_equal)
                        last.then_inc(edge_hot, 1)

            def table_layer(l):
                dve.wait_ge(taba, l + 1)
                setup.done(v.scalar_tensor_tensor(tab_a[:], tab_t[:], 1.0,
                                                  ps[:, 2, 0:4 * D].rearrange("p (e v) -> p e v", e=4), ALU.add, ALU.mult))
                setup.after()
                v.scalar_tensor_tensor(tab_z[:], ps[:, 3, 0:4 * D].rearrange("p (e v) -> p e v", e=4), 0.125,
                                       tab_a[:], ALU.mult, ALU.mult).then_inc(tabz, 1)
                dve.wait_ge(tabmm, 2 + 2 * l)
                dve.wait_ge(consts, 2 + l)
                v.tensor_tensor(tabT[:], tabT[:], ps[0:D, 4, 0:D], ALU.add).then_inc(consts, 1)

            v.tensor_copy(tabT[:], w("embT")).then_inc(consts, 1)
            edge_rows(0, 2)
            table_layer(0)
            edge_rows(2, 4)
            table_layer(1)
            edge_rows(4, 6)
            dve.wait_ge(tabmm, 5)
            setup.done(v.tensor_copy(tabs[:, 0, :], ps[0:D, 5, 0:D]))
            setup.after()
            setup.done(v.reduce_sum(tab_s[:, 0:1], tabs[:, 0, :], AX.X))
            setup.after()
            setup.done(v.scalar_tensor_tensor(tab_q[:], tab_s[:, 0:1].to_broadcast([D, D]), -1.0 / D, tabs[:, 0, :],
                                              ALU.mult, ALU.add))
            setup.after()
            setup.done(v.tensor_tensor(tabs[:, 1, :], tab_q[:], tab_q[:], ALU.mult))
            setup.after()
            setup.done(v.reduce_sum(tab_s[:, 1:2], tabs[:, 1, :], AX.X))
            setup.after()
            v.tensor_scalar(tab_s[:, 2:3], tab_s[:, 1:2], 1.0 / D, EPS, ALU.mult, ALU.add).then_inc(tabv, 1)
            dve.wait_ge(tabpow, 1)
            v.tensor_scalar(tabs[:, 1, :], tab_q[:], tab_s[:, 3:4], None, ALU.mult).then_inc(consts, 1)
            dve.wait_ge(tabmm, 6)
            v.tensor_copy(xtabT[0:D, 0, :], ps[0:D, 6, 0:D])
            v.tensor_copy(xtabT[0:D, 1, :], ps[0:D, 6, 0:D]).then_inc(consts, 1)
            edge_rows(6, 8)
            dve.wait_ge(tabmm, 7)
            v.tensor_copy(qtab[:].rearrange("p a b -> p (a b)"), ps[0:8, 2, :])
            v.tensor_copy(ktab[:].rearrange("p a b -> p (a b)"), ps[0:8, 3, :]).then_inc(consts, 1)
            dve.wait_ge(edge_total, 1)
            setup.done(v.tensor_scalar(allow[:], ps[:, 0:2, 0:T], 0.5, None, ALU.is_gt))
            for g in range(2):
                r = slice(g * D, g * D + D)
                setup.done(v.memset(vblk[r, :, g, 8:9], 1.0))
                setup.done(v.tensor_copy(vblk[r, :, g, 0:8],
                                         ps[r, 4, 0:D].rearrange("p (a g d) -> p a g d", a=4, g=2)[:, :, g, :]))
            dve.wait_ge(late, LATE)
            setup.done(v.tensor_copy(sel_b[:], w("sel8").rearrange("p (a b) -> p a b", a=4)))
            setup.done(v.tensor_scalar(w("L3_wqkv"), w("L3_wqkv"), ln1w[:, 0:1], None, ALU.mult))
            setup.done(v.tensor_scalar(w("L3_router"), w("L3_router"), ln2w[:, 0:1], None, ALU.mult))
            setup.done(v.tensor_scalar(w("L3_w13"), w("L3_w13"), ln2w[:, 0:1], None, ALU.mult))
            dve.wait_ge(tabmm, 8)
            setup.done(v.tensor_copy(score_tab[0:D].rearrange("p a b -> p (a b)"), ps[0:D, 5, :]))
            setup.after()
            dve.drain().then_inc(consts, 1)

            def bcast(ap, n):
                return ap.unsqueeze(2).to_broadcast([ap.shape[0], ap.shape[1], n])

            def bcast_mid(ap, n):
                return ap.unsqueeze(2).to_broadcast([ap.shape[0], ap.shape[1], n, ap.shape[2]])

            def bcast_heads(ap, n):
                return ap.unsqueeze(1).to_broadcast([ap.shape[0], n, ap.shape[1]])

            def tv(ap, t=2):
                return ap.rearrange("p (t f) -> p t f", t=t)

            with dve.Fori(0, PASSES) as i:
                steps = Steps(dve, vstep)
                done, after = steps.done, steps.after
                last = [0, 0]

                def statistics(name, src):
                    for c in CH:
                        after(last[c])
                        for t in TILES:
                            last[c] = done(v.bn_stats(parts[c][:, t, :], src[c][:, t, :]))
                    for c in CH:
                        after(last[c])
                        for t in TILES:
                            last[c] = done(v.bn_aggr(mv[c][:, t, :], parts[c][:, t, :]))
                    for c in CH:
                        after(last[c])
                        v.tensor_scalar(st[c][:, 2, 0:2], mv[c][:, :, 1], EPS, None, ALU.add).then_inc(var_ready, 1)

                def squares(src):
                    for c in CH:
                        after(last[c])
                        last[c] = done(v.tensor_tensor(sq[c][:], src[c][:], src[c][:], ALU.mult))
                    for c in CH:
                        after(last[c])
                        last[c] = done(v.reduce_sum(st[c][:, 1, 0:2], sq[c][:], AX.X))

                def inverse_root(name, eps):
                    n = NORM[name]
                    for c in CH:
                        after(last[c])
                        v.tensor_scalar(st[c][:, 2, 0:2], st[c][:, 1, 0:2], 1.0 / D, eps, ALU.mult,
                                        ALU.add).then_inc(var_ready, 1)

                def rooted(name, c):
                    dve.wait_ge(rstd_ready, nth(NORM[name], c))

                def norm_rows(name, src, dst=None):
                    statistics(name, src)
                    for c in CH:
                        rooted(name, c)
                        for t in TILES:
                            o = xn[c][:, t, :] if dst is None else xd[c][:, t]
                            x = src[c][:, t, :] if dst is None else bcast_heads(src[c][:, t, :], 2)
                            q = v.tensor_scalar(o, x, mv[c][:, t, 0:1], rstd[c][:, t:t + 1], ALU.subtract, ALU.mult)
                        q.then_inc(rows_ready, 1)

                def post_norm(name, proj, g):
                    for c in CH:
                        dve.wait_ge(proj_ready, nth(proj, c))
                        last[c] = done(v.tensor_tensor(xn[c][:], xn[c][:], tv(bank(c, 2)[:, 0:P]), ALU.add))
                    statistics(name, xn)
                    for c in CH:
                        for t in TILES:
                            done(v.scalar_tensor_tensor(xc[c][:, t, :], xn[c][:, t, :], mv[c][:, t, 0:1], vecs[:, g, :],
                                                        ALU.subtract, ALU.mult))
                        last[c] = done(v.tensor_tensor(sq[c][:], h[c][:], bcast_heads(vecs[:, g + 1, :], 2), ALU.add))
                    for c in CH:
                        rooted(name, c)
                        after(last[c])
                        for t in TILES:
                            last[c] = done(v.scalar_tensor_tensor(h[c][:, t, :], xc[c][:, t, :], rstd[c][:, t:t + 1],
                                                                  sq[c][:, t, :], ALU.mult, ALU.add))

                def route(proj, E, k, added=None):
                    lo = D - E
                    for c in CH:
                        dve.wait_ge(proj_ready, nth(proj, c))
                        if added is None:
                            last[c] = done(v.tensor_copy(lg[c][:, :, lo:D], tv(bank(c, 2)[:, 0:2 * E])))
                        else:
                            last[c] = done(v.tensor_tensor(lg[c][:, :, lo:D], tv(bank(c, 2)[:, 0:2 * E]),
                                                           bcast_heads(added, 2), ALU.add))
                    for c in CH:
                        after(last[c])
                        for t in TILES:
                            last[c] = done(v.max(top[c][:, t, :], lg[c][:, t, lo:D]))
                    for c in CH:
                        after(last[c])
                        last[c] = done(v.tensor_copy(pick[k][c][:, :, 0:k], top[c][:, :, 0:k]))
                    for c in CH:
                        after(last[c])
                        for t in TILES:
                            last[c] = done(v.match_replace(rep[c][:, t, lo:D + 8 - k], pick[k][c][:, t, :],
                                                           lg[c][:, t, lo:D + 8 - k], -BIG))
                    for c in CH:
                        after(last[c])
                        last[c] = done(v.tensor_scalar(sel[c][:, :, 0:E], rep[c][:, :, lo:D], -0.5 * BIG, None, ALU.is_lt))

                def shift(E):
                    for c in CH:
                        v.tensor_tensor(prob[c][:, :, 0:E], lg[c][:, :, D - E:D], bcast(top[c][:, :, 0], E),
                                        ALU.subtract).then_inc(shifted, 1)

                def attention(first, count, heads, full, exp_scale, out_, dv=D, masks=None):
                    def bias(s, c):
                        if first == STEP["L1"] and s == 0:
                            dve.wait_ge(scales_ready, 3 + c)
                        if first == STEP["L1"] and s == 2:
                            dve.wait_ge(scales_ready, 6 + 2 * c)
                        dve.wait_ge(at_scores, nth(first + s, c))
                        scored = [ps[:, 4 * c:4 * c + heads, at:at + wd] for at, wd in
                                  (((0, T), (T, T)) if full else ((0, P), (P, T)))]
                        if masks is not None:
                            if s > 0:
                                dve.wait_ge(at_probs, nth(first + s - 1, c))
                            room = masked_s[c]
                            for t in TILES:
                                last[c] = done(v.tensor_tensor(room[t], scored[t], bcast_heads(masks[t], heads), ALU.add))
                            scored = room
                            after(last[c])
                        for t in TILES:
                            last[c] = done(v.tensor_reduce(mx[c][:, 2 * t:2 * t + heads], scored[t], AX.X, ALU.max))
                        after(last[c])
                        m, n_ = tv(mx[c][:])[:, :, 0:heads], tv(nb[c][:])[:, :, 0:heads]
                        if isinstance(exp_scale, float):
                            v.tensor_scalar(n_, m, -exp_scale, None, ALU.mult).then_inc(at_bias, 1)
                        else:
                            v.scalar_tensor_tensor(n_, m, -1.0, exp_scale(s, c), ALU.mult, ALU.mult).then_inc(at_bias, 1)

                    def divide(s, c):
                        dve.wait_ge(at_av, nth(first + s, c))
                        r = tv(rr[c][:, 0:4])[:, :, 0:heads]
                        last[c] = done(v.reciprocal(r, tv(rs[c][:, s % 2])[:, :, 0:heads]))
                        after(last[c])
                        o = bank(c, 3)[:, 256:256 + heads * 2 * dv].rearrange("p (e t d) -> p t e d", t=2, d=dv)
                        v.tensor_tensor(out_(s, c), o, r.unsqueeze(3).to_broadcast([P, 2, heads, dv]),
                                        ALU.mult).then_inc(at_out, 1)

                    for c in CH:
                        bias(0, c)
                    for u in range(2 * count):
                        s, c = u // 2, u % 2
                        if s + 1 < count:
                            bias(s + 1, c)
                        if u > 0:
                            divide((u - 1) // 2, (u - 1) % 2)
                    divide(count - 1, 1)

                def add_to_h(step):
                    for c in CH:
                        dve.wait_ge(at_out, nth(step, c))
                        last[c] = done(v.tensor_tensor(h[c][:], h[c][:], xc[c][:], ALU.add))

                for c in CH:
                    v.tensor_scalar(hotT[c][0:D, :], ids_bc[:, bass.ds((i * 2 + c) * T, T)], w("iota_col")[0:D, :], None,
                                    ALU.is_equal).then_inc(hotT_ready, 1)
                    v.tensor_tensor(hot[c][:], bcast_heads(iota_b[:, 0:D], 2),
                                    bcast(ids_tok[:, bass.ds(i * 4 + 2 * c, 2)], D), ALU.is_equal).then_inc(hot_ready, 1)
                for c in CH:
                    dve.wait_ge(a0_counts, c + 1)
                    v.tensor_scalar(penT[c][:], bank(c, 3)[0:D, P:P + T], 0.5, NEG, ALU.is_lt, ALU.mult).then_inc(a0_pen, 1)
                for c in CH:
                    dve.wait_ge(a0_scores, c + 1)
                    s3 = banks2(c, 0).rearrange("p t (h v) -> p (t h) v", v=D)
                    last[c] = done(v.reduce_max(st[c][:, 0, :], s3, AX.X))
                    after(last[c])
                    v.tensor_tensor(sm[c][:].rearrange("p t h v -> p (t h) v"), s3, bcast(st[c][:, 0, :], D),
                                    ALU.subtract).then_inc(a0_max, 1)
                    g = bank(c, 2)[:, 0:2 * P].rearrange("p (t a d) -> p t a d", t=2, a=2)
                    last[c] = done(v.tensor_copy(h[c][:], g[:, :, 0, :]))
                    done(v.tensor_copy(xn[c][:], g[:, :, 1, :]))
                for c in CH:
                    dve.wait_ge(a0_exp, c + 1)
                    v.tensor_tensor(sm[c][:], sm[c][:], bcast_mid(tv(bank(c, 3)[:, 0:P]), 8),
                                    ALU.mult).then_inc(a0_probs, 1)
                for c in CH:
                    dve.wait_ge(a0_av, c + 1)
                    o = bank(c, 2)[:, 0:144].rearrange("p (a b) -> p a b", b=9)
                    last[c] = done(v.reciprocal(rr[c][:], o[:, :, 8]))
                    after(last[c])
                    for t in TILES:
                        q = v.tensor_tensor(att[c][:, t, 0:D].rearrange("p (h d) -> p h d", h=8),
                                            o[:, 8 * t:8 * t + 8, 0:8], bcast(rr[c][:, 8 * t:8 * t + 8], 8), ALU.mult)
                    q.then_inc(rows_ready, 1)
                post_norm("L0_attn_post", 0, 0)
                norm_rows("L0_ffn_pre", h)
                route(1, D, 6)
                shift(D)
                for c in CH:
                    dve.wait_ge(expd, c + 1)
                    last[c] = done(v.tensor_tensor(prob[c][:], prob[c][:], sel[c][:], ALU.mult))
                for c in CH:
                    after(last[c])
                    last[c] = done(v.reduce_sum(st[c][:, 0, 0:2], prob[c][:], AX.X))
                for c in CH:
                    after(last[c])
                    last[c] = done(v.reciprocal(rr[c][:, 0:2], st[c][:, 0, 0:2]))
                for c in CH:
                    after(last[c])
                    last[c] = done(v.tensor_tensor(prob[c][:], prob[c][:], bcast(rr[c][:, 0:2], D), ALU.mult))
                for c in CH:
                    after(last[c])
                for x in range(16):
                    t, k8 = x // 8, x % 8
                    for c in CH:
                        if x >= 2:
                            dve.wait_ge(z_turned, nth(x - 2, c))
                        v.tensor_tensor(zb[x % 2][c][:], bcast_heads(xn[c][:, t, :], 8),
                                        bcast(prob[c][:, t, 8 * k8:8 * k8 + 8], D), ALU.mult).then_inc(z_ready, 1)
                post_norm("L0_ffn_post", 2, 2)
                norm_rows("L1_attn_pre", h)
                for c in CH:
                    dve.wait_ge(proj_ready, nth(3, c))
                    kv = tv(bank(c, 2)[:, 0:256])
                    done(v.tensor_copy(vv[c][:], kv[:, :, D:P]))
                    done(v.tensor_tensor(kk[c][:, :, 0:D], kv[:, :, 0:D], cosq, ALU.mult))
                    done(v.tensor_tensor(kkm[c][:, :, 0:32], kv[:, :, 32:64], sinq[:, :, 0:32], ALU.mult))
                    last[c] = done(v.tensor_tensor(kkm[c][:, :, 32:64], kv[:, :, 0:32], sinq[:, :, 32:64], ALU.mult))
                for c in CH:
                    after(last[c])
                    last[c] = done(v.tensor_tensor(kk[c][:, :, 0:D], kk[c][:, :, 0:D], kkm[c][:, :, 0:D], ALU.add))
                squares([kk[c][:, :, 0:D] for c in CH])
                inverse_root("L1_k", 1.1920929e-07)

                def rope_q(t, c):
                    dve.wait_ge(q_proj, nth(t, c))
                    qp = banks2(c, 0).rearrange("p a (h f) -> p (a h) f", f=D)
                    qo = att[c][:, t, :].rearrange("p (h f) -> p h f", f=D)
                    qs = qb[c].rearrange("p (h f) -> p h f", f=D)
                    if t == 1:
                        dve.wait_ge(q_roped, c + 1)
                    v.tensor_tensor(qo, qp, bcast_heads(cosq[:, t, :], 16), ALU.mult)
                    v.tensor_tensor(qs[:, :, 0:32], qp[:, :, 32:64], bcast_heads(sinq[:, t, 0:32], 16), ALU.mult)
                    v.tensor_tensor(qs[:, :, 32:64], qp[:, :, 0:32], bcast_heads(sinq[:, t, 32:64], 16),
                                    ALU.mult).then_inc(q_used, 1)
                    if (t, c) == (1, 1):
                        dve.wait_ge(q_used, nth(t, c))
                        dve.wait_ge(q_roped, nth(1, 0))
                        v.tensor_tensor(att[c][:, t, :], att[c][:, t, :], qb[c], ALU.add).then_inc(q_roped, 1)

                def q_variance(t, c):
                    dve.wait_ge(q_sq, nth(t, c))
                    last[c] = done(v.reduce_sum(qsum[c][:, t, :], qa[c][:].rearrange("p (h f) -> p h f", f=D), AX.X))
                    after(last[c])
                    v.tensor_scalar(qsum[c][:, t, :], qsum[c][:, t, :], D * 1.1920929e-07, None,
                                    ALU.add).then_inc(q_var, 1)

                rope_q(0, 0)
                for c in CH:
                    rooted("L1_k", c)
                    last[c] = done(v.tensor_tensor(kk[c][:, :, 0:D], kk[c][:, :, 0:D], bcast(rstd[c][:, 0:2], D), ALU.mult))
                for c in CH:
                    after(last[c])
                    for t in TILES:
                        q = v.tensor_tensor(kd[c][:, t], bcast_heads(kk[c][:, t, 0:D], 2),
                                            bcast_heads(qk_norm[:], 2), ALU.mult)
                    q.then_inc(qk_rows, 1)
                rope_q(0, 1)
                q_variance(0, 0)
                rope_q(1, 0)
                q_variance(0, 1)
                rope_q(1, 1)
                for c in CH:
                    q_variance(1, c)
                attention(STEP["L1"], 8, 2, False, lambda s, c: exs[c][:, :, 2 * s:2 * s + 2],
                          lambda s, c: att[c][:, :, 2 * s * D:2 * (s + 1) * D].rearrange("p t (e d) -> p t e d", e=2),
                          masks=[w("causal"), w_pair])
                for c in CH:
                    dve.wait_ge(ao_rows, nth(1, c))
                    last[c] = done(v.tensor_tensor(h[c][:], h[c][:], tv(bank(c, 2)[:, 0:P]), ALU.add))
                norm_rows("L1_ffn_pre", h)
                route(4, 32, 1)
                for c in CH:
                    after(last[c])
                    dve.wait_ge(q_proj, nth(2, c))
                    for t in TILES:
                        v.scalar_tensor_tensor(z1[c][:, t, 0:512].rearrange("p (e f) -> p e f", f=16),
                                               bank(c, t).rearrange("p (e f) -> p e f", f=16), 0.0,
                                               bcast(sel[c][:, t, 0:32], 16), ALU.max, ALU.mult)
                    v.tensor_copy(z1[c][:, :, 512:544], sel[c][:, :, 0:32]).then_inc(f1_z, 1)
                for c in CH:
                    dve.wait_ge(ao_rows, nth(2, c))
                    last[c] = done(v.scalar_tensor_tensor(h[c][:], tv(bank(c, 2)[:, 0:P]), 0.0, h[c][:], ALU.max, ALU.add))
                norm_rows("L2_attn_pre", h)
                for c in CH:
                    dve.wait_ge(q_proj, nth(3, c))
                    x = bank(c, 0)[:, 0:384].rearrange("p (t g f) -> p t g f", t=2, g=3)
                    kq = kk[c][:].rearrange("p t (g f) -> p t g f", g=2)
                    km = kkm[c][:].rearrange("p t (g f) -> p t g f", g=2)
                    done(v.tensor_copy(vv[c][:], x[:, :, 2, :]))
                    done(v.tensor_copy(kq[:, :, :, 0:48], x[:, :, 0:2, 0:48]))
                    done(v.tensor_tensor(kq[:, :, :, 48:64], x[:, :, 0:2, 48:64], bcast_mid(cos2, 2), ALU.mult))
                    done(v.tensor_tensor(km[:, :, :, 0:8], x[:, :, 0:2, 56:64], bcast_mid(sin2[:, :, 0:8], 2), ALU.mult))
                    last[c] = done(v.tensor_tensor(km[:, :, :, 8:16], x[:, :, 0:2, 48:56],
                                                   bcast_mid(sin2[:, :, 8:16], 2), ALU.mult))
                    after(last[c])
                    v.tensor_tensor(kq[:, :, :, 48:64], kq[:, :, :, 48:64], km[:, :, :, 0:16], ALU.add).then_inc(qk_rows, 1)
                attention(STEP["L2"], 1, 1, False, 0.125, lambda s, c: xc[c][:].unsqueeze(2))
                add_to_h(STEP["L2"])
                CAP = -(-5 * SEQS * T // 4) // 8
                norm_rows("L2_ffn_pre", h, xd)
                route(5, 8, 1, vecs[:, 6, 0:8])
                shift(8)
                for c in CH:
                    after(last[c])
                    v.tensor_copy(mb[c][:], sel[c][:, :, 0:8]).then_inc(f2_hot, 1)
                for c in CH:
                    dve.wait_ge(expd, nth(1, c))
                    last[c] = done(v.reduce_sum(st[c][:, 0, 0:2], prob[c][:, :, 0:8], AX.X))
                    after(last[c])
                    last[c] = done(v.reciprocal(rr[c][:, 0:2], st[c][:, 0, 0:2]))
                for c in CH:
                    dve.wait_ge(f2_count, c + 1)
                    last[c] = done(v.tensor_tensor(pen[c][:, :, 0:8], tv(bank(c, 2)[:, 32:48]),
                                                   bcast_heads(carry[:], 2), ALU.add))
                    after(last[c])
                    last[c] = done(v.tensor_tensor(carry[:], carry[:], bank(c, 2)[:, 48:56], ALU.add))
                    last[c] = done(v.tensor_tensor(pen[c][:, :, 0:8], pen[c][:, :, 0:8], sel[c][:, :, 0:8], ALU.mult))
                    after(last[c])
                    last[c] = done(v.reduce_sum(keep[c][:], pen[c][:, :, 0:8], AX.X))
                    after(last[c])
                    last[c] = done(v.scalar_tensor_tensor(gate[c][:], keep[c][:], float(CAP) + 0.5, rr[c][:, 0:2],
                                                          ALU.is_lt, ALU.mult))
                for c in CH:
                    dve.wait_ge(f2_bc, c + 1)
                    x4 = pT[c][:].rearrange("p (a q) -> p a q", a=4)
                    v.tensor_tensor(x4, banks2(c, 0).rearrange("p a (b q) -> p (a b) q", q=T),
                                    bcast_heads(xT2[c][:], 4), ALU.mult).then_inc(f2_xm, 1)
                for c in CH:
                    dve.wait_ge(f2_y, c + 1)
                    for t in TILES:
                        y3 = bank(c, t).rearrange("p (e d) -> p e d", e=8)
                        last[c] = done(v.tensor_tensor(sm[c][:, t], y3, bcast(sel[c][:, t, 0:8], D), ALU.mult))
                    after(last[c])
                    for t in TILES:
                        last[c] = done(v.reduce_sum(xc[c][:, t, :], sm[c][:, t].rearrange("p e d -> p d e"), AX.X))
                    after(last[c])
                    last[c] = done(v.tensor_tensor(xc[c][:], xc[c][:], tv(bank(c, 2)[:, 0:P]), ALU.add))
                for c in CH:
                    after(last[c])
                    last[c] = done(v.tensor_tensor(xc[c][:], xc[c][:], bcast(gate[c][:], D), ALU.mult))
                for c in CH:
                    after(last[c])
                    done(v.tensor_scalar(fill[c][:], xc[c][:], 1e4, -1e4, ALU.min, ALU.max))
                    done(v.tensor_scalar(finite[c][:], xc[c][:], 0.0, 0.0, ALU.mult, ALU.is_equal))
                    last[c] = done(v.tensor_tensor(bad[c][:], xc[c][:], xc[c][:], ALU.not_equal))
                for c in CH:
                    after(last[c])
                    last[c] = done(v.copy_predicated(fill[c][:], finite[c][:], xc[c][:]))
                for c in CH:
                    after(last[c])
                    last[c] = done(v.copy_predicated(fill[c][:], bad[c][:], zero[:].unsqueeze(2).to_broadcast([P, 2, D])))
                for c in CH:
                    after(last[c])
                    last[c] = done(v.tensor_tensor(h[c][:], h[c][:], fill[c][:], ALU.add))
                norm_rows("L3_attn_pre", h)
                attention(STEP["L3"], 1, 1, True, 0.125, lambda s, c: xc[c][:].unsqueeze(2))
                add_to_h(STEP["L3"])
                statistics("L3_ffn_pre", h)
                for c in CH:
                    rooted("L3_ffn_pre", c)
                    for t in TILES:
                        last[c] = done(v.tensor_scalar(x3[c][:, t, :], h[c][:, t, :], mv[c][:, t, 0:1],
                                                       rstd[c][:, t:t + 1], ALU.subtract, ALU.mult))
                squares(x3)
                inverse_root("L3_rms1", 1e-6)
                for c in CH:
                    rooted("L3_rms1", c)
                    v.tensor_tensor(xc[c][:], x3[c][:], bcast(rstd[c][:, 0:2], D), ALU.mult).then_inc(rows_ready, 1)
                for c in CH:
                    dve.wait_ge(proj_ready, nth(6, c))
                    x = tv(bank(c, 2)[:, 0:256])
                    q6 = x[:, :, 0:96].rearrange("p t (h f) -> p t h f", f=16)
                    k6 = kk[c][:, :, 0:96].rearrange("p t (h f) -> p t h f", f=16)
                    m6 = kkm[c][:, :, 0:96].rearrange("p t (h f) -> p t h f", f=16)
                    done(v.tensor_copy(kk[c][:, :, 96:128], x[:, :, 96:128]))
                    done(v.tensor_tensor(k6, q6, bcast_mid(cos3, 6), ALU.mult))
                    done(v.tensor_tensor(m6[:, :, :, 0:8], q6[:, :, :, 8:16], bcast_mid(sin3[:, :, 0:8], 6), ALU.mult))
                    last[c] = done(v.tensor_tensor(m6[:, :, :, 8:16], q6[:, :, :, 0:8], bcast_mid(sin3[:, :, 8:16], 6), ALU.mult))
                    after(last[c])
                    pad = kd4[c][:].rearrange("p g t (h f) -> p g t h f", f=32)
                    v.tensor_tensor(pad[:, 0, :, :, 0:16], k6[:, :, 0:4, :], m6[:, :, 0:4, :], ALU.add)
                    for r in range(2):
                        q = v.tensor_tensor(pad[:, 1, :, r:4:2, 0:16], k6[:, :, 4:6, :], m6[:, :, 4:6, :], ALU.add)
                    q.then_inc(qk_rows, 1)
                attention(STEP["L3f"], 2, 2, False, 0.25,
                          lambda s, c: att[c][:, :, 32 * s:32 * s + 32].rearrange("p t (e d) -> p t e d", e=2), 16)
                for c in CH:
                    dve.wait_ge(at_out, nth(STEP["L3f"] + 1, c))
                    dve.drain().then_inc(rows_ready, 1)
                for c in CH:
                    dve.wait_ge(proj_ready, nth(7, c))
                    last[c] = done(v.tensor_tensor(x3[c][:], x3[c][:], tv(bank(c, 2)[:, 0:P]), ALU.add))
                squares(x3)
                inverse_root("L3_rms2", 1e-6)
                for c in CH:
                    rooted("L3_rms2", c)
                    v.tensor_tensor(xc[c][:], x3[c][:], bcast(rstd[c][:, 0:2], D), ALU.mult).then_inc(rows_ready, 1)
                route(8, 8, 2)
                shift(8)
                for c in CH:
                    dve.wait_ge(expd, nth(2, c))
                    last[c] = done(v.reduce_sum(st[c][:, 0, 0:2], prob[c][:, :, 0:8], AX.X))
                for c in CH:
                    after(last[c])
                    done(v.reciprocal(rr[c][:, 0:2], st[c][:, 0, 0:2]))
                    last[c] = done(v.tensor_tensor(prob[c][:, :, 0:8], prob[c][:, :, 0:8], sel[c][:, :, 0:8], ALU.mult))
                for c in CH:
                    after(last[c])
                    last[c] = done(v.tensor_tensor(prob[c][:, :, 0:8], prob[c][:, :, 0:8], bcast(rr[c][:, 0:2], 8), ALU.mult))
                for c in CH:
                    after(last[c])
                    last[c] = done(v.reduce_sum(st[c][:, 0, 0:2], prob[c][:, :, 0:8], AX.X))
                for c in CH:
                    after(last[c])
                    last[c] = done(v.tensor_scalar(st[c][:, 1, 0:2], st[c][:, 0, 0:2], 2.0, 2e-9, ALU.mult, ALU.add))
                for c in CH:
                    after(last[c])
                    last[c] = done(v.reciprocal(rr[c][:, 2:4], st[c][:, 1, 0:2]))
                for c in CH:
                    after(last[c])
                    last[c] = done(v.tensor_tensor(prob[c][:, :, 0:8], prob[c][:, :, 0:8], bcast(rr[c][:, 2:4], 8), ALU.mult))
                for c in CH:
                    after(last[c])
                for x in range(16):
                    t, e = x // 8, x % 8
                    for c in CH:
                        dve.wait_ge(f4_tanh, nth(x, c))
                        last[c] = done(v.scalar_tensor_tensor(th[c][:, x % 3, :], th[c][:, x % 3, :], 1.0,
                                                              bank(c, MOE_BANK[x % 3])[:, 0:HIDDEN3], ALU.add, ALU.mult))
                    for c in CH:
                        after(last[c])
                        v.scalar_tensor_tensor(hid[t][c][:, e * HIDDEN3:(e + 1) * HIDDEN3],
                                               bank(c, MOE_BANK[x % 3])[:, HIDDEN3:2 * HIDDEN3],
                                               prob[c][:, t, e:e + 1], th[c][:, x % 3, :], ALU.mult, ALU.mult).then_inc(f4_h, 1)
                for c in CH:
                    last[c] = done(v.tensor_tensor(h[c][:], h[c][:], x3[c][:], ALU.add))
                for c in CH:
                    dve.wait_ge(ao_rows, nth(4, c))
                    after(last[c])
                    last[c] = done(v.tensor_tensor(h[c][:], h[c][:], tv(bank(c, 2)[:, 0:P]), ALU.add))
                for c in CH:
                    after(last[c])
                    v.tensor_copy(h_all[:, bass.ds(i * 4 + 2 * c, 2), :], h[c][:])
                close_pass(dve, i)


def layout(x):
    f = np.float32

    def rows(a, b):
        return np.concatenate([a, b.reshape(1, -1)], 0)

    half_split = np.concatenate([np.arange(0, 64, 2), np.arange(1, 64, 2)])
    rope16 = np.concatenate([np.arange(0, 16, 2), np.arange(1, 16, 2)])
    i, j = np.arange(P)[:, None], np.arange(P)[None, :]


    def rope(freqs):
        ang = (np.arange(T, dtype=f)[:, None] * freqs[None, :].astype(f)).astype(f)
        s, c = np.sin(ang).astype(f), np.cos(ang).astype(f)
        both = lambda a, b: np.concatenate([a, b], 1).reshape(2, P, -1).transpose(1, 0, 2).reshape(P, -1)
        return both(c, c), both(-s, s)

    cos1, sin1 = rope(np.power(f(10000.0), (-2.0 * np.arange(32, dtype=f) / 64).astype(f)))
    cos2, sin2 = rope((f(1.0) / np.power(f(10000.0), np.arange(8, dtype=f) / f(8))).astype(f))
    cos3, sin3 = rope((1.0 / 10000.0 ** (np.arange(0, 16, 2, dtype=f) / 16)).astype(f))
    sel8 = np.zeros((8, 4, P), f)
    for p in range(4):
        sel8[2 * p, p, 0:64] = 1
        sel8[2 * p + 1, p, 64:128] = 1
    wq = x["L1_attn_wq"].reshape(16, 64, 64)[:, half_split].reshape(1024, 64)
    wk, wv = x["L1_attn_wkv"][0:64][half_split], x["L1_attn_wkv"][64:128]
    w2 = x["L3_ffn_w2"].transpose(0, 2, 1).reshape(8 * HIDDEN3, D)
    pieces = {
        "ident": ("early128", np.eye(P, dtype=f)),
        "window": ("early128", np.where(j >= i, 0, NEG).astype(f)),
        "causal": ("early128", np.where(j <= i, 0, NEG).astype(f)),
        "tri": ("early128", (i <= j).astype(f)),
        "cos_l1": ("early128", cos1), "sin_l1": ("early128", sin1),
        "cos_l2": ("early128", cos2), "sin_l2": ("early128", sin2),
        "cos_l3": ("early128", cos3), "sin_l3": ("early128", sin3),
        "iota_col": ("early128", np.arange(P, dtype=f).reshape(P, 1)),
        "WdT": ("early128", x["L0_tok_Wd"].transpose(3, 0, 1, 2).reshape(P, -1)),
        "WgT": ("early64", x["L0_tok_Wg"].transpose(3, 0, 1, 2).reshape(D, -1)),
        "WuT": ("early64", x["L0_tok_Wu"].transpose(3, 0, 1, 2).reshape(D, -1)),
        "embT": ("early64", x["L0_tok_embed"].T),
        "lmT": ("early64", x["L0_tok_lm_head"].T),
        "L0_Wq": ("early65", rows(x["L0_attn_Wq"], x["L0_attn_bq"])),
        "L0_Wk": ("early65", rows(x["L0_attn_Wk"], x["L0_attn_bk"])),
        "L0_Wv": ("early65", rows(x["L0_attn_Wv"], x["L0_attn_bv"])),
        "L0_Wo": ("early65", rows(x["L0_attn_Wo"], x["L0_attn_bo"])),
        "L0_out": ("early65", rows(x["L0_ffn_out_w"].T, x["L0_ffn_out_b"])),
        "sel8": ("late8", sel8.reshape(8, -1)),
        "L0_gate": ("late64", x["L0_ffn_gate_w"].T),
        "L1_wq": ("late64", wq.T),
        "L1_wkv": ("late64", np.concatenate([wk, wv], 0).T),
        "L2_Wqcomp": ("late64", x["L2_attn_Wq_comp"]), "L2_Wkvcomp": ("late64", x["L2_attn_Wkv_comp"]),
        "L2_Wq": ("late64", np.concatenate([x["L2_attn_Wqc"], x["L2_attn_Wqr"][:, rope16]], 1)),
        "L2_Wkv": ("late64", np.concatenate([x["L2_attn_Wkc"], x["L2_attn_Wkr"][:, rope16], x["L2_attn_Wv"]], 1)),
        "L2_gate": ("late64", x["L2_ffn_gate_w"]),
        "ln1": ("late64", x["L3_ffn_ln1_w"].reshape(D, 1)), "ln2": ("late64", x["L3_ffn_ln2_w"].reshape(D, 1)),
        "L3_wqkv": ("late64", np.concatenate([x["L3_ffn_wq"], x["L3_ffn_wk"], x["L3_ffn_wv"]], 0).T),
        "L3_wo": ("late64", x["L3_ffn_wo"].T),
        "L3_router": ("late64", x["L3_ffn_router_w"].T),
        "L3_w13": ("late64", np.concatenate([x["L3_ffn_w1"], x["L3_ffn_w3"]], 1).transpose(2, 0, 1).reshape(D, -1)),
        "L1_router": ("late65", rows(x["L1_ffn_router_w"].T, x["L1_ffn_router_b"])),
        "L1_W1": ("late65", rows(x["L1_ffn_W1"].transpose(1, 0, 2).reshape(D, 512), x["L1_ffn_b1"])),
        "L3_Wq": ("late65", rows(x["L3_attn_Wq"], x["L3_attn_bq"])),
        "L3_Wk": ("late65", rows(x["L3_attn_Wk"], x["L3_attn_bk"])),
        "L3_Wv": ("late65", rows(x["L3_attn_Wv"], x["L3_attn_bv"])),
        "L1_b2": ("late32", x["L1_ffn_b2"]),
        "L2_b1": ("late8", x["L2_ffn_b1"]),
        "L2_b2": ("late8", x["L2_ffn_b2"]),
        "lattice": ("late128", x["L0_ffn_lattice_weights"].reshape(32, P, D).transpose(1, 0, 2).reshape(P, -1)),
        "L1_wo": ("late128", x["L1_attn_wo"].T.reshape(8, P, D).transpose(1, 0, 2).reshape(P, -1)),
        "L1_W2": ("late128", x["L1_ffn_W2"].reshape(4, P, D).transpose(1, 0, 2).reshape(P, -1)),
        "L2_W1": ("late128", x["L2_ffn_w1"].reshape(4, P, 256).transpose(1, 0, 2).reshape(P, -1)),
        "L2_W2": ("late128", x["L2_ffn_w2"].reshape(8, 2, P, D).transpose(2, 1, 0, 3).reshape(P, -1)),
        "L3_w2": ("late128", w2[0:1280].reshape(10, P, D).transpose(1, 0, 2).reshape(P, -1)),
        "L3_w2t": ("late80", w2[1280:]),
    }
    packs, place = {}, {}
    for name, (pack, a) in pieces.items():
        at = sum(b.shape[1] for b in packs.get(pack, []))
        place[name] = (pack, at, a.shape[1], a.shape[0])
        packs.setdefault(pack, []).append(a)
    arrays = {k: np.ascontiguousarray(np.concatenate(b, 1)) for k, b in packs.items()}
    return arrays, place


def kernel(**inputs):
    import numpy as _np
    import concourse.bacc as _bacc
    from concourse import mybir as _mybir
    from concourse.bass_utils import run_bass_kernel_spmd as _run

    x = {k: _np.ascontiguousarray(a) for k, a in inputs.items()}
    arrays, place = layout(x)
    cols = {"packs": {k: a.shape for k, a in arrays.items()}, "pieces": place}
    ids = x["x"].reshape(-1)
    arrays["ids"] = ids
    arrays["ids_tok"] = _np.ascontiguousarray(ids.reshape(2 * SEQS, P).T)
    arrays["edges"] = _np.ascontiguousarray(x["L0_attn_edge_index"].reshape(2, P, P).transpose(1, 0, 2))
    arrays["vecs"] = _np.stack([x["L0_attn_gamma"], x["L0_attn_beta"], x["L0_ffn_ln_g"], x["L0_ffn_ln_b"],
                                _np.concatenate([x["L1_attn_q_norm_w"][0::2], x["L1_attn_q_norm_w"][1::2]]),
                                _np.concatenate([x["L1_attn_k_norm_w"][0::2], x["L1_attn_k_norm_w"][1::2]]),
                                _np.pad(x["L2_ffn_gate_b"], (0, D - 8))])
    nc = _bacc.Bacc("TRN2", target_bir_lowering=False, num_devices=1)
    dram = {k: nc.dram_tensor("in_" + k, a.shape, _mybir.dt.from_np(a.dtype), kind="ExternalInput").ap()
            for k, a in arrays.items()}
    out = nc.dram_tensor("tower_out", (SEQS * T, D), F32, kind="ExternalOutput").ap()
    build(nc, dram, out, cols)
    r = _run(nc, [{"in_" + k: a for k, a in arrays.items()}], core_ids=[0])
    return r.results[0]["tower_out"].reshape(SEQS, T, D)
```
